# Optimizing a Trainium2 kernel written in Bass

```python
import numpy as np
import jax
import jax.numpy as jnp

def _softmax(x, axis=-1):
    return jax.nn.softmax(x, axis=axis)

def _gelu(x):
    return jax.nn.gelu(x, approximate=True)

def _silu(x):
    return jax.nn.silu(x)

def _sigmoid(x):
    return jax.nn.sigmoid(x)

def _layernorm(x, axis=-1, eps=1e-05):
    m = jnp.mean(x, axis=axis, keepdims=True)
    v = jnp.var(x, axis=axis, keepdims=True)
    return (x - m) / jnp.sqrt(v + eps)

def _scatter_add(tgt, idx, src, axis=0):
    return tgt.at[idx].add(src)

def _segment_sum(src, seg, n):
    return jax.ops.segment_sum(src, seg, n)
kernel_name = 'mk_gnn_resnorm_d4_gnn_r64_980149'

def setup_inputs(seed: int=0):
    np.random.seed(seed)
    _w = jnp.asarray

    def _rec_inputs():
        import jax
        import jax.numpy as jnp
        _gk = jax.random.key(seed)
        x = -8.776e-05 + 1 * jax.random.normal(jax.random.fold_in(_gk, 1), (10000, 512), jnp.float32)
        src = jax.random.randint(jax.random.fold_in(_gk, 2), (2500,), 0, 10000, jnp.int32)
        dst = jax.random.randint(jax.random.fold_in(_gk, 3), (2500,), 0, 10000, jnp.int32)
        _o = jnp.argsort(dst, stable=True)
        src = src[_o]
        dst = dst[_o]
        edge_attr_20 = 0.000389844 + 1.00025 * jax.random.normal(jax.random.fold_in(_gk, 12), (2500, 20), jnp.float32)
        edge_attr_4 = -0.00185629 + 0.998788 * jax.random.normal(jax.random.fold_in(_gk, 13), (2500, 4), jnp.float32)
        edge_weight = jax.random.uniform(jax.random.fold_in(_gk, 16), (2500,), jnp.float32, 0.0, 0.999999)
        return (x, src, dst, edge_attr_20, edge_attr_4, edge_weight)
    x, src, dst, edge_attr_20, edge_attr_4, edge_weight = _rec_inputs()

    def _L0_gnn_setup():
        import jax, jax.numpy as jnp
        import numpy as np
        N = 10000
        E = 2500
        H = 4
        C = 256
        D_IN = 512
        D_OUT = 512
        NEG_SLOPE = 0.2

        def gat_conv(x, src, dst, W, a_src, a_dst, bias):
            n = x.shape[0]
            h = (x @ W).reshape(n, H, C)
            al_s = jnp.einsum('nhc,hc->nh', h, a_src)
            al_d = jnp.einsum('nhc,hc->nh', h, a_dst)
            e = jax.nn.leaky_relu(al_s[src] + al_d[dst], NEG_SLOPE)
            emax = jax.ops.segment_max(e, dst, num_segments=n)
            w = jnp.exp(e - emax[dst])
            denom = jax.ops.segment_sum(w, dst, num_segments=n)
            alpha = w / denom[dst]
            out = jax.ops.segment_sum(h[src] * alpha[:, :, None], dst, num_segments=n)
            return out.reshape(n, H * C) + bias
        key = jax.random.key(seed)
        ks = jax.random.split(key, 13)
        s = 0.05
        return {'x': jax.random.normal(ks[0], (N, D_IN), jnp.float32), 'edge_index': jax.random.randint(ks[1], (2, E), 0, N, dtype=jnp.int32), 'W1': jax.random.normal(ks[2], (D_IN, H * C), jnp.float32) * s, 'a_src1': jax.random.normal(ks[3], (H, C), jnp.float32) * s, 'a_dst1': jax.random.normal(ks[4], (H, C), jnp.float32) * s, 'b1': jnp.zeros((H * C,), jnp.float32), 'W2': jax.random.normal(ks[5], (H * C, H * C), jnp.float32) * s, 'a_src2': jax.random.normal(ks[6], (H, C), jnp.float32) * s, 'a_dst2': jax.random.normal(ks[7], (H, C), jnp.float32) * s, 'b2': jnp.zeros((H * C,), jnp.float32), 'Wfc': jax.random.normal(ks[8], (H * C, D_OUT), jnp.float32) * s, 'bfc': jnp.zeros((D_OUT,), jnp.float32)}
    _L0_gnn_all = _L0_gnn_setup()
    _L0_gnn_in = {k: v for k, v in _L0_gnn_all.items() if k in ('W1', 'a_src1', 'a_dst1', 'b1', 'W2', 'a_src2', 'a_dst2', 'b2', 'Wfc', 'bfc')}
    del _L0_gnn_all

    def _L1_gnn_setup():
        import jax, jax.numpy as jnp
        import numpy as np
        N_NODES = 100000
        N_EDGES = 25000
        D_IN = 512
        D_OUT = 512
        key = jax.random.key(seed)
        k1, k2, k3, k4, k5 = jax.random.split(key, 5)
        h = jax.random.normal(k1, (N_NODES, D_IN), dtype=jnp.float32)
        weight = jax.random.normal(k2, (D_IN, D_OUT), dtype=jnp.float32) * (1.0 / np.sqrt(D_IN))
        edge_weight = jax.random.uniform(k3, (N_EDGES,), dtype=jnp.float32)
        src = jax.random.randint(k4, (N_EDGES,), 0, N_NODES, dtype=jnp.int64)
        dst = jax.random.randint(k5, (N_EDGES,), 0, N_NODES, dtype=jnp.int64)
        return {'h': h, 'weight': weight, 'edge_weight': edge_weight, 'src': src, 'dst': dst}
    _L1_gnn_all = _L1_gnn_setup()
    _L1_gnn_in = {k: v for k, v in _L1_gnn_all.items() if k in ('weight',)}
    del _L1_gnn_all

    def _L2_gnn_setup():
        import jax, jax.numpy as jnp
        import numpy as np
        import math
        B = 128
        F = 32
        R = 20
        N = 256
        E = 4096
        LOG2 = 0.6931471805599453
        IS2 = 1.0 / math.sqrt(2.0)
        IS3 = 1.0 / math.sqrt(3.0)
        IS6 = 1.0 / math.sqrt(6.0)

        def ssp(x):
            return jax.nn.softplus(x) - LOG2
        key = jax.random.key(seed)
        ks = jax.random.split(key, 14)
        return dict(x=jax.random.normal(ks[0], (N, 4 * B), jnp.float32), idx_i=jax.random.randint(ks[1], (E,), 0, N), idx_j=jax.random.randint(ks[2], (E,), 0, N), f_ij=jax.random.normal(ks[3], (E, R), jnp.float32), rcut_ij=jax.random.uniform(ks[4], (E,), jnp.float32), Yr_ij=jax.random.normal(ks[5], (E, 4), jnp.float32), w_in2f_s=jax.random.normal(ks[6], (B, F), jnp.float32), w_in2f_v=jax.random.normal(ks[7], (B, F), jnp.float32), W1=jax.random.normal(ks[8], (R, F), jnp.float32) / math.sqrt(R), b1=jnp.zeros((F,), jnp.float32), W2=jax.random.normal(ks[9], (F, 6 * F), jnp.float32) / math.sqrt(F), b2=jnp.zeros((6 * F,), jnp.float32), w_f2o1_s=jax.random.normal(ks[10], (2 * F, B), jnp.float32), w_f2o1_v=jax.random.normal(ks[11], (2 * F, B), jnp.float32), w_f2o2_s=jax.random.normal(ks[12], (B, B), jnp.float32), w_f2o2_v=jax.random.normal(ks[13], (B, B), jnp.float32))
    _L2_gnn_all = _L2_gnn_setup()
    _L2_gnn_in = {k: v for k, v in _L2_gnn_all.items() if k in ('w_in2f_s', 'w_in2f_v', 'W1', 'b1', 'W2', 'b2', 'w_f2o1_s', 'w_f2o1_v', 'w_f2o2_s', 'w_f2o2_v')}
    del _L2_gnn_all

    def _L3_gnn_setup():
        import jax, jax.numpy as jnp
        import numpy as np
        N_NODES = 10000
        N_EDGES = 2500
        D_FEAT = 512
        OUT_CH = 512
        key = jax.random.key(seed)
        k1, k2, k3, k4 = jax.random.split(key, 4)
        x = jax.random.normal(k1, (N_NODES, D_FEAT), dtype=jnp.float32)
        edge_index = jax.random.randint(k2, (N_EDGES, 2), 0, N_NODES, dtype=jnp.int64)
        W = jax.random.normal(k3, (OUT_CH, 2 * D_FEAT), dtype=jnp.float32) / np.sqrt(2 * D_FEAT)
        b = jax.random.normal(k4, (OUT_CH,), dtype=jnp.float32) * 0.01
        return {'x': x, 'edge_index': edge_index, 'num_local_nodes': N_NODES, 'W': W, 'b': b}
    _L3_gnn_all = _L3_gnn_setup()
    _L3_gnn_in = {k: v for k, v in _L3_gnn_all.items() if k in ('W', 'b')}
    del _L3_gnn_all
    return {'x': x, 'src': src, 'dst': dst, 'edge_attr_20': edge_attr_20, 'edge_attr_4': edge_attr_4, 'edge_weight': edge_weight, 'L0_gnn_W1': _L0_gnn_in['W1'], 'L0_gnn_a_src1': _L0_gnn_in['a_src1'], 'L0_gnn_a_dst1': _L0_gnn_in['a_dst1'], 'L0_gnn_b1': _L0_gnn_in['b1'], 'L0_gnn_W2': _L0_gnn_in['W2'], 'L0_gnn_a_src2': _L0_gnn_in['a_src2'], 'L0_gnn_a_dst2': _L0_gnn_in['a_dst2'], 'L0_gnn_b2': _L0_gnn_in['b2'], 'L0_gnn_Wfc': _L0_gnn_in['Wfc'], 'L0_gnn_bfc': _L0_gnn_in['bfc'], 'L1_gnn_weight': _L1_gnn_in['weight'], 'L2_gnn_w_in2f_s': _L2_gnn_in['w_in2f_s'], 'L2_gnn_w_in2f_v': _L2_gnn_in['w_in2f_v'], 'L2_gnn_W1': _L2_gnn_in['W1'], 'L2_gnn_b1': _L2_gnn_in['b1'], 'L2_gnn_W2': _L2_gnn_in['W2'], 'L2_gnn_b2': _L2_gnn_in['b2'], 'L2_gnn_w_f2o1_s': _L2_gnn_in['w_f2o1_s'], 'L2_gnn_w_f2o1_v': _L2_gnn_in['w_f2o1_v'], 'L2_gnn_w_f2o2_s': _L2_gnn_in['w_f2o2_s'], 'L2_gnn_w_f2o2_v': _L2_gnn_in['w_f2o2_v'], 'L3_gnn_W': _L3_gnn_in['W'], 'L3_gnn_b': _L3_gnn_in['b']}

def reference(x, src, dst, edge_attr_20, edge_attr_4, edge_weight, L0_gnn_W1, L0_gnn_a_src1, L0_gnn_a_dst1, L0_gnn_b1, L0_gnn_W2, L0_gnn_a_src2, L0_gnn_a_dst2, L0_gnn_b2, L0_gnn_Wfc, L0_gnn_bfc, L1_gnn_weight, L2_gnn_w_in2f_s, L2_gnn_w_in2f_v, L2_gnn_W1, L2_gnn_b1, L2_gnn_W2, L2_gnn_b2, L2_gnn_w_f2o1_s, L2_gnn_w_f2o1_v, L2_gnn_w_f2o2_s, L2_gnn_w_f2o2_v, L3_gnn_W, L3_gnn_b):
    import jax
    import jax.numpy as jnp

    def _L0_gnn_ref(x, edge_index, W1, a_src1, a_dst1, b1, W2, a_src2, a_dst2, b2, Wfc, bfc):
        import jax, jax.numpy as jnp
        import numpy as np
        N = 10000
        E = 2500
        H = 4
        C = 256
        D_IN = 512
        D_OUT = 512
        NEG_SLOPE = 0.2

        def gat_conv(x, src, dst, W, a_src, a_dst, bias):
            n = x.shape[0]
            h = (x @ W).reshape(n, H, C)
            al_s = jnp.einsum('nhc,hc->nh', h, a_src)
            al_d = jnp.einsum('nhc,hc->nh', h, a_dst)
            e = jax.nn.leaky_relu(al_s[src] + al_d[dst], NEG_SLOPE)
            emax = jax.ops.segment_max(e, dst, num_segments=n)
            w = jnp.exp(e - emax[dst])
            denom = jax.ops.segment_sum(w, dst, num_segments=n)
            alpha = w / denom[dst]
            out = jax.ops.segment_sum(h[src] * alpha[:, :, None], dst, num_segments=n)
            return out.reshape(n, H * C) + bias
        loop = jnp.arange(N, dtype=edge_index.dtype)
        src = jnp.concatenate([edge_index[0], loop])
        dst = jnp.concatenate([edge_index[1], loop])
        h = jax.nn.relu(gat_conv(x, src, dst, W1, a_src1, a_dst1, b1))
        h = jax.nn.relu(gat_conv(h, src, dst, W2, a_src2, a_dst2, b2))
        return h @ Wfc + bfc

    def _L1_gnn_ref(h, weight, edge_weight, src, dst):
        import jax, jax.numpy as jnp
        import numpy as np
        N_NODES = 100000
        N_EDGES = 25000
        D_IN = 512
        D_OUT = 512
        hp = h @ weight
        msgs = hp[src] * edge_weight[:, None]
        agg = jax.ops.segment_sum(msgs, dst, num_segments=h.shape[0])
        return jax.nn.relu(agg)

    def _L2_gnn_ref(x, idx_i, idx_j, f_ij, rcut_ij, Yr_ij, w_in2f_s, w_in2f_v, W1, b1, W2, b2, w_f2o1_s, w_f2o1_v, w_f2o2_s, w_f2o2_v):
        import jax, jax.numpy as jnp
        import numpy as np
        import math
        B = 128
        F = 32
        R = 20
        N = 256
        E = 4096
        LOG2 = 0.6931471805599453
        IS2 = 1.0 / math.sqrt(2.0)
        IS3 = 1.0 / math.sqrt(3.0)
        IS6 = 1.0 / math.sqrt(6.0)

        def ssp(x):
            return jax.nn.softplus(x) - LOG2
        n = x.shape[0]
        xs = x[:, :B]
        xv = x[:, B:].reshape(n, B, 3)
        hs = xs @ w_in2f_s / math.sqrt(B)
        hv = jnp.einsum('nbc,bf->nfc', xv, w_in2f_v) / math.sqrt(B)
        s = hs[idx_j]
        v = hv[idx_j]
        ys = Yr_ij[:, 0]
        yv = Yr_ij[:, 1:4]
        t_s1 = s * ys[:, None]
        t_s2 = jnp.einsum('efc,ec->ef', v, yv) * IS3
        t_v1 = s[:, :, None] * yv[:, None, :]
        t_v2 = v * ys[:, None, None]
        t_pv = jnp.cross(v, yv[:, None, :]) * IS2
        ax, ay, az = (v[..., 0], v[..., 1], v[..., 2])
        bx, by, bz = (yv[:, None, 0:1], yv[:, None, 1:2], yv[:, None, 2:3])
        bx, by, bz = (bx[..., 0], by[..., 0], bz[..., 0])
        t_q = jnp.stack([(ax * by + ay * bx) * IS2, (ay * bz + az * by) * IS2, (2.0 * az * bz - ax * bx - ay * by) * IS6, (ax * bz + az * bx) * IS2, (ax * bx - ay * by) * IS2], axis=-1)
        h = ssp(f_ij @ W1 + b1)
        Wij = (h @ W2 + b2) * rcut_ij[:, None]
        Wf = Wij.reshape(-1, F, 6)
        edge = jnp.concatenate([(t_s1 * Wf[..., 0])[..., None], (t_s2 * Wf[..., 1])[..., None], t_v1 * Wf[..., 2:3], t_v2 * Wf[..., 3:4], t_pv * Wf[..., 4:5], t_q * Wf[..., 5:6]], axis=-1)
        agg = jax.ops.segment_sum(edge.reshape(edge.shape[0], -1), idx_i, num_segments=n).reshape(n, F, 16)
        s_in = jnp.concatenate([agg[..., 0], agg[..., 1]], axis=1)
        v_in = jnp.concatenate([agg[..., 2:5], agg[..., 5:8]], axis=1)
        os1 = s_in @ w_f2o1_s / math.sqrt(2 * F)
        ov1 = jnp.einsum('nmc,mb->nbc', v_in, w_f2o1_v) / math.sqrt(2 * F)
        os1 = ssp(os1)
        os2 = os1 @ w_f2o2_s / math.sqrt(B)
        ov2 = jnp.einsum('nbc,bd->ndc', ov1, w_f2o2_v) / math.sqrt(B)
        return jnp.concatenate([os2, ov2.reshape(n, -1)], axis=-1)

    def _L3_gnn_ref(x, edge_index, num_local_nodes, W, b):
        import jax, jax.numpy as jnp
        import numpy as np
        N_NODES = 10000
        N_EDGES = 2500
        D_FEAT = 512
        OUT_CH = 512
        src = edge_index[:, 0]
        tgt = edge_index[:, 1]
        x_i = x[src]
        x_j = x[tgt]
        x_ij = jnp.concatenate([x_i, x_j], axis=1)
        m_ij = jax.nn.relu(x_ij @ W.T + b)
        out = jax.ops.segment_sum(m_ij, src, num_segments=num_local_nodes)
        return out
    edge_index = jnp.stack([src, dst])
    edge_index_t = jnp.stack([src, dst], axis=1)
    x = _layernorm(x + _L0_gnn_ref(x, edge_index, L0_gnn_W1, L0_gnn_a_src1, L0_gnn_a_dst1, L0_gnn_b1, L0_gnn_W2, L0_gnn_a_src2, L0_gnn_a_dst2, L0_gnn_b2, L0_gnn_Wfc, L0_gnn_bfc), axis=-1)
    x = _layernorm(x + _L1_gnn_ref(x, L1_gnn_weight, edge_weight, src, dst), axis=-1)
    x = _layernorm(x + _L2_gnn_ref(x, src, dst, edge_attr_20, edge_weight, edge_attr_4, L2_gnn_w_in2f_s, L2_gnn_w_in2f_v, L2_gnn_W1, L2_gnn_b1, L2_gnn_W2, L2_gnn_b2, L2_gnn_w_f2o1_s, L2_gnn_w_f2o1_v, L2_gnn_w_f2o2_s, L2_gnn_w_f2o2_v), axis=-1)
    x = _layernorm(x + _L3_gnn_ref(x, edge_index_t, 10000, L3_gnn_W, L3_gnn_b), axis=-1)
    return x

_drawn_inputs = setup_inputs


def setup_inputs(seed=0):
    import zlib

    import numpy as np

    out = dict(_drawn_inputs(seed))
    spreads = {'L0_gnn_b1': (0.0, 0.1),
     'L0_gnn_b2': (0.0, 0.1),
     'L0_gnn_bfc': (0.0, 0.1),
     'L2_gnn_b1': (0.0, 0.797),
     'L2_gnn_b2': (0.0, 0.351)}
    factors = {'L0_gnn_a_dst2': 4.586, 'L3_gnn_b': 8.0}
    for name, (base, spread) in spreads.items():
        noise = np.random.default_rng([zlib.crc32(name.encode()), seed]).standard_normal(out[name].shape)
        drawn = base * np.exp(spread * noise) if base else spread * noise
        out[name] = jnp.asarray(drawn.astype(out[name].dtype))
    for name, factor in factors.items():
        out[name] = (out[name] * factor).astype(out[name].dtype)
    return out
```

```python
from contextlib import ExitStack

import concourse.bass as bass
from concourse import mybir

F32 = mybir.dt.float32
F32R = mybir.dt.float32r
I32 = mybir.dt.int32
ALU = mybir.AluOpType
ACT = mybir.ActivationFunctionType

P = 128
N, E = 10000, 2500
NP = -(-N // (4 * P)) * 4 * P
ET = -(-E // P)
EP = ET * P
NT = NP + EP
H, C = 4, 256
HC = H * C
D = 512
EPS = 1e-5

REC = 8
TAB = 8
D_SRC, D_DST, D_OUT, KEY, D_EW = range(5)
S_X2DST, S_X2SRC, S_X3SRC, _, S_X3DST, S_OUT, S_EDGE = range(7)


def edge_prep(nc, sem, ends_row, ends_col, ew_col, rec_d, rec_s, row_d, row_s, map_d, map_s, tab_d, tab_s):
    with ExitStack() as ctx:
        sb = lambda n, s, d=F32: ctx.enter_context(nc.sbuf_tensor(f"prep_{n}", s, d))
        int_row = sb("int_row", [P, EP], I32)
        row = [sb(f"row{o}", [P, EP]) for o in range(2)]
        junk = [[sb(f"junk{e}{q}", [P, EP]) for q in range(2)] for e in range(2)]
        int_col = sb("int_col", [P, 2, ET], I32)
        col = sb("col", [P, 2, ET])
        neg = sb("neg", [P, 2, ET])
        lower = sb("lower", [P, P])
        count = [sb(f"count{o}", [P, 4, ET]) for o in range(2)]
        total = sb("total", [P, 2, ET])
        rank = sb("rank", [P, 2, ET])
        rank_i = sb("rank_i", [P, 2, ET], I32)
        weight = sb("weight", [P, ET])
        rec = sb("rec", [P, ET, REC])
        srt = [sb(f"srt{o}", [P, ET, REC]) for o in range(2)]
        ident = sb("ident", [P, P])
        key_t = sb("key_t", [ET, 2, P])
        nxt_t = sb("nxt_t", [ET, 2, P])
        ends = sb("ends", [1, 2, 2])
        zero = sb("zero", [P, NT // P])
        r_i = sb("r_i", [P, ET], I32)
        r_f = sb("r_f", [P, ET])
        dump = sb("dump", [P, ET])
        r1 = sb("r1", [P, ET])
        r_next = sb("r_next", [P, ET])
        is_last = sb("is_last", [P, 2, ET])
        off = sb("off", [P, 2, ET])
        scat = sb("scat", [P, 2, ET])
        scat_i = sb("scat_i", [P, 2, ET], I32)
        node_i = sb("node_i", [P, 2, 2, ET], I32)
        found = sb("found", [P, ET, 4])
        has = sb("has", [P, 2, ET])
        alt = sb("alt", [P, 2, ET])
        diff = sb("diff", [P, 2, ET])
        pick = sb("pick", [P, 4, ET])
        out_d = sb("out_d", [P, ET, TAB])
        out_s = sb("out_s", [P, ET, TAB])
        t_ps = ctx.enter_context(nc.psum_tensor("prep_t_ps", [P, 512], F32))
        u_ps = ctx.enter_context(nc.psum_tensor("prep_u_ps", [P, 512], F32))

        rows_in = sem("prep_rows_in")
        rows_in2 = sem("prep_rows_in2")
        cols_in = sem("prep_cols_in")
        zeroed = sem("prep_zeroed")
        const_done = sem("prep_const_done")
        v = sem("prep_v")
        sign_sums = sem("prep_sign_sums")
        ranked = sem("prep_ranked")
        d_scattered = sem("prep_d_scattered")
        s_scattered = sem("prep_s_scattered")
        sorted_in = [sem(f"prep_sorted_in{o}") for o in range(2)]
        keys_t = sem("prep_keys_t")
        keys_sb = sem("prep_keys_sb")
        keys_out = sem("prep_keys_out")
        next_in = sem("prep_next_in")
        next_t = sem("prep_next_t")
        scat_done = sem("prep_scat_done")
        mapped = sem("prep_mapped")
        looked = sem("prep_looked")
        tabs_done = sem("prep_tabs_done")
        tabs_out = sem("prep_tabs_out")
        ends_done = sem("prep_ends_done")

        CONST = 7

        with nc.Block() as block:

            @block.sync
            def _(sp):
                sp.dma_start(int_row[:, :], ends_row[0].partition_broadcast(P)).then_inc(rows_in, 16)
                sp.dma_start(int_col[:, :, :], ends_col).then_inc(cols_in, 16)
                sp.dma_start(weight[:, :], ew_col).then_inc(cols_in, 16)
                sp.wait_ge(v, 1)
                sp.dma_start(int_row[:, :], ends_row[1].partition_broadcast(P)).then_inc(rows_in2, 16)
                sp.wait_ge(const_done, CONST)
                sp.wait_ge(ends_done, 1)
                sp.dma_start(map_d.rearrange("(p k) o -> p (k o)", p=P), zero[:, :]).then_inc(zeroed, 16)
                sp.dma_start(map_s.rearrange("(p k) o -> p (k o)", p=P), zero[:, :]).then_inc(zeroed, 16)
                for o, row_out in enumerate((row_d, row_s)):
                    sp.dma_start(row_out[0:1].rearrange("(a b) -> a b", a=1), ends[0:1, o, 0:1]).then_inc(zeroed, 16)
                    sp.dma_start(row_out[EP + 1:EP + 2].rearrange("(a b) -> a b", a=1),
                                 ends[0:1, o, 1:2]).then_inc(zeroed, 16)
                for o, (rec_out, scattered) in enumerate(((rec_d, d_scattered), (rec_s, s_scattered))):
                    sp.wait_ge(scattered, 16 * ET)
                    sp.dma_start(srt[o][:, :, :], rec_out.rearrange("(t p) k -> p t k", p=P)).then_inc(sorted_in[o], 16)
                sp.wait_ge(keys_sb, 1)
                for o, row_out in enumerate((row_d, row_s)):
                    sp.dma_start(row_out[1:EP + 1].rearrange("(t p) -> t p", p=P), key_t[:, o, :]).then_inc(keys_out, 16)
                sp.wait_ge(keys_out, 32)
                sp.wait_ge(zeroed, 96)
                for o, row_out in enumerate((row_d, row_s)):
                    sp.dma_start(nxt_t[:, o, :], row_out[2:EP + 2].rearrange("(t p) -> t p", p=P)).then_inc(next_in, 16)
                sp.wait_ge(tabs_done, 1)
                sp.dma_start(tab_d.rearrange("(t p) k -> p t k", p=P), out_d[:, :, :]).then_inc(tabs_out, 16)
                sp.dma_start(tab_s.rearrange("(t p) k -> p t k", p=P), out_s[:, :, :]).then_inc(tabs_out, 16)
                sp.wait_ge(tabs_out, 32)

            @block.gpsimd
            def _(pool):
                pool.memset(zero[:, :], 0.0).then_inc(const_done, 1)
                pool.memset(ident[:, :], 0.0).then_inc(const_done, 1)
                pool.memset(lower[:, :], 1.0).then_inc(const_done, 1)
                pool.iota(r_i[:, :], [[P, ET]], base=0, channel_multiplier=1).then_inc(const_done, 1)
                pool.iota(r_next[:, :].bitcast(I32), [[P, ET]], base=NP, channel_multiplier=1).then_inc(const_done, 1)
                pool.wait_ge(const_done, 5)
                pool.affine_select(out=ident[:, :], in_=ident[:, :], compare_op=ALU.not_equal, fill=1.0,
                                   base=0, pattern=[[-1, P]], channel_multiplier=1).then_inc(const_done, 1)
                pool.affine_select(out=lower[:, :], in_=lower[:, :], compare_op=ALU.is_gt, fill=0.0,
                                   base=0, pattern=[[-1, P]], channel_multiplier=1).then_inc(const_done, 1)
                for o, (rec_out, scattered) in enumerate(((rec_d, d_scattered), (rec_s, s_scattered))):
                    pool.wait_ge(ranked, o + 1)
                    for t in range(ET):
                        pool.indirect_dma_start(
                            rec_out, bass.IndirectOffsetOnAxis(rank_i[:, o, t:t + 1], 0),
                            rec[:, t, :], None).then_inc(scattered, 16)
                pool.wait_ge(scat_done, 1)
                pool.wait_ge(zeroed, 96)
                for o, map_out in enumerate((map_d, map_s)):
                    for t in range(ET):
                        pool.indirect_dma_start(
                            map_out, bass.IndirectOffsetOnAxis(scat_i[:, o, t:t + 1], 0),
                            r1[:, t:t + 1], None).then_inc(mapped, 16)
                pool.wait_ge(mapped, 32 * ET)
                for n, (map_in, end) in enumerate(((map_d, 1), (map_d, 0), (map_s, 0), (map_s, 1))):
                    for t in range(ET):
                        pool.indirect_dma_start(
                            found[:, t, n:n + 1], None, map_in,
                            bass.IndirectOffsetOnAxis(node_i[:, 1, end, t:t + 1], 0)).then_inc(looked, 16)

            @block.tensor
            def _(pe):
                pe.wait_ge(const_done, CONST)
                for o in range(2):
                    pe.wait_ge(sorted_in[o], 16)
                    last = pe.transpose(t_ps[0:ET, o * P:(o + 1) * P], srt[o][:, :, 0], ident[:, :])
                last.then_inc(keys_t, 1)
                pe.wait_ge(next_in, 32)
                for o in range(2):
                    last = pe.transpose(u_ps[:, o * ET:(o + 1) * ET], nxt_t[:, o, :], ident[0:ET, 0:ET])
                last.then_inc(next_t, 1)

            @block.scalar
            def _(act):
                act.wait_ge(v, 4)
                n_sums = 0
                for t in range(ET):
                    for n, (lo, hi, b) in enumerate(((0, t * P, 0), ((t + 1) * P, EP, 1), (t * P, (t + 1) * P, 1))):
                        if hi > lo:
                            if n_sums >= 2:
                                act.wait_ge(sign_sums, n_sums - 1)
                            act.activation(junk[1][n_sums % 2][:, lo:hi], row[1][:, lo:hi], ACT.Sign,
                                           bias=neg[:, b, t:t + 1],
                                           accum_out=count[1][:, n, t:t + 1]).then_inc(sign_sums, 1)
                            n_sums += 1
                act.wait_ge(keys_t, 1)
                act.activation(key_t[:, :, :], t_ps[0:ET, 0:2 * P].rearrange("t (o p) -> t o p", o=2),
                               ACT.Copy).then_inc(keys_sb, 1)

            @block.vector
            def _(dve):
                steps = 0

                def step(ins):
                    nonlocal steps
                    ins.then_inc(v, 1)
                    steps += 1

                def settle():
                    dve.wait_ge(v, steps)

                dve.memset(ends[:, :, 0:1], -1.0)
                dve.memset(ends[:, :, 1:2], -2.0).then_inc(ends_done, 1)
                dve.wait_ge(rows_in, 16)
                step(dve.tensor_copy(row[0][:, :], int_row[:, :]))
                dve.wait_ge(cols_in, 32)
                step(dve.tensor_copy(col[:, :, :], int_col[:, :, :]))
                dve.wait_ge(rows_in2, 16)
                settle()
                dve.tensor_scalar(neg[:, 0, :], col[:, 1, :], -1.0, -0.5, ALU.mult, ALU.add)
                step(dve.tensor_scalar(neg[:, 1, :], col[:, 1, :], -1.0, 0.5, ALU.mult, ALU.add))
                step(dve.tensor_copy(row[1][:, :], int_row[:, :]))
                dve.wait_ge(const_done, CONST)
                dve.memset(count[0][:, :, :], 0.0)
                dve.memset(count[1][:, 3, :], 0.0)
                dve.memset(count[1][:, 0, 0:1], 0.0)
                dve.memset(count[1][:, 1, ET - 1:ET], 0.0)
                dve.tensor_copy(r_f[:, :], r_i[:, :])
                dve.tensor_copy(dump[:, :], r_next[:, :].bitcast(I32))
                settle()
                dve.memset(rec[:, :, 5:REC], 0.0)
                dve.tensor_copy(rec[:, :, 4], weight[:, :])
                dve.tensor_copy(rec[:, :, 0], col[:, 0, :])
                step(dve.tensor_copy(rec[:, :, 1], col[:, 1, :]))
                settle()
                dve.tensor_copy(rec[:, :, 3], r_f[:, :])
                step(dve.tensor_scalar(r1[:, :], r_f[:, :], 1.0, None, ALU.add))
                settle()
                for t in range(ET):
                    c = col[:, 0, t:t + 1]
                    tile = slice(t * P, (t + 1) * P)
                    if t:
                        dve.tensor_scalar(junk[0][t % 2][:, 0:t * P], row[0][:, 0:t * P], c, None, ALU.is_le, ALU.add,
                                          accum_out=count[0][:, 0, t:t + 1])
                    if t < ET - 1:
                        dve.tensor_scalar(junk[0][t % 2][:, (t + 1) * P:EP], row[0][:, (t + 1) * P:EP], c, None,
                                          ALU.is_lt, ALU.add, accum_out=count[0][:, 1, t:t + 1])
                    step(dve.tensor_scalar(junk[0][t % 2][:, tile], row[0][:, tile], c, None, ALU.is_lt, ALU.add,
                                           accum_out=count[0][:, 2, t:t + 1]))
                    settle()
                    step(dve.scalar_tensor_tensor(junk[0][t % 2][:, tile], row[0][:, tile], c, lower[:, :],
                                                  ALU.is_equal, ALU.mult, accum_out=count[0][:, 3, t:t + 1]))
                    settle()
                    step(dve.scalar_tensor_tensor(junk[0][t % 2][:, tile], row[1][:, tile], col[:, 1, t:t + 1],
                                                  lower[:, :], ALU.is_equal, ALU.mult,
                                                  accum_out=count[1][:, 3, t:t + 1]))
                    settle()
                for o in range(2):
                    if o == 1:
                        dve.wait_ge(sign_sums, 3 * ET - 2)
                    c = count[o]
                    step(dve.tensor_tensor(total[:, 0, :], c[:, 0, :], c[:, 1, :], ALU.add))
                    settle()
                    step(dve.tensor_tensor(total[:, 1, :], total[:, 0, :], c[:, 2, :], ALU.add))
                    settle()
                    if o == 1:
                        step(dve.tensor_scalar(total[:, 0, :], total[:, 1, :], -0.5, EP / 2, ALU.mult, ALU.add))
                    else:
                        step(dve.tensor_copy(total[:, 0, :], total[:, 1, :]))
                    settle()
                    step(dve.tensor_tensor(rank[:, o, :], total[:, 0, :], c[:, 3, :], ALU.add))
                    settle()
                    if o == 0:
                        step(dve.tensor_copy(rec[:, :, 2], rank[:, 0, :]))
                    else:
                        dve.wait_ge(d_scattered, 16 * ET)
                        step(dve.tensor_copy(rec[:, :, 0], col[:, 1, :]))
                        step(dve.tensor_copy(rec[:, :, 1], col[:, 0, :]))
                        settle()
                    dve.tensor_copy(rank_i[:, o, :], rank[:, o, :]).then_inc(ranked, 1)
                dve.wait_ge(next_t, 1)
                for o in range(2):
                    key = srt[o][:, :, 0]
                    step(dve.tensor_tensor(is_last[:, o, :], key, u_ps[:, o * ET:(o + 1) * ET], ALU.not_equal))
                    step(dve.tensor_tensor(off[:, o, :], key, dump[:, :], ALU.subtract))
                    settle()
                    step(dve.tensor_tensor(scat[:, o, :], off[:, o, :], is_last[:, o, :], ALU.mult))
                    settle()
                    step(dve.tensor_tensor(off[:, o, :], scat[:, o, :], dump[:, :], ALU.add))
                    settle()
                    step(dve.tensor_copy(scat_i[:, o, :], off[:, o, :]))
                    for end in range(2):
                        step(dve.tensor_copy(node_i[:, o, end, :], srt[o][:, :, end]))
                settle()
                dve.memset(out_d[:, :, :], 0.0)
                step(dve.memset(out_s[:, :, :], 0.0))
                dve.tensor_copy(diff[:, 0, :], is_last[:, 0, :]).then_inc(scat_done, 1)
                dve.wait_ge(looked, 16 * 4 * ET)
                f = [found[:, :, n] for n in range(4)]
                settle()
                for n, (m, own) in enumerate(((f[1], srt[1][:, :, 2]), (f[3], r_f[:, :]))):
                    step(dve.tensor_scalar(has[:, n, :], m, 0.5, None, ALU.is_ge))
                    step(dve.tensor_scalar(alt[:, n, :], own, float(EP), None, ALU.add))
                    settle()
                    step(dve.scalar_tensor_tensor(diff[:, n, :], m, -1.0, alt[:, n, :], ALU.add, ALU.subtract))
                    settle()
                    step(dve.tensor_tensor(pick[:, n, :], diff[:, n, :], has[:, n, :], ALU.mult))
                    settle()
                    step(dve.tensor_tensor(pick[:, 2 + n, :], pick[:, n, :], alt[:, n, :], ALU.add))
                settle()
                di, si = out_d[:, :, :].bitcast(I32), out_s[:, :, :].bitcast(I32)
                dve.tensor_copy(di[:, :, D_SRC], node_i[:, 0, 1, :])
                dve.tensor_copy(di[:, :, D_DST], node_i[:, 0, 0, :])
                dve.tensor_copy(di[:, :, D_OUT], scat_i[:, 0, :])
                dve.tensor_copy(out_d[:, :, KEY], srt[0][:, :, 0])
                dve.tensor_copy(out_d[:, :, D_EW], srt[0][:, :, 4])
                dve.tensor_scalar(si[:, :, S_X2DST], f[0], -1.0, None, ALU.add)
                dve.tensor_copy(si[:, :, S_X2SRC], pick[:, 2, :])
                dve.tensor_scalar(si[:, :, S_X3SRC], f[2], -1.0, None, ALU.add)
                dve.tensor_copy(out_s[:, :, KEY], srt[1][:, :, 0])
                dve.tensor_copy(si[:, :, S_X3DST], pick[:, 3, :])
                dve.tensor_copy(si[:, :, S_OUT], scat_i[:, 1, :])
                dve.tensor_copy(si[:, :, S_EDGE], srt[1][:, :, 3]).then_inc(tabs_done, 1)


def gat_dense(nc, sem, name, src, w, bias, avec, h_out, al_out, from_rows):
    K = w.shape[0]
    KC = K // P
    G = 2 * P
    MACROS = NP // G
    FILLS = KC // 2
    with ExitStack() as ctx:
        sb = lambda n, s, d=F32: ctx.enter_context(nc.sbuf_tensor(f"{name}_{n}", s, d))
        ps = lambda n, s: ctx.enter_context(nc.psum_tensor(f"{name}_{n}", s, F32))
        w_raw = sb("w_raw", [P, 2, HC])
        w_hi = sb("w_hi", [P, KC, HC], F32R)
        w_lo = sb("w_lo", [P, KC, HC], F32R)
        a_rows = sb("a_rows", [P, 2, HC])
        x_in = [sb(f"x_in{s}", [P, 2, K] if from_rows else [P, KC, G]) for s in range(2)]
        act_t = [sb(f"act_t{s}", [P, KC, G]) for s in range(2)] if from_rows else x_in
        x_hi = [sb(f"x_hi{s}", [P, KC, G], F32R) for s in range(2)]
        x_lo = [sb(f"x_lo{s}", [P, KC, G], F32R) for s in range(2)]
        h_sb = [sb(f"h_sb{s}", [P, HC]) for s in range(4)]
        al_sb = [sb(f"al_sb{s}", [P, 2, 2 * H]) for s in range(2)]
        prod = [sb(f"prod{s}", [P, C]) for s in range(2)]
        h_ps = [ps(f"h_ps{s}", [P, HC]) for s in range(2)]
        if from_rows:
            ident = sb("ident", [P, P])
            b_col = sb("b_col", [P, KC])
            t_ps = [ps(f"t_ps{s}", [P, 2, G]) for s in range(2)]

        w_in = [sem(f"{name}_w_in{s}") for s in range(2)]
        a_in = sem(f"{name}_a_in")
        x_loaded = [sem(f"{name}_x_loaded{s}") for s in range(2)]
        h_stored = [sem(f"{name}_h_stored{s}") for s in range(4)]
        al_stored = [sem(f"{name}_al_stored{s}") for s in range(2)]
        w_hi_done = sem(f"{name}_w_hi_done")
        w_lo_done = sem(f"{name}_w_lo_done")
        hi_done = sem(f"{name}_hi_done")
        lo_done = sem(f"{name}_lo_done")
        filled = sem(f"{name}_filled")
        relu_done = sem(f"{name}_relu_done")
        tile_done = sem(f"{name}_tile_done")
        evac_done = sem(f"{name}_evac_done")
        al_done = sem(f"{name}_al_done")
        ident_done = sem(f"{name}_ident_done")

        def rows(ap, m):
            return ap[bass.ds(m * G, G), :].rearrange("(j p) k -> p j k", p=P)

        def x_from(m):
            if from_rows:
                return rows(src, m)
            return src[:, bass.ds(m * G, G)].rearrange("(c p) n -> p c n", p=P)

        def first(i):
            return isinstance(i, int) and i == 0

        with nc.Block() as block:

            @block.sync
            def _(sp):
                for s in range(2):
                    sp.dma_start(x_in[s][:, :, :], x_from(s)).then_inc(x_loaded[s], 16)
                sp.dma_start(a_rows[:, :, :], avec.partition_broadcast(P)).then_inc(a_in, 16)
                if from_rows:
                    sp.dma_start(b_col[:, :], bias).then_inc(a_in, 16)
                for k in range(KC):
                    if k >= 2:
                        sp.wait_ge(w_lo_done, k - 1)
                    sp.dma_start(w_raw[:, k % 2, :], w[k * P:(k + 1) * P, :]).then_inc(w_in[k % 2], 16)

                with sp.Fori(0, MACROS // 2 - 1) as i:
                    for s in range(2):
                        m = 2 * i + s
                        if from_rows:
                            sp.wait_ge(filled, FILLS * (m + 1))
                        else:
                            sp.wait_ge(lo_done, m + 1)
                        sp.dma_start(x_in[s][:, :, :], x_from(m + 2)).then_inc(x_loaded[s], 16)

            @block.gpsimd
            def _(pool):
                if from_rows:
                    pool.memset(ident[:, :], 0.0).then_inc(ident_done, 1)
                    pool.wait_ge(ident_done, 1)
                    pool.affine_select(out=ident[:, :], in_=ident[:, :], compare_op=ALU.not_equal, fill=1.0,
                                       base=0, pattern=[[-1, P]], channel_multiplier=1).then_inc(ident_done, 1)
                with pool.Fori(0, MACROS // 2) as i:
                    for s in range(2):
                        m = 2 * i + s
                        for j in range(2):
                            pool.wait_ge(evac_done, 2 + 2 * m + j + 1)
                            pool.dma_start(h_out[bass.ds(m * G + j * P, P), :],
                                           h_sb[2 * s + j][:, :]).then_inc(h_stored[2 * s + j], 16)
                        pool.wait_ge(al_done, 32 + 16 * (m + 1))
                        pool.dma_start(rows(al_out, m), al_sb[s][:, :, :]).then_inc(al_stored[s], 16)
                for s in range(4):
                    pool.wait_ge(h_stored[s], 16 * (MACROS // 2))
                for s in range(2):
                    pool.wait_ge(al_stored[s], 16 * (MACROS // 2))

            @block.tensor
            def _(pe):
                pe.sem_inc(tile_done, 4)
                if from_rows:
                    pe.wait_ge(ident_done, 2)

                def transposes(m, i, s):
                    if not from_rows:
                        return
                    pe.wait_ge(x_loaded[s], 16 * (i + 1))
                    for f in range(FILLS):
                        pe.wait_ge(relu_done, FILLS * m + f + 1)
                        for c in range(2):
                            for j in range(2):
                                k = 2 * f + c
                                last = pe.transpose(t_ps[f % 2][:, c, j * P:(j + 1) * P],
                                                    x_in[s][:, j, k * P:(k + 1) * P], ident[:, :])
                        last.then_inc(filled, 1)

                def products(m, i, s):
                    pe.wait_ge(lo_done, (FILLS if from_rows else 1) * (m + 1))
                    for j in range(2):
                        pe.wait_ge(evac_done, 2 * m + j + 1)
                        for n in range(2):
                            out = h_ps[j][:, n * 512:(n + 1) * 512]
                            for k in range(KC):
                                xh = x_hi[s][:, k, j * P:(j + 1) * P]
                                xl = x_lo[s][:, k, j * P:(j + 1) * P]
                                wh = w_hi[:, k, n * 512:(n + 1) * 512]
                                wl = w_lo[:, k, n * 512:(n + 1) * 512]
                                pe.matmul(out, xh, wh, start=(k == 0), stop=False)
                                pe.matmul(out, xh, wl, start=False, stop=False)
                                last = pe.matmul(out, xl, wh, start=False, stop=(k == KC - 1))
                        last.then_inc(tile_done, 1)

                transposes(0, 0, 0)
                pe.wait_ge(w_lo_done, KC)

                def body(i, last):
                    transposes(2 * i + 1, i, 1)
                    products(2 * i, i, 0)
                    if not last:
                        transposes(2 * i + 2, i + 1, 0)
                    products(2 * i + 1, i, 1)

                with pe.Fori(0, MACROS // 2 - 1) as i:
                    body(i, False)
                body(MACROS // 2 - 1, True)

            @block.scalar
            def _(act):
                act.sem_inc(evac_done, 2)
                if from_rows:
                    act.sem_inc(relu_done, 2)
                    act.wait_ge(a_in, 32)

                def relus(m, i, s):
                    if not from_rows:
                        return

                    for f in range(FILLS):
                        act.wait_ge(filled, FILLS * m + f + 1)
                        for c in range(2):
                            k = 2 * f + c
                            last = act.activation(act_t[s][:, k, :], t_ps[f % 2][:, c, :], ACT.Relu,
                                                  bias=b_col[:, k:k + 1])
                        last.then_inc(relu_done, 1)

                def evacs(m, i, s):
                    for j in range(2):
                        act.wait_ge(tile_done, 4 + 2 * m + j + 1)
                        if not first(i):
                            act.wait_ge(h_stored[2 * s + j], 16 * i)
                        act.wait_ge(al_done, 8 * (2 * m + j + 1))
                        act.activation(h_sb[2 * s + j][:, :], h_ps[j][:, :], ACT.Copy).then_inc(evac_done, 1)

                relus(0, 0, 0)

                def body(i, last):
                    relus(2 * i + 1, i, 1)
                    evacs(2 * i, i, 0)
                    if not last:
                        relus(2 * i + 2, i + 1, 0)
                    evacs(2 * i + 1, i, 1)

                body(0, False)
                with act.Fori(1, MACROS // 2 - 1) as i:
                    body(i, False)
                body(MACROS // 2 - 1, True)

            @block.vector
            def _(dve):
                dve.sem_inc(al_done, 32)
                def split_w(k):
                    dve.wait_ge(w_in[k % 2], 16 * (k // 2 + 1))
                    dve.tensor_copy(w_hi[:, k, :], w_raw[:, k % 2, :]).then_inc(w_hi_done, 1)
                    dve.wait_ge(w_hi_done, k + 1)
                    dve.tensor_tensor(w_lo[:, k, :], w_raw[:, k % 2, :], w_hi[:, k, :].bitcast(F32),
                                      ALU.subtract).then_inc(w_lo_done, 1)

                def splits(m, i, s):
                    dve.wait_ge(tile_done, 2 * m + 2)
                    if not from_rows:
                        dve.wait_ge(x_loaded[s], 16 * (i + 1))
                        dve.tensor_copy(x_hi[s][:, :, :], x_in[s][:, :, :]).then_inc(hi_done, 1)
                        dve.wait_ge(hi_done, m + 1)
                        dve.tensor_tensor(x_lo[s][:, :, :], x_in[s][:, :, :], x_hi[s][:, :, :].bitcast(F32),
                                          ALU.subtract).then_inc(lo_done, 1)
                        return
                    for f in range(FILLS):
                        ks = slice(2 * f, 2 * f + 2)
                        dve.wait_ge(relu_done, 2 + FILLS * m + f + 1)
                        dve.tensor_copy(x_hi[s][:, ks, :], act_t[s][:, ks, :]).then_inc(hi_done, 1)
                        dve.wait_ge(hi_done, FILLS * m + f + 1)
                        dve.tensor_tensor(x_lo[s][:, ks, :], act_t[s][:, ks, :], x_hi[s][:, ks, :].bitcast(F32),
                                          ALU.subtract).then_inc(lo_done, 1)

                def attention(m, i, s):
                    if not first(i):
                        dve.wait_ge(al_stored[s], 16 * i)
                    for j in range(2):
                        dve.wait_ge(evac_done, 2 + 2 * m + j + 1)
                        for a in range(2):
                            for hd in range(H):
                                cols = slice(hd * C, (hd + 1) * C)
                                dve.wait_ge(al_done, 32 + 16 * m + 8 * j + 4 * a + hd - 1)
                                dve.tensor_tensor_reduce(
                                    prod[hd % 2][:, :], h_sb[2 * s + j][:, cols], a_rows[:, a, cols], 1.0, 0.0,
                                    ALU.mult, ALU.add, al_sb[s][:, j, a * H + hd:a * H + hd + 1]).then_inc(al_done, 1)

                splits(0, 0, 0) if not from_rows else None
                for k in range(KC):
                    split_w(k)
                splits(0, 0, 0) if from_rows else None
                dve.wait_ge(a_in, 32 if from_rows else 16)

                def body(i, last):
                    splits(2 * i + 1, i, 1)
                    attention(2 * i, i, 0)
                    if not last:
                        splits(2 * i + 2, i + 1, 0)
                    attention(2 * i + 1, i, 1)

                body(0, False)
                with dve.Fori(1, MACROS // 2 - 1) as i:
                    body(i, False)
                body(MACROS // 2 - 1, True)


def gat_edges(nc, sem, name, h_rows, al_rows, row_d, tab_d, bounce, w_tab):
    RING = 4
    with ExitStack() as ctx:
        sb = lambda n, s, d=F32: ctx.enter_context(nc.sbuf_tensor(f"{name}_{n}", s, d))
        ps = lambda n, s: ctx.enter_context(nc.psum_tensor(f"{name}_{n}", s, F32))
        tabs = sb("tabs", [P, ET, TAB])
        al_src = sb("al_src", [P, ET, 2 * H])
        al_dst = sb("al_dst", [P, ET, 2 * H])
        keys = sb("keys", [H, EP + 2])
        same = sb("same", [H, EP + 1])
        cut = sb("cut", [H, EP + 1])
        ident = sb("ident", [P, P])
        score = sb("score", [P, 2, H, ET])
        raised = sb("raised", [P, 2, H, ET])
        top_pair = sb("top_pair", [P, H, ET])
        top_t = sb("top_t", [H * ET, P])
        top_row = sb("top_row", [H, EP])
        fwd = sb("fwd", [H, EP])
        bwd = sb("bwd", [H, EP])
        max_t = sb("max_t", [H * ET, P])
        below = sb("below", [P, 2, H, ET])
        w_all = sb("w_all", [P, ET, 2, H])
        last_row = sb("last_row", [P, 1])
        tab = [sb(f"tab{s}", [P, TAB]) for s in range(RING)]
        w = [sb(f"w{s}", [P, 2, H]) for s in range(RING)]
        key_row = [sb(f"key_row{s}", [P, P]) for s in range(RING)]
        h_src = [sb(f"h_src{s}", [P, HC]) for s in range(RING)]
        h_dst = [sb(f"h_dst{s}", [P, HC]) for s in range(RING)]
        mask = [sb(f"mask{s}", [P, H + 2, P]) for s in range(2)]
        sums = [sb(f"sums{s}", [P, HC + H]) for s in range(2)]
        own = [sb(f"own{s}", [P, HC]) for s in range(2)]
        den = sb("den", [P, 2, H])
        rden = sb("rden", [P, 2, H])
        w_own = sb("w_own", [P, 2, H])
        out = sb("out", [P, ET * HC])
        sum_ps = [ps(f"sum_ps{s}", [P, HC]) for s in range(2)]
        den_ps = [ps(f"den_ps{s}", [P, 512]) for s in range(2)]
        t_ps = ps("t_ps", [P, 512])

        small_in = sem(f"{name}_small_in")
        al_in = sem(f"{name}_al_in")
        const_done = sem(f"{name}_const_done")
        v = sem(f"{name}_v")
        top_turned = sem(f"{name}_top_turned")
        top_copied = sem(f"{name}_top_copied")
        bounced = sem(f"{name}_bounced")
        scanned = sem(f"{name}_scanned")
        max_turned = sem(f"{name}_max_turned")
        below_done = sem(f"{name}_below_done")
        w_done = sem(f"{name}_w_done")
        w_stored = sem(f"{name}_w_stored")
        tab_in = [sem(f"{name}_tab_in{s}") for s in range(RING)]
        h_in = [sem(f"{name}_h_in{s}") for s in range(RING)]
        masks_done = sem(f"{name}_masks_done")
        den_done = sem(f"{name}_den_done")
        own_scaled = sem(f"{name}_own_scaled")
        summed = sem(f"{name}_summed")
        sums_out = sem(f"{name}_sums_out")
        finished = sem(f"{name}_finished")
        scattered = sem(f"{name}_scattered")
        zeroed = sem(f"{name}_zeroed")

        with nc.Block() as block:

            @block.sync
            def _(sp):
                sp.dma_start(tabs[:, :, :], tab_d.rearrange("(t p) k -> p t k", p=P)).then_inc(small_in, 16)
                sp.dma_start(keys[:, :], row_d.partition_broadcast(H)).then_inc(small_in, 16)
                sp.wait_ge(top_copied, 1)
                sp.dma_start(bounce[0], top_t[:, :]).then_inc(bounced, 16)
                sp.wait_ge(bounced, 16)
                sp.dma_start(top_row[:, :], bounce[0].rearrange("(h t) p -> h (t p)", h=H)).then_inc(bounced, 16)
                sp.wait_ge(scanned, 3)
                sp.dma_start(bounce[1].rearrange("(h t) p -> h (t p)", h=H), bwd[:, :]).then_inc(bounced, 16)
                sp.wait_ge(bounced, 48)
                sp.dma_start(max_t[:, :], bounce[1]).then_inc(bounced, 16)
                sp.wait_ge(w_done, 1)
                sp.dma_start(w_tab.rearrange("(t p) k -> p t k", p=P),
                             w_all[:, :, :, :].rearrange("p t a h -> p t (a h)")).then_inc(w_stored, 16)
                sp.wait_ge(w_stored, 16)
                sp.wait_ge(zeroed, 3)
                with sp.Fori(0, ET // RING) as i:
                    for s in range(RING):
                        t = RING * i + s
                        sp.wait_ge(finished, t + 1)
                        if s == RING - 1:
                            sp.wait_ge(masks_done, t - 2)
                        sp.dma_start(tab[s][:, :], tab_d[bass.ds(t * P, P), :]).then_inc(tab_in[s], 16)
                        sp.dma_start(w[s][:, :, :].rearrange("p a h -> p (a h)"),
                                     w_tab[bass.ds(t * P, P), :]).then_inc(tab_in[s], 16)
                        sp.dma_start(key_row[s][:, :],
                                     row_d[bass.ds(t * P + 1, P)].partition_broadcast(P)).then_inc(tab_in[s], 16)

            @block.gpsimd
            def _(pool):
                pool.memset(ident[:, :], 0.0).then_inc(const_done, 1)
                pool.memset(last_row[:, :], 0.0).then_inc(const_done, 1)
                pool.wait_ge(const_done, 2)
                pool.affine_select(out=ident[:, :], in_=ident[:, :], compare_op=ALU.not_equal, fill=1.0,
                                   base=0, pattern=[[-1, P]], channel_multiplier=1).then_inc(const_done, 1)
                pool.affine_select(out=last_row[:, :], in_=last_row[:, :], compare_op=ALU.not_equal, fill=1.0,
                                   base=1 - P, pattern=[[0, 1]], channel_multiplier=1).then_inc(const_done, 1)
                pool.wait_ge(small_in, 32)
                index = lambda t, k: bass.IndirectOffsetOnAxis(tabs[:, t, k:k + 1].bitcast(I32), 0)
                for t in range(ET):
                    pool.indirect_dma_start(al_src[:, t, :], None, al_rows, index(t, D_SRC)).then_inc(al_in, 16)
                    pool.indirect_dma_start(al_dst[:, t, :], None, al_rows, index(t, D_DST)).then_inc(al_in, 16)
                for t in range(ET):
                    s = t % RING
                    if t >= RING:
                        pool.wait_ge(finished, t + 1)
                    pool.indirect_dma_start(h_src[s][:, :], None, h_rows[0:NP], index(t, D_SRC)).then_inc(h_in[s], 16)
                    pool.indirect_dma_start(h_dst[s][:, :], None, h_rows[0:NP], index(t, D_DST)).then_inc(h_in[s], 16)
                pool.wait_ge(finished, RING + ET)
                for t in range(ET):
                    pool.indirect_dma_start(h_rows, index(t, D_OUT), out[:, t * HC:(t + 1) * HC],
                                            None).then_inc(scattered, 16)
                pool.wait_ge(scattered, 16 * ET)

            @block.tensor
            def _(pe):
                pe.sem_inc(summed, 2)
                pe.wait_ge(const_done, 4)
                pe.wait_ge(v, 3)
                pe.transpose(t_ps[0:H * ET, 0:P], top_pair[:, :, :].rearrange("p h t -> p (h t)"),
                             ident[:, :]).then_inc(top_turned, 1)
                pe.wait_ge(bounced, 64)
                pe.wait_ge(top_copied, 1)
                pe.transpose(t_ps[:, 128:128 + H * ET], max_t[:, :], ident[0:H * ET, 0:H * ET]).then_inc(max_turned, 1)
                pe.wait_ge(zeroed, 3)
                with pe.Fori(0, ET // RING) as i:
                    for s in range(RING):
                        t = RING * i + s
                        m = mask[s % 2]
                        pe.wait_ge(masks_done, t + 1)
                        pe.wait_ge(h_in[s], 32 * (i + 1))
                        pe.wait_ge(sums_out, t + 1)
                        for hd in range(H):
                            cols = slice(hd * C, (hd + 1) * C)
                            pe.matmul(sum_ps[s % 2][:, cols], m[:, hd, :], h_src[s][:, cols],
                                      start=(hd % 2 == 0), stop=False, skip_group_check=True)
                        pe.matmul(den_ps[s % 2][:, 0:H], m[:, H, :], w[s][:, 0, :], start=True, stop=False)
                        prev = sums[(s + 1) % 2]
                        pe.wait_ge(sums_out, t + 2)
                        pe.matmul(den_ps[s % 2][:, 0:H], m[:, H + 1, :], prev[:, HC:HC + H], start=False, stop=True)
                        for n in range(2):
                            last = pe.matmul(sum_ps[s % 2][:, n * 512:(n + 1) * 512], m[:, H + 1, :],
                                             prev[:, n * 512:(n + 1) * 512], start=False, stop=True,
                                             skip_group_check=True)
                        last.then_inc(summed, 1)

            @block.scalar
            def _(act):
                act.sem_inc(sums_out, 2)
                act.wait_ge(top_turned, 1)
                act.activation(top_t[:, :], t_ps[0:H * ET, 0:P], ACT.Copy).then_inc(top_copied, 1)
                act.wait_ge(below_done, 2)
                act.activation(w_all[:, :, :, :].rearrange("p t a h -> p a h t"), below[:, :, :, :],
                               ACT.Exp).then_inc(w_done, 1)
                with act.Fori(0, ET // RING) as i:
                    for s in range(RING):
                        t = RING * i + s
                        act.wait_ge(summed, t + 3)
                        act.wait_ge(finished, t + 3)
                        act.activation(sums[s % 2][:, 0:HC], sum_ps[s % 2][:, :], ACT.Copy)
                        act.activation(sums[s % 2][:, HC:HC + H], den_ps[s % 2][:, 0:H], ACT.Copy).then_inc(sums_out, 1)

            @block.vector
            def _(dve):
                dve.sem_inc(finished, 4)
                dve.memset(tab[RING - 1][:, :], -5.0).then_inc(zeroed, 1)
                for s in range(2):
                    dve.memset(sums[s][:, :], 0.0).then_inc(zeroed, 1)
                dve.wait_ge(small_in, 32)
                dve.tensor_tensor(same[:, :], keys[:, 0:EP + 1], keys[:, 1:EP + 2], ALU.is_equal).then_inc(v, 1)
                dve.wait_ge(v, 1)
                dve.tensor_scalar(cut[:, :], same[:, :], -1.0, 1e30, ALU.add, ALU.mult)
                dve.wait_ge(al_in, 16 * 2 * ET)
                hv = lambda ap, k: ap[:, :, k * H:(k + 1) * H].rearrange("p t h -> p h t")
                dve.tensor_tensor(score[:, 0, :, :], hv(al_src, 0), hv(al_dst, 1), ALU.add)
                dve.tensor_tensor(score[:, 1, :, :], hv(al_dst, 0), hv(al_dst, 1), ALU.add).then_inc(v, 1)
                dve.wait_ge(v, 2)
                flat = lambda ap: ap[:, :, :, :].rearrange("p a h t -> p (a h t)")
                dve.scalar_tensor_tensor(flat(raised), flat(score), 0.2, flat(score), ALU.mult, ALU.max).then_inc(below_done, 1)
                dve.wait_ge(below_done, 1)
                dve.tensor_tensor(top_pair[:, :, :], raised[:, 0, :, :], raised[:, 1, :, :], ALU.max).then_inc(v, 1)
                dve.wait_ge(bounced, 32)
                dve.tensor_tensor_scan(fwd[:, :], cut[:, 0:EP], top_row[:, :], 0.0, ALU.add, ALU.max).then_inc(scanned, 1)
                dve.wait_ge(scanned, 1)
                dve.tensor_tensor_scan(bwd[:, ::-1], cut[:, EP:0:-1], fwd[:, ::-1], 0.0, ALU.add, ALU.max).then_inc(scanned, 2)
                dve.wait_ge(max_turned, 1)
                mx = t_ps[:, 128:128 + H * ET].rearrange("p (h t) -> p h t", h=H)
                dve.tensor_tensor(below[:, 0, :, :], raised[:, 0, :, :], mx, ALU.subtract)
                dve.tensor_tensor(below[:, 1, :, :], raised[:, 1, :, :], mx, ALU.subtract).then_inc(below_done, 1)

                def masks(i, s, first):
                    dve.wait_ge(tab_in[s], 48 * (i + 1))
                    t = RING * i + s
                    dve.wait_ge(summed, t + 1)
                    key = tab[s][:, KEY:KEY + 1]
                    m = mask[s % 2]
                    for hd in range(H):
                        dve.tensor_scalar(m[:, hd, :], key_row[s][:, :], key, w[s][:, 0, hd:hd + 1],
                                          ALU.is_equal, ALU.mult)
                    dve.tensor_scalar(m[:, H, :], key_row[s][:, :], key, None, ALU.is_equal)
                    dve.tensor_scalar(m[:, H + 1, :], key_row[s][:, :], tab[(s - 1) % RING][:, KEY:KEY + 1],
                                      last_row[:, 0:1], ALU.is_equal, ALU.mult).then_inc(masks_done, 1)

                def finish(i, s):
                    t = RING * i + s
                    q = s % 2
                    dve.wait_ge(sums_out, t + 3)
                    dve.tensor_tensor(den[:, q, :], sums[q][:, HC:HC + H], w[s][:, 1, :], ALU.add).then_inc(den_done, 1)
                    dve.wait_ge(den_done, 3 * t + 1)
                    dve.reciprocal(rden[:, q, :], den[:, q, :]).then_inc(den_done, 1)
                    dve.wait_ge(den_done, 3 * t + 2)
                    dve.tensor_tensor(w_own[:, q, :], rden[:, q, :], w[s][:, 1, :], ALU.mult).then_inc(den_done, 1)
                    dve.wait_ge(den_done, 3 * t + 3)
                    for hd in range(H):
                        cols = slice(hd * C, (hd + 1) * C)
                        last = dve.tensor_scalar(own[q][:, cols], h_dst[s][:, cols], w_own[:, q, hd:hd + 1], None,
                                                 ALU.mult)
                    last.then_inc(own_scaled, 1)
                    dve.wait_ge(own_scaled, t + 1)
                    for hd in range(H):
                        cols = slice(hd * C, (hd + 1) * C)
                        last = dve.scalar_tensor_tensor(out[:, bass.ds(t * HC + hd * C, C)], sums[q][:, cols],
                                                        rden[:, q, hd:hd + 1], own[q][:, cols], ALU.mult, ALU.add)
                    last.then_inc(finished, 1)

                dve.wait_ge(const_done, 4)
                dve.wait_ge(zeroed, 3)
                masks(0, 0, True)

                def body(i, last):
                    for s in range(RING):
                        if s < RING - 1:
                            masks(i, s + 1, False)
                        elif not last:
                            masks(i + 1, 0, False)
                        finish(i, s)

                with dve.Fori(0, ET // RING - 1) as i:
                    body(i, False)
                body(ET // RING - 1, True)


def fc_dense(nc, sem, src, w, bias, x_rows, b_out, x1_out, y_out):
    KC = HC // P
    G = 2 * P
    MACROS = NP // G
    FILLS = KC // 2
    with ExitStack() as ctx:
        sb = lambda n, s, d=F32: ctx.enter_context(nc.sbuf_tensor(f"fc_{n}", s, d))
        ps = lambda n, s: ctx.enter_context(nc.psum_tensor(f"fc_{n}", s, F32))
        w_raw = sb("w_raw", [P, 2, D])
        w_hi = sb("w_hi", [P, KC, D], F32R)
        w_lo = sb("w_lo", [P, KC, D], F32R)
        b_rows = sb("b_rows", [P, 2, D])
        h_in = [sb(f"h_in{s}", [P, 2, HC]) for s in range(2)]
        x_in = [sb(f"x_in{s}", [P, 2, D]) for s in range(2)]
        x_b = [sb(f"x_b{s}", [P, 2, D]) for s in range(2)]
        act_t = [sb(f"act_t{s}", [P, KC, G]) for s in range(2)]
        x_hi = [sb(f"x_hi{s}", [P, KC, G], F32R) for s in range(2)]
        x_lo = [sb(f"x_lo{s}", [P, KC, G], F32R) for s in range(2)]
        ident = sb("ident", [P, P])
        b_col = sb("b_col", [P, KC])
        z = [sb(f"z{s}", [P, 2, D]) for s in range(2)]
        stats = [sb(f"stats{s}", [P, 2, 6]) for s in range(2)]
        mv = [sb(f"mv{s}", [P, 2, 2]) for s in range(2)]
        ds = [sb(f"ds{s}", [P, 4, 2]) for s in range(2)]
        inv = [sb(f"inv{s}", [P, 2, 2]) for s in range(2)]
        rstd = [sb(f"rstd{s}", [P, 2, 2]) for s in range(2)]
        shift = [sb(f"shift{s}", [P, 2, 2]) for s in range(2)]
        x1 = [sb(f"x1{s}", [P, 2, D]) for s in range(2)]
        y = [sb(f"y{s}", [P, 2, D]) for s in range(2)]
        o_ps = [ps(f"o_ps{s}", [P, D]) for s in range(4)]
        t_ps = [ps(f"t_ps{s}", [P, 2, G]) for s in range(2)]

        w_in = [sem(f"fc_w_in{s}") for s in range(2)]
        b_in = sem("fc_b_in")
        h_loaded = [sem(f"fc_h_loaded{s}") for s in range(2)]
        x_loaded = [sem(f"fc_x_loaded{s}") for s in range(2)]
        x1_stored = [sem(f"fc_x1_stored{s}") for s in range(2)]
        y_stored = [sem(f"fc_y_stored{s}") for s in range(2)]
        w_hi_done = sem("fc_w_hi_done")
        w_lo_done = sem("fc_w_lo_done")
        hi_done = sem("fc_hi_done")
        lo_done = sem("fc_lo_done")
        filled = sem("fc_filled")
        relu_done = sem("fc_relu_done")
        tile_done = sem("fc_tile_done")
        xb_done = sem("fc_xb_done")
        summed = sem("fc_summed")
        ln = sem("fc_ln")
        rooted = sem("fc_rooted")
        x1_done = sem("fc_x1_done")
        ident_done = sem("fc_ident_done")
        passed = sem("fc_passed")
        LN_STEPS = 9

        def rows(ap, m):
            return ap[bass.ds(m * G, G), :].rearrange("(j p) k -> p j k", p=P)

        def first(i):
            return isinstance(i, int) and i == 0

        with nc.Block() as block:

            @block.sync
            def _(sp):
                def load(m, s):
                    sp.dma_start(h_in[s][:, :, :], rows(src, m)).then_inc(h_loaded[s], 16)
                    sp.dma_start(x_in[s][:, :, :], rows(x_rows, m)).then_inc(x_loaded[s], 16)

                load(0, 0)
                sp.dma_start(b_col[:, :], bias).then_inc(b_in, 16)
                sp.dma_start(b_rows[:, 0, :], b_out.partition_broadcast(P)).then_inc(b_in, 16)
                sp.dma_start(b_rows[:, 1, :], b_out.partition_broadcast(P)).then_inc(b_in, 16)
                for k in range(KC):
                    if k >= 2:
                        sp.wait_ge(w_lo_done, k - 1)
                    sp.dma_start(w_raw[:, k % 2, :], w[k * P:(k + 1) * P, :]).then_inc(w_in[k % 2], 16)
                load(1, 1)

                with sp.Fori(0, MACROS // 2 - 1) as i:
                    for s in range(2):
                        m = 2 * i + s
                        sp.wait_ge(filled, FILLS * (m + 1))
                        sp.sem_inc(passed, 1)
                        sp.wait_ge(xb_done, m + 3)
                        sp.sem_inc(passed, 1)
                        load(m + 2, s)

            @block.gpsimd
            def _(pool):
                pool.sem_inc(xb_done, 2)
                pool.memset(ident[:, :], 0.0).then_inc(ident_done, 1)
                pool.wait_ge(ident_done, 1)
                pool.affine_select(out=ident[:, :], in_=ident[:, :], compare_op=ALU.not_equal, fill=1.0,
                                   base=0, pattern=[[-1, P]], channel_multiplier=1).then_inc(ident_done, 1)
                pool.wait_ge(b_in, 48)

                def add_bias(m, i, s):
                    pool.wait_ge(x_loaded[s], 16 * (i + 1))
                    pool.wait_ge(summed, 2 * m + 2)
                    pool.tensor_tensor(x_b[s][:, :, :], x_in[s][:, :, :], b_rows[:, :, :], ALU.add).then_inc(xb_done, 1)

                def store(m, i, s):
                    pool.wait_ge(x1_done, m + 3)
                    pool.sem_inc(passed, 1)
                    pool.dma_start(rows(x1_out, m), x1[s][:, :, :]).then_inc(x1_stored[s], 16)
                    pool.wait_ge(ln, LN_STEPS * (m + 1))
                    pool.sem_inc(passed, 1)
                    pool.dma_start(rows(y_out, m), y[s][:, :, :]).then_inc(y_stored[s], 16)

                add_bias(0, 0, 0)

                def body(i, last):
                    add_bias(2 * i + 1, i, 1)
                    store(2 * i, i, 0)
                    if not last:
                        add_bias(2 * i + 2, i + 1, 0)
                    store(2 * i + 1, i, 1)

                with pool.Fori(0, MACROS // 2 - 1) as i:
                    body(i, False)
                body(MACROS // 2 - 1, True)
                for s in range(2):
                    pool.wait_ge(x1_stored[s], 16 * (MACROS // 2))
                    pool.wait_ge(y_stored[s], 16 * (MACROS // 2))

            @block.tensor
            def _(pe):
                pe.sem_inc(tile_done, 4)
                pe.wait_ge(ident_done, 2)

                def transposes(m, i, s):
                    pe.wait_ge(h_loaded[s], 16 * (i + 1))
                    for f in range(FILLS):
                        pe.wait_ge(relu_done, FILLS * m + f + 1)
                        for c in range(2):
                            for j in range(2):
                                k = 2 * f + c
                                last = pe.transpose(t_ps[f % 2][:, c, j * P:(j + 1) * P],
                                                    h_in[s][:, j, k * P:(k + 1) * P], ident[:, :])
                        last.then_inc(filled, 1)

                def products(m, i, s, tiles):
                    pe.wait_ge(lo_done, FILLS * (m + 1))
                    for j in tiles:
                        pe.wait_ge(summed, 2 * m + j + 1)
                        for k in range(KC):
                            xh = x_hi[s][:, k, j * P:(j + 1) * P]
                            xl = x_lo[s][:, k, j * P:(j + 1) * P]
                            out = o_ps[2 * s + j][:, :]
                            pe.matmul(out, xh, w_hi[:, k, :], start=(k == 0), stop=False)
                            pe.matmul(out, xh, w_lo[:, k, :], start=False, stop=False)
                            last = pe.matmul(out, xl, w_hi[:, k, :], start=False, stop=(k == KC - 1))
                        last.then_inc(tile_done, 1)

                transposes(0, 0, 0)
                pe.wait_ge(w_lo_done, KC)

                def body(i, last):
                    products(2 * i, i, 0, [0])
                    transposes(2 * i + 1, i, 1)
                    products(2 * i, i, 0, [1])
                    products(2 * i + 1, i, 1, [0])
                    if not last:
                        transposes(2 * i + 2, i + 1, 0)
                    products(2 * i + 1, i, 1, [1])

                with pe.Fori(0, MACROS // 2 - 1) as i:
                    body(i, False)
                body(MACROS // 2 - 1, True)

            @block.scalar
            def _(act):
                act.sem_inc(relu_done, 2)
                act.sem_inc(x1_done, 2)
                act.wait_ge(b_in, 48)

                def relus(m, i, s):
                    for f in range(FILLS):
                        act.wait_ge(filled, FILLS * m + f + 1)
                        for c in range(2):
                            k = 2 * f + c
                            last = act.activation(act_t[s][:, k, :], t_ps[f % 2][:, c, :], ACT.Relu,
                                                  bias=b_col[:, k:k + 1])
                        last.then_inc(relu_done, 1)

                def normalize(m, i, s):
                    act.wait_ge(ln, LN_STEPS * m + 7)
                    act.activation(rstd[s][:, :, :], inv[s][:, :, :], ACT.Sqrt).then_inc(rooted, 1)
                    act.wait_ge(ln, LN_STEPS * m + 8)
                    if not first(i):
                        act.wait_ge(x1_stored[s], 16 * i)
                    for j in range(2):
                        last = act.activation(x1[s][:, j, :], z[s][:, j, :], ACT.Identity,
                                              bias=shift[s][:, 0, j:j + 1], scale=rstd[s][:, 0, j:j + 1])
                    last.then_inc(x1_done, 1)

                relus(0, 0, 0)

                def body(i, last):
                    relus(2 * i + 1, i, 1)
                    normalize(2 * i, i, 0)
                    if not last:
                        relus(2 * i + 2, i + 1, 0)
                    normalize(2 * i + 1, i, 1)

                body(0, False)
                with act.Fori(1, MACROS // 2 - 1) as i:
                    body(i, False)
                body(MACROS // 2 - 1, True)

            @block.vector
            def _(dve):
                dve.sem_inc(summed, 4)
                for k in range(KC):
                    dve.wait_ge(w_in[k % 2], 16 * (k // 2 + 1))
                    dve.tensor_copy(w_hi[:, k, :], w_raw[:, k % 2, :]).then_inc(w_hi_done, 1)
                    dve.wait_ge(w_hi_done, k + 1)
                    dve.tensor_tensor(w_lo[:, k, :], w_raw[:, k % 2, :], w_hi[:, k, :].bitcast(F32),
                                      ALU.subtract).then_inc(w_lo_done, 1)

                def splits(m, i, s):
                    dve.wait_ge(tile_done, 2 * m + 2)
                    for f in range(FILLS):
                        ks = slice(2 * f, 2 * f + 2)
                        dve.wait_ge(relu_done, 2 + FILLS * m + f + 1)
                        dve.tensor_copy(x_hi[s][:, ks, :], act_t[s][:, ks, :]).then_inc(hi_done, 1)
                        dve.wait_ge(hi_done, FILLS * m + f + 1)
                        dve.tensor_tensor(x_lo[s][:, ks, :], act_t[s][:, ks, :], x_hi[s][:, ks, :].bitcast(F32),
                                          ALU.subtract).then_inc(lo_done, 1)

                def layer_norm(m, i, s):
                    dve.wait_ge(xb_done, m + 3)
                    dve.wait_ge(x1_done, m + 1)
                    for j in range(2):
                        dve.wait_ge(tile_done, 4 + 2 * m + j + 1)
                        dve.tensor_tensor(z[s][:, j, :], o_ps[2 * s + j][:, :], x_b[s][:, j, :], ALU.add).then_inc(summed, 1)
                        dve.wait_ge(summed, 4 + 2 * m + j + 1)
                        last = dve.bn_stats(stats[s][:, j, :], z[s][:, j, :])
                    last.then_inc(ln, 1)
                    dve.wait_ge(ln, LN_STEPS * m + 1)
                    dve.sem_inc(passed, 1)
                    for j in range(2):
                        last = dve.bn_aggr(mv[s][:, j, :], stats[s][:, j, :])
                    last.then_inc(ln, 1)
                    dve.wait_ge(ln, LN_STEPS * m + 2)
                    var = mv[s][:, :, 1]
                    dve.tensor_scalar(ds[s][:, 0, :], var, EPS, None, ALU.add).then_inc(ln, 1)
                    dve.wait_ge(ln, LN_STEPS * m + 3)
                    for n, (a, b) in enumerate(((0, 2), (2, 3), (3, 1))):
                        dve.scalar_tensor_tensor(ds[s][:, b, :], ds[s][:, a, :], EPS, var,
                                                 ALU.mult, ALU.add).then_inc(ln, 1)
                        dve.wait_ge(ln, LN_STEPS * m + 4 + n)
                    dve.reciprocal(inv[s][:, :, :], ds[s][:, 0:2, :]).then_inc(ln, 1)
                    dve.wait_ge(rooted, m + 1)
                    for n in range(2):
                        last = dve.scalar_tensor_tensor(shift[s][:, n, :], mv[s][:, :, 0], -1.0, rstd[s][:, n, :],
                                                        ALU.mult, ALU.mult)
                    last.then_inc(ln, 1)
                    dve.wait_ge(ln, LN_STEPS * m + 8)
                    if not first(i):
                        dve.wait_ge(y_stored[s], 16 * i)
                    for j in range(2):
                        last = dve.tensor_scalar(y[s][:, j, :], z[s][:, j, :], rstd[s][:, 1, j:j + 1],
                                                 shift[s][:, 1, j:j + 1], ALU.mult, ALU.add)
                    last.then_inc(ln, 1)

                dve.wait_ge(b_in, 48)
                splits(0, 0, 0)

                def body(i, last):
                    splits(2 * i + 1, i, 1)
                    layer_norm(2 * i, i, 0)
                    if not last:
                        splits(2 * i + 2, i + 1, 0)
                    layer_norm(2 * i + 1, i, 1)

                body(0, False)
                with dve.Fori(1, MACROS // 2 - 1) as i:
                    body(i, False)
                body(MACROS // 2 - 1, True)


def conv_edges(nc, sem, x1_rows, row_d, tab_d, w, x2_rows, y_rows):
    RING = 4
    KC = D // P
    with ExitStack() as ctx:
        sb = lambda n, s, d=F32: ctx.enter_context(nc.sbuf_tensor(f"conv_{n}", s, d))
        ps = lambda n, s: ctx.enter_context(nc.psum_tensor(f"conv_{n}", s, F32))
        tabs = sb("tabs", [P, ET, TAB])
        w_raw = sb("w_raw", [P, KC, D])
        w_hi = sb("w_hi", [P, KC, D], F32R)
        w_lo = sb("w_lo", [P, KC, D], F32R)
        ident = sb("ident", [P, P])
        last_row = sb("last_row", [P, 1])
        tab = [sb(f"tab{s}", [P, TAB]) for s in range(RING)]
        key_row = [sb(f"key_row{s}", [P, P]) for s in range(RING)]
        x_src = sb("x_src", [P, ET * D])
        x_dst = [sb(f"x_dst{s}", [P, D]) for s in range(RING)]
        mask = [sb(f"mask{s}", [P, 2, P]) for s in range(2)]
        sums = [sb(f"sums{s}", [P, D]) for s in range(2)]
        t_hi = [sb(f"t_hi{s}", [P, KC, P], F32R) for s in range(2)]
        t_lo = [sb(f"t_lo{s}", [P, KC, P], F32R) for s in range(2)]
        z = sb("z", [P, ET * D])
        stats = sb("stats", [P, 2 * ET * 6])
        mv = sb("mv", [P, 2 * ET, 2])
        ds = sb("ds", [P, 3, 2 * ET])
        inv = sb("inv", [P, 2, 2 * ET])
        rstd = sb("rstd", [P, 2, 2 * ET])
        shift = sb("shift", [P, 2, 2 * ET])
        normed = [sb(f"normed{s}", [P, 3, D]) for s in range(3)]
        sum_ps = [ps(f"sum_ps{s}", [P, D]) for s in range(2)]
        t_ps = [ps(f"t_ps{s}", [P, KC, P]) for s in range(2)]
        y_ps = [ps(f"y_ps{s}", [P, D]) for s in range(2)]

        small_in = sem("conv_small_in")
        w_in = sem("conv_w_in")
        w_split = sem("conv_w_split")
        const_done = sem("conv_const_done")
        zeroed = sem("conv_zeroed")
        tab_in = [sem(f"conv_tab_in{s}") for s in range(RING)]
        src_in = [sem(f"conv_src_in{s}") for s in range(RING)]
        dst_in = [sem(f"conv_dst_in{s}") for s in range(RING)]
        masks_done = sem("conv_masks_done")
        summed = sem("conv_summed")
        sums_out = sem("conv_sums_out")
        turned = sem("conv_turned")
        hi_done = sem("conv_hi_done")
        lo_done = sem("conv_lo_done")
        multiplied = sem("conv_multiplied")
        z_done = sem("conv_z_done")
        stats_done = sem("conv_stats_done")
        ln = sem("conv_ln")
        rooted = sem("conv_rooted")
        x2_done = sem("conv_x2_done")
        y_done = sem("conv_y_done")
        stored = [sem(f"conv_stored{s}") for s in range(3)]
        scattered = [sem(f"conv_scattered{s}") for s in range(3)]

        with nc.Block() as block:

            @block.sync
            def _(sp):
                sp.dma_start(tabs[:, :, :], tab_d.rearrange("(t p) k -> p t k", p=P)).then_inc(small_in, 16)
                sp.dma_start(w_raw[:, :, :], w.rearrange("(c p) n -> p c n", p=P)).then_inc(w_in, 16)
                sp.wait_ge(zeroed, 2)
                with sp.Fori(0, ET // RING) as i:
                    for s in range(RING):
                        t = RING * i + s
                        sp.wait_ge(z_done, t + 1)
                        if s == RING - 1:
                            sp.wait_ge(masks_done, t - 2)
                        sp.dma_start(tab[s][:, :], tab_d[bass.ds(t * P, P), :]).then_inc(tab_in[s], 16)
                        sp.dma_start(key_row[s][:, :],
                                     row_d[bass.ds(t * P + 1, P)].partition_broadcast(P)).then_inc(tab_in[s], 16)
                for t in range(ET):
                    out = normed[t % 3]
                    sp.wait_ge(x2_done, t + 1)
                    sp.dma_start(x2_rows[t * P:(t + 1) * P, :], out[:, 0, :]).then_inc(stored[t % 3], 16)
                    sp.dma_start(x2_rows[EP + t * P:EP + (t + 1) * P, :], out[:, 1, :]).then_inc(stored[t % 3], 16)
                for s in range(3):
                    sp.wait_ge(stored[s], 32 * len(range(s, ET, 3)))

            @block.gpsimd
            def _(pool):
                pool.memset(ident[:, :], 0.0).then_inc(const_done, 1)
                pool.memset(last_row[:, :], 0.0).then_inc(const_done, 1)
                pool.wait_ge(const_done, 2)
                pool.affine_select(out=ident[:, :], in_=ident[:, :], compare_op=ALU.not_equal, fill=1.0,
                                   base=0, pattern=[[-1, P]], channel_multiplier=1).then_inc(const_done, 1)
                pool.affine_select(out=last_row[:, :], in_=last_row[:, :], compare_op=ALU.not_equal, fill=1.0,
                                   base=1 - P, pattern=[[0, 1]], channel_multiplier=1).then_inc(const_done, 1)
                pool.wait_ge(small_in, 16)
                index = lambda t, k: bass.IndirectOffsetOnAxis(tabs[:, t, k:k + 1].bitcast(I32), 0)
                for t in range(ET):
                    s = t % RING
                    if t >= RING:
                        pool.wait_ge(z_done, t + 1)
                    pool.indirect_dma_start(x_src[:, t * D:(t + 1) * D], None, x1_rows,
                                            index(t, D_SRC)).then_inc(src_in[s], 16)
                    pool.indirect_dma_start(x_dst[s][:, :], None, x1_rows, index(t, D_DST)).then_inc(dst_in[s], 16)
                for t in range(ET):
                    pool.wait_ge(y_done, t + 1)
                    pool.indirect_dma_start(y_rows, index(t, D_OUT), normed[t % 3][:, 2, :],
                                            None).then_inc(scattered[t % 3], 16)
                for s in range(3):
                    pool.wait_ge(scattered[s], 16 * len(range(s, ET, 3)))

            @block.tensor
            def _(pe):
                pe.sem_inc(summed, 2)
                pe.sem_inc(turned, 2)
                pe.sem_inc(multiplied, 2)
                pe.wait_ge(const_done, 4)
                pe.wait_ge(zeroed, 2)

                def sum_edges(i, s):
                    t = RING * i + s
                    q = s % 2
                    pe.wait_ge(masks_done, t + 1)
                    pe.wait_ge(src_in[s], 16 * (i + 1))
                    pe.wait_ge(sums_out, t + 1)
                    pe.matmul(sum_ps[q][:, :], mask[q][:, 0, :], x_src[:, bass.ds(t * D, D)], start=True, stop=False)
                    pe.wait_ge(sums_out, t + 2)
                    pe.matmul(sum_ps[q][:, :], mask[q][:, 1, :], sums[1 - q][:, :], start=False, stop=True).then_inc(summed, 1)

                def product(i, s):
                    t = RING * i + s
                    q = s % 2
                    pe.wait_ge(sums_out, t + 3)
                    pe.wait_ge(lo_done, t + 1)
                    for k in range(KC):
                        last = pe.transpose(t_ps[q][:, k, :], sums[q][:, k * P:(k + 1) * P], ident[:, :])
                    last.then_inc(turned, 1)
                    pe.wait_ge(lo_done, t + 3)
                    pe.wait_ge(z_done, t + 3)
                    for k in range(KC):
                        pe.matmul(y_ps[q][:, :], t_hi[q][:, k, :], w_hi[:, k, :], start=(k == 0), stop=False)
                        pe.matmul(y_ps[q][:, :], t_hi[q][:, k, :], w_lo[:, k, :], start=False, stop=False)
                        last = pe.matmul(y_ps[q][:, :], t_lo[q][:, k, :], w_hi[:, k, :], start=False, stop=(k == KC - 1))
                    last.then_inc(multiplied, 1)

                pe.wait_ge(w_split, 2)
                sum_edges(0, 0)

                def body(i, last):
                    for s in range(RING):
                        if s < RING - 1:
                            sum_edges(i, s + 1)
                        elif not last:
                            sum_edges(i + 1, 0)
                        product(i, s)

                with pe.Fori(0, ET // RING - 1) as i:
                    body(i, False)
                body(ET // RING - 1, True)

            @block.scalar
            def _(act):
                act.sem_inc(sums_out, 2)
                with act.Fori(0, ET // RING) as i:
                    for s in range(RING):
                        t = RING * i + s
                        act.wait_ge(summed, t + 3)
                        act.wait_ge(turned, t + 1)
                        act.activation(sums[s % 2][:, :], sum_ps[s % 2][:, :], ACT.Copy).then_inc(sums_out, 1)
                act.wait_ge(ln, 5)
                act.activation(rstd[:, :, :], inv[:, :, :], ACT.Sqrt).then_inc(rooted, 1)
                act.wait_ge(ln, 6)
                for t in range(ET):
                    out = normed[t % 3]
                    if t >= 3:
                        act.wait_ge(stored[t % 3], 32 * (t // 3))
                    act.activation(out[:, 0, :], z[:, t * D:(t + 1) * D], ACT.Identity,
                                   bias=shift[:, 0, 2 * t:2 * t + 1], scale=rstd[:, 0, 2 * t:2 * t + 1])
                    act.activation(out[:, 1, :], x_src[:, t * D:(t + 1) * D], ACT.Identity,
                                   bias=shift[:, 0, 2 * t + 1:2 * t + 2],
                                   scale=rstd[:, 0, 2 * t + 1:2 * t + 2]).then_inc(x2_done, 1)

            @block.vector
            def _(dve):
                dve.sem_inc(lo_done, 2)
                dve.sem_inc(z_done, 4)
                dve.memset(tab[RING - 1][:, :], -5.0).then_inc(zeroed, 1)
                dve.memset(sums[1][:, :], 0.0).then_inc(zeroed, 1)
                dve.wait_ge(w_in, 16)
                dve.tensor_copy(w_hi[:, :, :], w_raw[:, :, :]).then_inc(w_split, 1)
                dve.wait_ge(w_split, 1)
                dve.tensor_tensor(w_lo[:, :, :], w_raw[:, :, :], w_hi[:, :, :].bitcast(F32), ALU.subtract).then_inc(w_split, 1)

                def masks(i, s):
                    t = RING * i + s
                    dve.wait_ge(tab_in[s], 32 * (i + 1))
                    dve.wait_ge(summed, t + 1)
                    m = mask[s % 2]
                    dve.tensor_scalar(m[:, 0, :], key_row[s][:, :], tab[s][:, KEY:KEY + 1], tab[s][:, D_EW:D_EW + 1],
                                      ALU.is_equal, ALU.mult)
                    dve.tensor_scalar(m[:, 1, :], key_row[s][:, :], tab[(s - 1) % RING][:, KEY:KEY + 1],
                                      last_row[:, 0:1], ALU.is_equal, ALU.mult).then_inc(masks_done, 1)

                def split(i, s):
                    t = RING * i + s
                    q = s % 2
                    dve.wait_ge(turned, t + 3)
                    dve.wait_ge(multiplied, t + 1)
                    dve.tensor_copy(t_hi[q][:, :, :], t_ps[q][:, :, :]).then_inc(hi_done, 1)
                    dve.wait_ge(hi_done, t + 1)
                    dve.tensor_tensor(t_lo[q][:, :, :], t_ps[q][:, :, :], t_hi[q][:, :, :].bitcast(F32),
                                      ALU.subtract).then_inc(lo_done, 1)

                def finish(i, s):
                    t = RING * i + s
                    dve.bn_stats(stats[:, bass.ds((2 * t + 1) * 6, 6)], x_src[:, bass.ds(t * D, D)])
                    dve.wait_ge(multiplied, t + 3)
                    dve.wait_ge(dst_in[s], 16 * (i + 1))
                    dve.scalar_tensor_tensor(z[:, bass.ds(t * D, D)], y_ps[s % 2][:, :], 0.0, x_dst[s][:, :],
                                             ALU.max, ALU.add).then_inc(z_done, 1)
                    dve.wait_ge(z_done, t + 5)
                    dve.bn_stats(stats[:, bass.ds(2 * t * 6, 6)], z[:, bass.ds(t * D, D)]).then_inc(stats_done, 1)

                dve.wait_ge(const_done, 4)
                dve.wait_ge(zeroed, 2)
                masks(0, 0)

                def body(i, last):
                    for s in range(RING):
                        if s < RING - 1:
                            masks(i, s + 1)
                        elif not last:
                            masks(i + 1, 0)
                        split(i, s)
                        finish(i, s)

                with dve.Fori(0, ET // RING - 1) as i:
                    body(i, False)
                body(ET // RING - 1, True)
                dve.wait_ge(stats_done, ET)
                for n in range(2 * ET):
                    last = dve.bn_aggr(mv[:, n, :], stats[:, 6 * n:6 * n + 6])
                last.then_inc(ln, 1)
                dve.wait_ge(ln, 1)
                var = mv[:, :, 1]
                dve.tensor_scalar(ds[:, 0, :], var, EPS, None, ALU.add).then_inc(ln, 1)
                for n, (a, b) in enumerate(((0, 2), (2, 1))):
                    dve.wait_ge(ln, 2 + n)
                    dve.scalar_tensor_tensor(ds[:, b, :], ds[:, a, :], EPS, var, ALU.mult, ALU.add).then_inc(ln, 1)
                dve.wait_ge(ln, 4)
                dve.reciprocal(inv[:, :, :], ds[:, 0:2, :]).then_inc(ln, 1)
                dve.wait_ge(rooted, 1)
                for n in range(2):
                    last = dve.scalar_tensor_tensor(shift[:, n, :], mv[:, :, 0], -1.0, rstd[:, n, :], ALU.mult, ALU.mult)
                last.then_inc(ln, 1)
                dve.wait_ge(ln, 6)
                for t in range(ET):
                    if t >= 3:
                        dve.wait_ge(scattered[t % 3], 16 * (t // 3))
                    dve.tensor_scalar(normed[t % 3][:, 2, :], z[:, t * D:(t + 1) * D], rstd[:, 1, 2 * t:2 * t + 1],
                                      shift[:, 1, 2 * t:2 * t + 1], ALU.mult, ALU.add).then_inc(y_done, 1)


def painn_filters(nc, sem, attr_t, w1, b1, w2b, y_col, ew_col, u_tab):
    R, F = attr_t.shape[0], w1.shape[1]
    CH = 512
    with ExitStack() as ctx:
        sb = lambda n, s, d=F32: ctx.enter_context(nc.sbuf_tensor(f"filt_{n}", s, d))
        attr = sb("attr", [R, EP])
        w1_sb = sb("w1_sb", [R, F])
        b1_sb = sb("b1_sb", [F, 1])
        w2_sb = sb("w2_sb", [F + 1, 4 * F])
        y = sb("y", [P, ET, 4])
        r = sb("r", [P, ET])
        half = sb("half", [P, 1])
        pre = sb("pre", [F, EP])
        mag = sb("mag", [F, EP])
        decay = sb("decay", [F, EP])
        soft = sb("soft", [F, EP])
        hid = sb("hid", [F + 1, EP])
        yr = sb("yr", [P, 7, ET])
        u = sb("u", [P, ET, 8 * F])
        h_ps = [ctx.enter_context(nc.psum_tensor(f"filt_h_ps{s}", [F, CH], F32)) for s in range(2)]
        f_ps = [ctx.enter_context(nc.psum_tensor(f"filt_f_ps{s}", [P, 4 * F], F32)) for s in range(2)]

        loaded = sem("filt_loaded")
        const_done = sem("filt_const_done")
        multiplied = sem("filt_multiplied")
        pre_out = sem("filt_pre_out")
        soft_steps = sem("filt_soft_steps")
        hid_done = sem("filt_hid_done")
        yr_done = sem("filt_yr_done")
        f_done = sem("filt_f_done")
        u_done = sem("filt_u_done")
        u_stored = sem("filt_u_stored")

        with nc.Block() as block:

            @block.sync
            def _(sp):
                sp.dma_start(attr[:, :], attr_t).then_inc(loaded, 16)
                sp.dma_start(w1_sb[:, :], w1).then_inc(loaded, 16)
                sp.dma_start(b1_sb[:, :], b1).then_inc(loaded, 16)
                sp.dma_start(w2_sb[:, :], w2b[:, 0:4 * F]).then_inc(loaded, 16)
                sp.dma_start(y[:, :, :], y_col).then_inc(loaded, 16)
                sp.dma_start(r[:, :], ew_col).then_inc(loaded, 16)
                sp.wait_ge(u_done, ET)
                sp.dma_start(u_tab.rearrange("(t p) k -> p t k", p=P), u[:, :, :]).then_inc(u_stored, 16)
                sp.wait_ge(u_stored, 16)

            @block.tensor
            def _(pe):
                pe.wait_ge(loaded, 96)
                for n in range(EP // CH):
                    if n >= 2:
                        pe.wait_ge(pre_out, n - 1)
                    pe.matmul(h_ps[n % 2][:, :], w1_sb[:, :], attr[:, n * CH:(n + 1) * CH],
                              start=True, stop=True).then_inc(multiplied, 1)
                pe.wait_ge(hid_done, 2)
                for t in range(ET):
                    if t >= 2:
                        pe.wait_ge(u_done, t - 1)
                    pe.matmul(f_ps[t % 2][:, :], hid[:, t * P:(t + 1) * P], w2_sb[:, :],
                              start=True, stop=True).then_inc(f_done, 1)

            @block.scalar
            def _(act):
                act.wait_ge(loaded, 96)
                for n in range(EP // CH):
                    act.wait_ge(multiplied, n + 1)
                    act.activation(pre[:, n * CH:(n + 1) * CH], h_ps[n % 2][:, :], ACT.Identity,
                                   bias=b1_sb[:, 0:1]).then_inc(pre_out, 1)
                act.wait_ge(pre_out, EP // CH)
                act.activation(mag[:, :], pre[:, :], ACT.Abs).then_inc(soft_steps, 1)
                act.wait_ge(soft_steps, 1)
                act.activation(decay[:, :], mag[:, :], ACT.Exp, scale=-1.0).then_inc(soft_steps, 1)
                act.wait_ge(soft_steps, 2)
                act.wait_ge(const_done, 2)
                act.activation(soft[:, :], decay[:, :], ACT.Ln, bias=half[0:F, 0:1], scale=0.5).then_inc(soft_steps, 1)

            @block.vector
            def _(dve):
                dve.memset(half[:, :], 0.5).then_inc(const_done, 1)
                dve.memset(hid[F:F + 1, :], 1.0).then_inc(const_done, 1)
                dve.wait_ge(loaded, 96)
                for c in range(4):
                    last = dve.tensor_tensor(yr[:, c, :], y[:, :, c], r[:, :], ALU.mult)
                last.then_inc(yr_done, 1)
                dve.wait_ge(yr_done, 1)
                dve.tensor_scalar(yr[:, 4:7, :], yr[:, 1:4, :], 3 ** -0.5, None, ALU.mult).then_inc(yr_done, 1)
                dve.wait_ge(soft_steps, 3)
                dve.scalar_tensor_tensor(hid[0:F, :], pre[:, :], 0.0, soft[:, :], ALU.max, ALU.add).then_inc(hid_done, 2)
                dve.wait_ge(yr_done, 2)
                parts = ((0, 0), (1, 4), (1, 5), (1, 6), (2, 1), (2, 2), (2, 3), (3, 0))
                for t in range(ET):
                    dve.wait_ge(f_done, t + 1)
                    for n, (k, c) in enumerate(parts):
                        last = dve.tensor_scalar(u[:, t, n * F:(n + 1) * F], f_ps[t % 2][:, k * F:(k + 1) * F],
                                                 yr[:, c, t:t + 1], None, ALU.mult)
                    last.then_inc(u_done, 1)


def painn_edges(nc, sem, x2_rows, row_s, tab_s, u_tab, w_in, w_o1s, w_o1v, w_o2s, w_o2v, x3_rows):
    RING = 4
    B = P
    F = w_in.shape[2]
    M_COLS = 4 * F + 3 * 2 * F
    with ExitStack() as ctx:
        sb = lambda n, s, d=F32: ctx.enter_context(nc.sbuf_tensor(f"painn_{n}", s, d))
        ps = lambda n, s: ctx.enter_context(nc.psum_tensor(f"painn_{n}", s, F32))
        tabs = sb("tabs", [P, ET, TAB])
        w_in_sb = sb("w_in_sb", [B, 2, F])
        o1s_raw = sb("o1s_raw", [P, B])
        o1v_raw = sb("o1v_raw", [2 * F, B])
        o1s = sb("o1s", [P, B])
        o1v = sb("o1v", [2 * F, B])
        o2s = sb("o2s", [B, B])
        o2v = sb("o2v", [B, B])
        ident = sb("ident", [P, P])
        last_row = sb("last_row", [P, 1])
        half = sb("half", [P, 1])
        tab = [sb(f"tab{s}", [P, TAB]) for s in range(RING)]
        key_row = [sb(f"key_row{s}", [P, P]) for s in range(RING)]
        x_dst = [sb(f"x_dst{s}", [P, D]) for s in range(RING)]
        x_kept = sb("x_kept", [P, ET * D])
        x_src = [sb(f"x_src{s}", [P, D]) for s in range(RING)]
        u = [sb(f"u{s}", [P, 8 * F]) for s in range(RING)]
        x_t = sb("x_t", [B, 4, P])
        feat = sb("feat", [P, 4, F])
        mask = sb("mask", [P, 2, P])
        msg = sb("msg", [P, M_COLS])
        sums = [sb(f"sums{s}", [P, M_COLS]) for s in range(2)]
        sums_t = sb("sums_t", [P, 4, P])
        hid = sb("hid", [B, 4, P])
        mag = sb("mag", [B, P])
        decay = sb("decay", [B, P])
        soft = sb("soft", [B, P])
        scal = sb("scal", [B, P])
        z = sb("z", [P, ET * D])
        stats = sb("stats", [P, 2 * ET * 6])
        mv = sb("mv", [P, 2 * ET, 2])
        var = sb("var", [P, 2 * ET])
        inv = sb("inv", [P, 2 * ET])
        rstd = sb("rstd", [P, 2 * ET])
        shift = sb("shift", [P, 2 * ET])
        normed = [sb(f"normed{s}", [P, 2, D]) for s in range(3)]
        x_ps = ps("x_ps", [B, 4, P])
        feat_ps = ps("feat_ps", [P, 4, F])
        sum_ps = ps("sum_ps", [P, M_COLS])
        sums_t_ps = ps("sums_t_ps", [P, 4, P])
        o1_ps = ps("o1_ps", [B, 4, P])
        o2_ps = ps("o2_ps", [P, 4, B])

        small_in = sem("painn_small_in")
        w_scaled = sem("painn_w_scaled")
        const_done = sem("painn_const_done")
        zeroed = sem("painn_zeroed")
        tab_in = [sem(f"painn_tab_in{s}") for s in range(RING)]
        x_in = [sem(f"painn_x_in{s}") for s in range(RING)]
        kept = sem("painn_kept")
        x_turned = sem("painn_x_turned")
        xt_out = sem("painn_xt_out")
        feat_done = sem("painn_feat_done")
        feat_out = sem("painn_feat_out")
        masks_done = sem("painn_masks_done")
        msg_done = sem("painn_msg_done")
        summed = sem("painn_summed")
        sums_out = sem("painn_sums_out")
        sums_turned = sem("painn_sums_turned")
        st_out = sem("painn_st_out")
        o1_done = sem("painn_o1_done")
        o1_out = sem("painn_o1_out")
        soft_steps = sem("painn_soft_steps")
        scal_done = sem("painn_scal_done")
        o2_done = sem("painn_o2_done")
        z_done = sem("painn_z_done")
        stats_done = sem("painn_stats_done")
        ln = sem("painn_ln")
        rooted = sem("painn_rooted")
        own_done = sem("painn_own_done")
        far_done = sem("painn_far_done")
        stored = [sem(f"painn_stored{s}") for s in range(3)]

        with nc.Block() as block:

            @block.sync
            def _(sp):
                sp.dma_start(tabs[:, :, :], tab_s.rearrange("(t p) k -> p t k", p=P)).then_inc(small_in, 16)
                sp.dma_start(w_in_sb[:, :, :], w_in).then_inc(small_in, 16)
                sp.dma_start(o1s_raw[0:F, :], w_o1s[0:F, :]).then_inc(small_in, 16)
                for c in range(3):
                    sp.dma_start(o1s_raw[(1 + c) * F:(2 + c) * F, :], w_o1s[F:2 * F, :]).then_inc(small_in, 16)
                sp.dma_start(o1v_raw[:, :], w_o1v).then_inc(small_in, 16)
                sp.dma_start(o2s[:, :], w_o2s).then_inc(small_in, 16)
                sp.dma_start(o2v[:, :], w_o2v).then_inc(small_in, 16)
                sp.wait_ge(zeroed, 3)
                with sp.Fori(0, ET // RING) as i:
                    for s in range(RING):
                        t = RING * i + s
                        sp.wait_ge(z_done, t + 1)
                        if s == RING - 1:
                            sp.wait_ge(masks_done, t - 2)
                        sp.dma_start(tab[s][:, :], tab_s[bass.ds(t * P, P), :]).then_inc(tab_in[s], 16)
                        sp.dma_start(key_row[s][:, :],
                                     row_s[bass.ds(t * P + 1, P)].partition_broadcast(P)).then_inc(tab_in[s], 16)
                for t in range(ET):
                    out = normed[t % 3]
                    sp.wait_ge(own_done, t + 1)
                    sp.dma_start(x3_rows[t * P:(t + 1) * P, :], out[:, 0, :]).then_inc(stored[t % 3], 16)
                    sp.wait_ge(far_done, t + 1)
                    sp.dma_start(x3_rows[EP + t * P:EP + (t + 1) * P, :], out[:, 1, :]).then_inc(stored[t % 3], 16)
                for s in range(3):
                    sp.wait_ge(stored[s], 32 * len(range(s, ET, 3)))

            @block.gpsimd
            def _(pool):
                pool.memset(ident[:, :], 0.0).then_inc(const_done, 1)
                pool.memset(last_row[:, :], 0.0).then_inc(const_done, 1)
                pool.memset(half[:, :], 0.5).then_inc(const_done, 1)
                pool.wait_ge(const_done, 3)
                pool.affine_select(out=ident[:, :], in_=ident[:, :], compare_op=ALU.not_equal, fill=1.0,
                                   base=0, pattern=[[-1, P]], channel_multiplier=1).then_inc(const_done, 1)
                pool.affine_select(out=last_row[:, :], in_=last_row[:, :], compare_op=ALU.not_equal, fill=1.0,
                                   base=1 - P, pattern=[[0, 1]], channel_multiplier=1).then_inc(const_done, 1)
                pool.wait_ge(small_in, 16 * 9)
                index = lambda t, k: bass.IndirectOffsetOnAxis(tabs[:, t, k:k + 1].bitcast(I32), 0)

                def keep(t):
                    pool.wait_ge(x_in[t % RING], 48 * (t // RING + 1))
                    pool.tensor_copy(x_kept[:, t * D:(t + 1) * D], x_dst[t % RING][:, :]).then_inc(kept, 1)

                for t in range(ET):
                    s = t % RING
                    if t >= RING:
                        keep(t - RING)
                        pool.wait_ge(z_done, t + 1)
                        pool.wait_ge(kept, t - RING + 1)
                    pool.indirect_dma_start(x_dst[s][:, :], None, x2_rows,
                                            index(t, S_X2DST)).then_inc(x_in[s], 16)
                    pool.indirect_dma_start(u[s][:, :], None, u_tab, index(t, S_EDGE)).then_inc(x_in[s], 16)
                    pool.indirect_dma_start(x_src[s][:, :], None, x2_rows, index(t, S_X2SRC)).then_inc(x_in[s], 16)
                for t in range(ET - RING, ET):
                    keep(t)

            @block.tensor
            def _(pe):
                for done in (feat_done, o1_done, o2_done, summed):
                    pe.sem_inc(done, 1)
                pe.wait_ge(const_done, 5)
                pe.wait_ge(w_scaled, 2)
                pe.wait_ge(zeroed, 3)

                def turn_x(i, s):
                    t = RING * i + s
                    pe.wait_ge(x_in[s], 48 * (i + 1))
                    pe.wait_ge(xt_out, t + 1)
                    pe.transpose(x_ps[:, 0, :], x_dst[s][:, 0:B], ident[:, :])
                    vec = x_dst[s][:, B:D].rearrange("p (b c) -> p c b", c=3)
                    for c in range(3):
                        last = pe.transpose(x_ps[:, 1 + c, :], vec[:, c, :], ident[:, :])
                    last.then_inc(x_turned, 1)

                def features(i, s):
                    t = RING * i + s
                    pe.wait_ge(xt_out, t + 2)
                    pe.wait_ge(feat_out, t + 1)
                    for c in range(4):
                        last = pe.matmul(feat_ps[:, c, :], x_t[:, c, :], w_in_sb[:, min(c, 1), :], start=True, stop=True)
                    last.then_inc(feat_done, 1)

                def sum_edges(i, s):
                    t = RING * i + s
                    pe.wait_ge(masks_done, t + 1)
                    pe.wait_ge(msg_done, 3 * t + 4)
                    pe.wait_ge(sums_out, t + 1)
                    pe.matmul(sum_ps[:, :], mask[:, 0, :], msg[:, :], start=True, stop=False)
                    pe.matmul(sum_ps[:, :], mask[:, 1, :], sums[(s + 1) % 2][:, :], start=False, stop=True).then_inc(summed, 1)

                def turn_sums(i, s):
                    t = RING * i + s
                    pe.wait_ge(sums_out, t + 2)
                    pe.wait_ge(st_out, 2 * t + 1)
                    pe.transpose(sums_t_ps[:, 0, :], sums[s % 2][:, 0:4 * F], ident[:, :])
                    for c in range(3):
                        last = pe.transpose(sums_t_ps[0:2 * F, 1 + c, :], sums[s % 2][:, (4 + 2 * c) * F:(6 + 2 * c) * F],
                                            ident[:, :])
                    last.then_inc(sums_turned, 1)

                def out_one(i, s):
                    t = RING * i + s
                    pe.wait_ge(st_out, 2 * t + 3)
                    pe.wait_ge(o1_out, t + 1)
                    pe.matmul(o1_ps[:, 0, :], o1s[:, :], sums_t[:, 0, :], start=True, stop=True)
                    pe.matmul(o1_ps[:, 1:4, :], o1v[:, :], sums_t[0:2 * F, 1:4, :], start=True, stop=True).then_inc(o1_done, 1)

                def out_two(i, s):
                    t = RING * i + s
                    pe.wait_ge(o1_out, t + 2)
                    pe.wait_ge(z_done, t + 4)
                    for c in range(3):
                        pe.matmul(o2_ps[:, 1 + c, :], hid[:, 1 + c, :], o2v[:, :], start=True, stop=True)
                    pe.wait_ge(scal_done, t + 2)
                    pe.matmul(o2_ps[:, 0, :], scal[:, :], o2s[:, :], start=True, stop=True).then_inc(o2_done, 1)

                turn_x(0, 0)
                features(0, 0)
                sum_edges(0, 0)

                def body(i, last):
                    for s in range(RING):
                        nxt = (i, s + 1) if s < RING - 1 else None if last else (i + 1, 0)
                        if nxt:
                            turn_x(*nxt)
                        turn_sums(i, s)
                        if nxt:
                            features(*nxt)
                        out_one(i, s)
                        if nxt:
                            sum_edges(*nxt)
                        out_two(i, s)

                with pe.Fori(0, ET // RING - 1) as i:
                    body(i, False)
                body(ET // RING - 1, True)

            @block.scalar
            def _(act):
                for done in (xt_out, feat_out, sums_out, st_out, o1_out):
                    act.sem_inc(done, 1)
                act.wait_ge(const_done, 5)

                def copy_xt(i, s):
                    t = RING * i + s
                    act.wait_ge(x_turned, t + 1)
                    act.wait_ge(feat_done, t + 1)
                    act.activation(x_t[:, :, :], x_ps[:, :, :], ACT.Copy).then_inc(xt_out, 1)

                def copy_features(i, s):
                    t = RING * i + s
                    act.wait_ge(feat_done, t + 2)
                    act.wait_ge(msg_done, 3 * t + 1)
                    act.activation(feat[:, :, :], feat_ps[:, :, :], ACT.Copy, scale=B ** -0.5).then_inc(feat_out, 1)

                def copy_sums(i, s):
                    t = RING * i + s
                    act.wait_ge(summed, t + 2)
                    act.activation(sums[s % 2][:, :], sum_ps[:, :], ACT.Copy).then_inc(sums_out, 1)

                def copy_sums_t(i, s):
                    t = RING * i + s
                    act.wait_ge(sums_turned, t + 1)
                    act.wait_ge(o1_done, t + 1)
                    act.activation(sums_t[:, 0, :], sums_t_ps[:, 0, :], ACT.Copy).then_inc(st_out, 1)
                    act.activation(sums_t[0:2 * F, 1:4, :], sums_t_ps[0:2 * F, 1:4, :], ACT.Copy).then_inc(st_out, 1)

                def softplus(i, s):
                    t = RING * i + s
                    act.wait_ge(o1_done, t + 2)
                    act.wait_ge(o2_done, t + 1)
                    act.wait_ge(scal_done, t + 1)
                    act.activation(hid[:, :, :], o1_ps[:, :, :], ACT.Copy).then_inc(o1_out, 1)
                    act.wait_ge(o1_out, t + 2)
                    act.activation(mag[:, :], hid[:, 0, :], ACT.Abs).then_inc(soft_steps, 1)
                    act.wait_ge(soft_steps, 3 * t + 1)
                    act.activation(decay[:, :], mag[:, :], ACT.Exp, scale=-1.0).then_inc(soft_steps, 1)
                    act.wait_ge(soft_steps, 3 * t + 2)
                    act.activation(soft[:, :], decay[:, :], ACT.Ln, bias=half[:, 0:1], scale=0.5).then_inc(soft_steps, 1)

                copy_xt(0, 0)
                copy_features(0, 0)

                def body(i, last):
                    for s in range(RING):
                        nxt = (i, s + 1) if s < RING - 1 else None if last else (i + 1, 0)
                        copy_sums(i, s)
                        if nxt:
                            copy_xt(*nxt)
                        copy_sums_t(i, s)
                        if nxt:
                            copy_features(*nxt)
                        softplus(i, s)

                with act.Fori(0, ET // RING - 1) as i:
                    body(i, False)
                body(ET // RING - 1, True)
                act.wait_ge(ln, 3)
                act.activation(rstd[:, :], inv[:, :], ACT.Sqrt).then_inc(rooted, 1)
                act.wait_ge(ln, 4)
                for t in range(ET):
                    if t >= 3:
                        act.wait_ge(stored[t % 3], 32 * (t // 3))
                    act.activation(normed[t % 3][:, 0, :], z[:, t * D:(t + 1) * D], ACT.Identity,
                                   bias=shift[:, 2 * t:2 * t + 1], scale=rstd[:, 2 * t:2 * t + 1]).then_inc(own_done, 1)

            @block.vector
            def _(dve):
                for done in (msg_done, scal_done):
                    dve.sem_inc(done, 1)
                dve.sem_inc(z_done, 4)
                dve.memset(tab[RING - 1][:, :], -5.0).then_inc(zeroed, 1)
                for s in range(2):
                    dve.memset(sums[s][:, :], 0.0).then_inc(zeroed, 1)
                dve.wait_ge(small_in, 16 * 9)
                dve.tensor_scalar(o1s[:, :], o1s_raw[:, :], (2 * F) ** -0.5, None, ALU.mult).then_inc(w_scaled, 1)
                dve.tensor_scalar(o1v[:, :], o1v_raw[:, :], (2 * F) ** -0.5, None, ALU.mult).then_inc(w_scaled, 1)
                dve.wait_ge(const_done, 5)
                dve.wait_ge(zeroed, 3)

                def masks(i, s):
                    t = RING * i + s
                    dve.wait_ge(tab_in[s], 32 * (i + 1))
                    dve.wait_ge(summed, t + 1)
                    dve.tensor_scalar(mask[:, 0, :], key_row[s][:, :], tab[s][:, KEY:KEY + 1], None, ALU.is_equal)
                    dve.tensor_scalar(mask[:, 1, :], key_row[s][:, :], tab[(s - 1) % RING][:, KEY:KEY + 1],
                                      last_row[:, 0:1], ALU.is_equal, ALU.mult).then_inc(masks_done, 1)

                def messages(i, s):
                    t = RING * i + s
                    dve.wait_ge(x_in[s], 48 * (i + 1))
                    dve.bn_stats(stats[:, bass.ds((2 * t + 1) * 6, 6)], x_dst[s][:, :])
                    dve.wait_ge(feat_out, t + 2)
                    dve.wait_ge(summed, t + 1)
                    flat = feat[:, :, :].rearrange("p c f -> p (c f)")
                    dve.tensor_tensor(msg[:, 0:4 * F], flat, u[s][:, 0:4 * F], ALU.mult).then_inc(msg_done, 1)
                    pairs = msg[:, 4 * F:].rearrange("p (c k f) -> p k c f", c=3, k=2)
                    dve.tensor_tensor(pairs[:, 0, :, :], feat[:, 0:1, :].to_broadcast([P, 3, F]),
                                      u[s][:, 4 * F:7 * F].rearrange("p (c f) -> p c f", c=3), ALU.mult).then_inc(msg_done, 1)
                    dve.tensor_tensor(pairs[:, 1, :, :], feat[:, 1:4, :],
                                      u[s][:, 7 * F:8 * F].rearrange("p (c f) -> p c f", c=1).to_broadcast([P, 3, F]),
                                      ALU.mult).then_inc(msg_done, 1)

                def finish(i, s):
                    t = RING * i + s
                    dve.wait_ge(soft_steps, 3 * t + 3)
                    dve.wait_ge(o2_done, t + 1)
                    dve.scalar_tensor_tensor(scal[:, :], hid[:, 0, :], 0.0, soft[:, :], ALU.max, ALU.add).then_inc(scal_done, 1)
                    dve.wait_ge(o2_done, t + 2)
                    dve.scalar_tensor_tensor(z[:, bass.ds(t * D, B)], o2_ps[:, 0, :], B ** -0.5, x_src[s][:, 0:B],
                                             ALU.mult, ALU.add)
                    vec = lambda ap: ap.rearrange("p (d c) -> p c d", c=3)
                    dve.scalar_tensor_tensor(vec(z[:, bass.ds(t * D + B, 3 * B)]), o2_ps[:, 1:4, :], B ** -0.5,
                                             vec(x_src[s][:, B:D]), ALU.mult, ALU.add).then_inc(z_done, 1)
                    dve.wait_ge(z_done, t + 5)
                    dve.bn_stats(stats[:, bass.ds(2 * t * 6, 6)], z[:, bass.ds(t * D, D)]).then_inc(stats_done, 1)

                masks(0, 0)
                messages(0, 0)

                def body(i, last):
                    for s in range(RING):
                        nxt = (i, s + 1) if s < RING - 1 else None if last else (i + 1, 0)
                        if nxt:
                            masks(*nxt)
                            messages(*nxt)
                        finish(i, s)

                with dve.Fori(0, ET // RING - 1) as i:
                    body(i, False)
                body(ET // RING - 1, True)
                dve.wait_ge(stats_done, ET)
                for n in range(2 * ET):
                    last = dve.bn_aggr(mv[:, n, :], stats[:, 6 * n:6 * n + 6])
                last.then_inc(ln, 1)
                dve.wait_ge(ln, 1)
                dve.tensor_scalar(var[:, :], mv[:, :, 1], EPS, None, ALU.add).then_inc(ln, 1)
                dve.wait_ge(ln, 2)
                dve.reciprocal(inv[:, :], var[:, :]).then_inc(ln, 1)
                dve.wait_ge(rooted, 1)
                dve.scalar_tensor_tensor(shift[:, :], mv[:, :, 0], -1.0, rstd[:, :], ALU.mult, ALU.mult).then_inc(ln, 1)
                dve.wait_ge(ln, 4)
                dve.wait_ge(kept, ET)
                for t in range(ET):
                    if t >= 3:
                        dve.wait_ge(stored[t % 3], 32 * (t // 3))
                    n = 2 * t + 1
                    dve.tensor_scalar(normed[t % 3][:, 1, :], x_kept[:, t * D:(t + 1) * D], rstd[:, n:n + 1],
                                      shift[:, n:n + 1], ALU.mult, ALU.add).then_inc(far_done, 1)


def mlp_edges(nc, sem, x3_rows, row_s, tab_s, w_t, b, y_rows):
    RING = 4
    KC = 2 * D // P
    with ExitStack() as ctx:
        sb = lambda n, s, d=F32: ctx.enter_context(nc.sbuf_tensor(f"mlp_{n}", s, d))
        ps = lambda n, s: ctx.enter_context(nc.psum_tensor(f"mlp_{n}", s, F32))
        tabs = sb("tabs", [P, ET, TAB])
        w_raw = sb("w_raw", [P, 2, D])
        w_hi = sb("w_hi", [P, KC, D], F32R)
        w_lo = sb("w_lo", [P, KC, D], F32R)
        b_rows = sb("b_rows", [P, D])
        ident = sb("ident", [P, P])
        last_row = sb("last_row", [P, 1])
        tab = [sb(f"tab{s}", [P, TAB]) for s in range(RING)]
        key_row = [sb(f"key_row{s}", [P, P]) for s in range(RING)]
        pair = [sb(f"pair{s}", [P, 2, D]) for s in range(RING)]
        mask = [sb(f"mask{s}", [P, 2, P]) for s in range(2)]
        t_hi = [sb(f"t_hi{s}", [P, KC, P], F32R) for s in range(2)]
        t_lo = [sb(f"t_lo{s}", [P, KC, P], F32R) for s in range(2)]
        pre = [sb(f"pre{s}", [P, D]) for s in range(2)]
        msg = [sb(f"msg{s}", [P, D]) for s in range(2)]
        sums = [sb(f"sums{s}", [P, D]) for s in range(2)]
        z = sb("z", [P, ET * D])
        stats = sb("stats", [P, ET * 6])
        mv = sb("mv", [P, ET, 2])
        var = sb("var", [P, ET])
        inv = sb("inv", [P, ET])
        rstd = sb("rstd", [P, ET])
        shift = sb("shift", [P, ET])
        y = [sb(f"y{s}", [P, D]) for s in range(4)]
        t_ps = [ps(f"t_ps{s}", [P, KC // 2, P]) for s in range(2)]
        m_ps = [ps(f"m_ps{s}", [P, D]) for s in range(2)]
        sum_ps = [ps(f"sum_ps{s}", [P, D]) for s in range(2)]

        small_in = sem("mlp_small_in")
        w_in = [sem(f"mlp_w_in{s}") for s in range(2)]
        w_hi_done = sem("mlp_w_hi_done")
        w_lo_done = sem("mlp_w_lo_done")
        const_done = sem("mlp_const_done")
        zeroed = sem("mlp_zeroed")
        tab_in = [sem(f"mlp_tab_in{s}") for s in range(RING)]
        pair_in = [sem(f"mlp_pair_in{s}") for s in range(RING)]
        turned = sem("mlp_turned")
        hi_done = sem("mlp_hi_done")
        lo_done = sem("mlp_lo_done")
        multiplied = sem("mlp_multiplied")
        pre_done = sem("mlp_pre_done")
        msg_done = sem("mlp_msg_done")
        masks_done = sem("mlp_masks_done")
        summed = sem("mlp_summed")
        sums_out = sem("mlp_sums_out")
        z_done = sem("mlp_z_done")
        stats_done = sem("mlp_stats_done")
        ln = sem("mlp_ln")
        rooted = sem("mlp_rooted")
        even_done = sem("mlp_even_done")
        odd_done = sem("mlp_odd_done")
        scattered = [sem(f"mlp_scattered{s}") for s in range(4)]

        with nc.Block() as block:

            @block.sync
            def _(sp):
                sp.dma_start(tabs[:, :, :], tab_s.rearrange("(t p) k -> p t k", p=P)).then_inc(small_in, 16)
                sp.dma_start(b_rows[:, :], b.partition_broadcast(P)).then_inc(small_in, 16)
                for k in range(KC):
                    if k >= 2:
                        sp.wait_ge(w_lo_done, k - 1)
                    sp.dma_start(w_raw[:, k % 2, :], w_t[k * P:(k + 1) * P, :]).then_inc(w_in[k % 2], 16)
                sp.wait_ge(zeroed, 3)
                with sp.Fori(0, ET // RING) as i:
                    for s in range(RING):
                        t = RING * i + s
                        sp.wait_ge(z_done, t + 1)
                        if s == RING - 1:
                            sp.wait_ge(masks_done, t - 2)
                        sp.dma_start(tab[s][:, :], tab_s[bass.ds(t * P, P), :]).then_inc(tab_in[s], 16)
                        sp.dma_start(key_row[s][:, :],
                                     row_s[bass.ds(t * P + 1, P)].partition_broadcast(P)).then_inc(tab_in[s], 16)

            @block.gpsimd
            def _(pool):
                pool.memset(ident[:, :], 0.0).then_inc(const_done, 1)
                pool.memset(last_row[:, :], 0.0).then_inc(const_done, 1)
                pool.wait_ge(const_done, 2)
                pool.affine_select(out=ident[:, :], in_=ident[:, :], compare_op=ALU.not_equal, fill=1.0,
                                   base=0, pattern=[[-1, P]], channel_multiplier=1).then_inc(const_done, 1)
                pool.affine_select(out=last_row[:, :], in_=last_row[:, :], compare_op=ALU.not_equal, fill=1.0,
                                   base=1 - P, pattern=[[0, 1]], channel_multiplier=1).then_inc(const_done, 1)
                pool.wait_ge(small_in, 32)
                index = lambda t, k: bass.IndirectOffsetOnAxis(tabs[:, t, k:k + 1].bitcast(I32), 0)
                for t in range(ET):
                    s = t % RING
                    if t >= RING:
                        pool.wait_ge(z_done, t + 1)
                    pool.indirect_dma_start(pair[s][:, 0, :], None, x3_rows, index(t, S_X3SRC)).then_inc(pair_in[s], 16)
                    pool.indirect_dma_start(pair[s][:, 1, :], None, x3_rows, index(t, S_X3DST)).then_inc(pair_in[s], 16)
                for t in range(ET):
                    pool.wait_ge((even_done, odd_done)[t % 2], t // 2 + 1)
                    pool.indirect_dma_start(y_rows, index(t, S_OUT), y[t % 4][:, :], None).then_inc(scattered[t % 4], 16)
                for s in range(4):
                    pool.wait_ge(scattered[s], 16 * len(range(s, ET, 4)))

            @block.tensor
            def _(pe):
                pe.sem_inc(multiplied, 2)
                pe.sem_inc(summed, 2)
                pe.wait_ge(const_done, 4)

                def turn(i, s):
                    t = RING * i + s
                    pe.wait_ge(pair_in[s], 32 * (i + 1))
                    for n in range(2):
                        pe.wait_ge(lo_done, 2 * t + n + 1)
                        for k in range(KC // 2):
                            last = pe.transpose(t_ps[n][:, k, :], pair[s][:, n, k * P:(k + 1) * P], ident[:, :])
                        last.then_inc(turned, 1)

                def product(i, s):
                    t = RING * i + s
                    q = s % 2
                    pe.wait_ge(pre_done, t + 1)
                    for k in range(KC):
                        if k % (KC // 2) == 0:
                            pe.wait_ge(lo_done, 2 * t + 3 if k else 2 * t + 2)
                        pe.matmul(m_ps[q][:, :], t_hi[q][:, k, :], w_hi[:, k, :], start=(k == 0), stop=False)
                        pe.matmul(m_ps[q][:, :], t_hi[q][:, k, :], w_lo[:, k, :], start=False, stop=False)
                        last = pe.matmul(m_ps[q][:, :], t_lo[q][:, k, :], w_hi[:, k, :], start=False, stop=(k == KC - 1))
                    last.then_inc(multiplied, 1)

                def sum_edges(i, s):
                    t = RING * i + s
                    q = s % 2
                    pe.wait_ge(masks_done, t + 1)
                    pe.wait_ge(msg_done, t + 3)
                    pe.wait_ge(sums_out, t + 1)
                    pe.matmul(sum_ps[q][:, :], mask[q][:, 0, :], msg[q][:, :], start=True, stop=False)
                    pe.wait_ge(sums_out, t + 2)
                    pe.matmul(sum_ps[q][:, :], mask[q][:, 1, :], sums[1 - q][:, :], start=False, stop=True).then_inc(summed, 1)

                pe.wait_ge(zeroed, 3)
                turn(0, 0)
                pe.wait_ge(w_lo_done, KC)
                product(0, 0)
                turn(0, 1)

                def body(i, last):
                    for s in range(RING):
                        if s + 1 < RING:
                            product(i, s + 1)
                        elif not last:
                            product(i + 1, 0)
                        if s + 2 < RING:
                            turn(i, s + 2)
                        elif not last:
                            turn(i + 1, s + 2 - RING)
                        sum_edges(i, s)

                with pe.Fori(0, ET // RING - 1) as i:
                    body(i, False)
                body(ET // RING - 1, True)

            @block.scalar
            def _(act):
                act.sem_inc(sums_out, 2)
                act.sem_inc(msg_done, 2)

                def relu(i, s):
                    t = RING * i + s
                    act.wait_ge(pre_done, t + 3)
                    act.wait_ge(summed, t + 1)
                    act.activation(msg[s % 2][:, :], pre[s % 2][:, :], ACT.Relu).then_inc(msg_done, 1)

                def copy_sums(i, s):
                    t = RING * i + s
                    act.wait_ge(summed, t + 3)
                    act.wait_ge(z_done, t + 3)
                    act.activation(sums[s % 2][:, :], sum_ps[s % 2][:, :], ACT.Copy).then_inc(sums_out, 1)

                relu(0, 0)

                def body(i, last):
                    for s in range(RING):
                        if s + 1 < RING:
                            relu(i, s + 1)
                        elif not last:
                            relu(i + 1, 0)
                        copy_sums(i, s)

                with act.Fori(0, ET // RING - 1) as i:
                    body(i, False)
                body(ET // RING - 1, True)
                act.wait_ge(ln, 3)
                act.activation(rstd[:, :], inv[:, :], ACT.Sqrt).then_inc(rooted, 1)
                act.wait_ge(ln, 4)
                for t in range(0, ET, 2):
                    if t >= 4:
                        act.wait_ge(scattered[t % 4], 16 * (t // 4))
                    act.activation(y[t % 4][:, :], z[:, t * D:(t + 1) * D], ACT.Identity, bias=shift[:, t:t + 1],
                                   scale=rstd[:, t:t + 1]).then_inc(even_done, 1)

            @block.vector
            def _(dve):
                dve.sem_inc(lo_done, 1)
                dve.sem_inc(pre_done, 2)
                dve.sem_inc(z_done, 4)
                dve.memset(tab[RING - 1][:, :], -5.0).then_inc(zeroed, 1)
                for s in range(2):
                    dve.memset(sums[s][:, :], 0.0).then_inc(zeroed, 1)
                for k in range(KC):
                    dve.wait_ge(w_in[k % 2], 16 * (k // 2 + 1))
                    dve.tensor_copy(w_hi[:, k, :], w_raw[:, k % 2, :]).then_inc(w_hi_done, 1)
                    dve.wait_ge(w_hi_done, k + 1)
                    dve.tensor_tensor(w_lo[:, k, :], w_raw[:, k % 2, :], w_hi[:, k, :].bitcast(F32),
                                      ALU.subtract).then_inc(w_lo_done, 1)

                def split(i, s):
                    t = RING * i + s
                    q = s % 2
                    dve.wait_ge(multiplied, t + 1)
                    for n in range(2):
                        ks = slice(n * KC // 2, (n + 1) * KC // 2)
                        dve.wait_ge(turned, 2 * t + n + 1)
                        dve.tensor_copy(t_hi[q][:, ks, :], t_ps[n][:, :, :]).then_inc(hi_done, 1)
                        dve.wait_ge(hi_done, 2 * t + n + 1)
                        dve.tensor_tensor(t_lo[q][:, ks, :], t_ps[n][:, :, :], t_hi[q][:, ks, :].bitcast(F32),
                                          ALU.subtract).then_inc(lo_done, 1)

                def masks(i, s):
                    t = RING * i + s
                    dve.wait_ge(tab_in[s], 32 * (i + 1))
                    dve.wait_ge(summed, t + 1)
                    m = mask[s % 2]
                    dve.tensor_scalar(m[:, 0, :], key_row[s][:, :], tab[s][:, KEY:KEY + 1], None, ALU.is_equal)
                    dve.tensor_scalar(m[:, 1, :], key_row[s][:, :], tab[(s - 1) % RING][:, KEY:KEY + 1],
                                      last_row[:, 0:1], ALU.is_equal, ALU.mult).then_inc(masks_done, 1)

                def add_bias(i, s):
                    t = RING * i + s
                    dve.wait_ge(multiplied, t + 3)
                    dve.wait_ge(msg_done, t + 1)
                    dve.tensor_tensor(pre[s % 2][:, :], m_ps[s % 2][:, :], b_rows[:, :], ALU.add).then_inc(pre_done, 1)

                def finish(i, s):
                    t = RING * i + s
                    dve.wait_ge(sums_out, t + 3)
                    dve.wait_ge(pair_in[s], 32 * (i + 1))
                    dve.tensor_tensor(z[:, bass.ds(t * D, D)], sums[s % 2][:, :], pair[s][:, 0, :], ALU.add).then_inc(z_done, 1)
                    dve.wait_ge(z_done, t + 5)
                    dve.bn_stats(stats[:, bass.ds(t * 6, 6)], z[:, bass.ds(t * D, D)]).then_inc(stats_done, 1)

                dve.wait_ge(small_in, 32)
                dve.wait_ge(const_done, 4)
                dve.wait_ge(zeroed, 3)
                split(0, 0)
                masks(0, 0)
                add_bias(0, 0)
                split(0, 1)

                def body(i, last):
                    for s in range(RING):
                        if s + 1 < RING:
                            masks(i, s + 1)
                            add_bias(i, s + 1)
                        elif not last:
                            masks(i + 1, 0)
                            add_bias(i + 1, 0)
                        if s + 2 < RING:
                            split(i, s + 2)
                        elif not last:
                            split(i + 1, s + 2 - RING)
                        finish(i, s)

                with dve.Fori(0, ET // RING - 1) as i:
                    body(i, False)
                body(ET // RING - 1, True)
                dve.wait_ge(stats_done, ET)
                for t in range(ET):
                    last = dve.bn_aggr(mv[:, t, :], stats[:, 6 * t:6 * t + 6])
                last.then_inc(ln, 1)
                dve.wait_ge(ln, 1)
                dve.tensor_scalar(var[:, :], mv[:, :, 1], EPS, None, ALU.add).then_inc(ln, 1)
                dve.wait_ge(ln, 2)
                dve.reciprocal(inv[:, :], var[:, :]).then_inc(ln, 1)
                dve.wait_ge(rooted, 1)
                dve.scalar_tensor_tensor(shift[:, :], mv[:, :, 0], -1.0, rstd[:, :], ALU.mult, ALU.mult).then_inc(ln, 1)
                dve.wait_ge(ln, 4)
                for t in range(1, ET, 2):
                    if t >= 4:
                        dve.wait_ge(scattered[t % 4], 16 * (t // 4))
                    dve.tensor_scalar(y[t % 4][:, :], z[:, t * D:(t + 1) * D], rstd[:, t:t + 1], shift[:, t:t + 1],
                                      ALU.mult, ALU.add).then_inc(odd_done, 1)


def graph_layers(nc, x_t, x, ends_row, ends_col, ew_col, attr20_t, attr4_col, w1, a1, b1, w2, a2, b2, wfc, bfc,
                 conv_w, w_in, pw1, pb1, pw2b, w_o1s, w_o1v, w_o2s, w_o2v, mlp_w_t, mlp_b, out):
    table = lambda n, s: nc.dram_tensor(n, s, F32, kind="Internal").ap()
    rec_d, rec_s = table("rec_d", [EP, REC]), table("rec_s", [EP, REC])
    row_d, row_s = table("row_d", [EP + 2]), table("row_s", [EP + 2])
    map_d, map_s = table("map_d", [NT, 1]), table("map_s", [NT, 1])
    tab_d, tab_s = table("tab_d", [EP, TAB]), table("tab_s", [EP, TAB])
    h1, al1 = table("h1", [NT, HC]), table("al1", [NP, 2 * H])
    h2, al2 = table("h2", [NT, HC]), table("al2", [NP, 2 * H])
    bounce1, bounce2 = table("bounce1", [2, H * ET, P]), table("bounce2", [2, H * ET, P])
    w_tab1, w_tab2 = table("w_tab1", [EP, 2 * H]), table("w_tab2", [EP, 2 * H])
    x1 = table("x1", [NP, D])
    x2, x3 = table("x2", [2 * EP, D]), table("x3", [2 * EP, D])
    u_tab = table("u_tab", [EP, 256])
    def stage(build, *args):
        held = []

        def sem(name):
            held.append(nc.alloc_semaphore(name=name))
            return held[-1]

        build(nc, sem, *args)
        nc.clear_and_free_semaphores(held)
        nc.all_engine_barrier()

    stage(edge_prep, ends_row, ends_col, ew_col, rec_d, rec_s, row_d, row_s, map_d, map_s, tab_d, tab_s)
    stage(painn_filters, attr20_t, pw1, pb1, pw2b, attr4_col, ew_col, u_tab)
    stage(gat_dense, "g1", x_t, w1, None, a1, h1, al1, False)
    stage(gat_edges, "e1", h1, al1, row_d, tab_d, bounce1, w_tab1)
    stage(gat_dense, "g2", h1, w2, b1, a2, h2, al2, True)
    stage(gat_edges, "e2", h2, al2, row_d, tab_d, bounce2, w_tab2)
    stage(fc_dense, h2, wfc, b2, x, bfc, x1, out)
    stage(conv_edges, x1, row_d, tab_d, conv_w, x2, out)
    stage(painn_edges, x2, row_s, tab_s, u_tab, w_in, w_o1s, w_o1v, w_o2s, w_o2v, x3)
    stage(mlp_edges, x3, row_s, tab_s, mlp_w_t, mlp_b, out)


def kernel(**inputs):
    import numpy as np
    import concourse.bacc as bacc
    from concourse.bass_utils import run_bass_kernel_spmd

    a = {k: np.asarray(v) for k, v in inputs.items()}
    g = lambda layer, name: a[f"L{layer}_gnn_{name}"]

    def padded(v, rows):
        return np.concatenate([v, np.zeros((rows - v.shape[0],) + v.shape[1:], v.dtype)])

    own = np.arange(N, N + EP - E, dtype=np.int32)
    ends = np.stack([np.concatenate([a[k].astype(np.int32), own]) for k in ("dst", "src")])
    x = padded(a["x"], NP)
    tiled = lambda v: padded(v, EP).reshape(ET, P, -1).transpose(1, 0, 2)
    columns = lambda v: v.reshape(-1, P).T
    pw2 = np.concatenate([g(2, "W2"), g(2, "b2")[None]])
    pw2 = pw2.reshape(pw2.shape[0], -1, 6).transpose(0, 2, 1).reshape(pw2.shape[0], -1)
    ins = [x.T, x, ends, ends.reshape(2, ET, P).transpose(2, 0, 1), tiled(a["edge_weight"])[:, :, 0],
           padded(a["edge_attr_20"], EP).T, tiled(a["edge_attr_4"]),
           g(0, "W1"), np.stack([g(0, "a_src1").ravel(), g(0, "a_dst1").ravel()]), columns(g(0, "b1")),
           g(0, "W2"), np.stack([g(0, "a_src2").ravel(), g(0, "a_dst2").ravel()]), columns(g(0, "b2")),
           g(0, "Wfc"), g(0, "bfc"), g(1, "weight"), np.stack([g(2, "w_in2f_s"), g(2, "w_in2f_v")], 1),
           g(2, "W1"), g(2, "b1")[:, None], pw2, g(2, "w_f2o1_s"), g(2, "w_f2o1_v"), g(2, "w_f2o2_s"),
           g(2, "w_f2o2_v"), g(3, "W").T, g(3, "b")]

    nc = bacc.Bacc("TRN2", target_bir_lowering=False, num_devices=1)
    arrays, args = {}, []
    for n, v in enumerate(ins):
        v = np.ascontiguousarray(v)
        arrays[f"in_{n}_dram"] = v
        args.append(nc.dram_tensor(f"in_{n}_dram", list(v.shape), mybir.dt.from_np(v.dtype), kind="ExternalInput").ap())
    out = nc.dram_tensor("out_0_dram", [NT, D], F32, kind="ExternalOutput").ap()
    graph_layers(nc, *args, out)
    r = run_bass_kernel_spmd(nc, [arrays], core_ids=[0])
    return r.results[0]["out_0_dram"][:N]
```

```python
from contextlib import ExitStack

import concourse.bass as bass
from concourse import mybir

F32 = mybir.dt.float32
F32R = mybir.dt.float32r
I32 = mybir.dt.int32
ALU = mybir.AluOpType
ACT = mybir.ActivationFunctionType

P = 128
N, E = 10000, 2500
NP = -(-N // (4 * P)) * 4 * P
ET = -(-E // P)
EP = ET * P
NT = NP + EP
H, C = 4, 256
HC = H * C
D = 512
EPS = 1e-5

REC = 8
TAB = 8
D_SRC, D_DST, D_OUT, KEY, D_EW = range(5)
S_X2DST, S_X2SRC, S_X3SRC, _, S_X3DST, S_OUT, S_EDGE = range(7)


def dense_and_prep(nc, sem, x_t, w, avec, h_out, al_out, ends_row, ends_col, ew_col, rec_d, rec_s, row_d, row_s,
                   map_d, map_s, tab_d, tab_s, attr_t, fw1, fb1, fw2b, attr4_col, u_tab):
    KC = w.shape[0] // P
    G = 2 * P
    MACROS = NP // G
    PASSES = MACROS // 2
    R, F = attr_t.shape[0], fw1.shape[1]
    CH = 512
    CHUNKS = EP // CH
    PER = 4
    RANKED = ET // PER
    GROUPS = ET // PER
    with ExitStack() as ctx:
        sb = lambda n, s, d=F32: ctx.enter_context(nc.sbuf_tensor(f"g1_{n}", s, d))
        ps = lambda n, s: ctx.enter_context(nc.psum_tensor(f"g1_{n}", s, F32))
        w_raw = sb("w_raw", [P, 2, HC])
        w_hi = sb("w_hi", [P, KC, HC], F32R)
        w_lo = sb("w_lo", [P, KC, HC], F32R)
        a_rows = sb("a_rows", [P, 2, HC])
        x_in = [sb(f"x_in{s}", [P, KC, G]) for s in range(2)]
        x_hi = [sb(f"x_hi{s}", [P, KC, G], F32R) for s in range(2)]
        x_lo = [sb(f"x_lo{s}", [P, KC, G], F32R) for s in range(2)]
        h_sb = [sb(f"h_sb{s}", [P, HC]) for s in range(4)]
        al_sb = [sb(f"al_sb{s}", [P, 2, 2 * H]) for s in range(2)]
        prod = [sb(f"prod{s}", [P, C]) for s in range(2)]
        row = [sb(f"row{o}", [P, EP]) for o in range(2)]
        signs = [sb(f"signs{q}", [P, EP]) for q in range(2)]
        tile_row, int_row = (buffer[:, :].bitcast(I32) for buffer in signs)
        ties = sb("ties", [P, 2 * PER, P])
        int_col = sb("int_col", [P, 2, ET], I32)
        tile_col = sb("tile_col", [P, ET], I32)
        node = sb("node", [P, 2, ET])
        col = sb("col", [P, 2, ET])
        neg = sb("neg", [P, 2, ET])
        lower = sb("lower", [P, P])
        later = sb("later", [P, 2, ET])
        tied = sb("tied", [P, 2, ET])
        before = sb("before", [P, 2, ET])
        rank = sb("rank", [P, 2, ET])
        rank_i = sb("rank_i", [P, 2, ET], I32)
        weight = sb("weight", [P, ET])
        rec = [sb(f"rec{o}", [P, ET, REC]) for o in range(2)]
        srt = [sb(f"srt{o}", [P, ET, REC]) for o in range(2)]
        nxt = [sb(f"nxt{o}", [P, ET, REC]) for o in range(2)]
        ends = sb("ends", [1, 2, REC])
        zero = sb("zero", [P, NT // P])
        r_i = sb("r_i", [P, ET], I32)
        r_f = sb("r_f", [P, ET])
        dump = sb("dump", [P, ET])
        r1 = sb("r1", [P, ET])
        r_next = sb("r_next", [P, ET], I32)
        is_last = sb("is_last", [P, 2, ET])
        off = sb("off", [P, 2, ET])
        cut = sb("cut", [P, 2, ET])
        where = sb("where", [P, 2, ET])
        scat_i = sb("scat_i", [P, 2, ET], I32)
        node_i = sb("node_i", [P, 2, 2, ET], I32)
        found = sb("found", [P, ET, 4])
        has = sb("has", [P, 2, ET])
        alt = sb("alt", [P, 2, ET])
        diff = sb("diff", [P, 2, ET])
        gap = sb("gap", [P, 2, ET])
        pick = sb("pick", [P, 2, ET])
        out_d = sb("out_d", [P, ET, TAB])
        out_s = sb("out_s", [P, ET, TAB])
        attr = sb("attr", [R, EP])
        fw1_sb = sb("fw1_sb", [R, F])
        fb1_sb = sb("fb1_sb", [F, 1])
        fw2_sb = sb("fw2_sb", [F + 1, 4 * F])
        y = sb("y", [P, ET, 4])
        half = sb("half", [F, 1])
        pre = sb("pre", [F, EP])
        mag = sb("mag", [F, EP])
        hid = sb("hid", [F + 1, EP])
        yr = sb("yr", [P, 7, ET])
        u = [sb(f"u{s}", [P, PER, 8 * F]) for s in range(2)]
        h_ps = [ps(f"h_ps{s}", [P, HC]) for s in range(2)]
        f_ps = [ps(f"f_ps{s}", [P, PER, 4 * F]) for s in range(4)]

        w_in = [sem(f"g1_w_in{s}") for s in range(2)]
        a_in = sem("g1_a_in")
        x_loaded = [sem(f"g1_x_loaded{s}") for s in range(2)]
        h_stored = [sem(f"g1_h_stored{s}") for s in range(4)]
        al_stored = [sem(f"g1_al_stored{s}") for s in range(2)]
        w_hi_done = sem("g1_w_hi_done")
        w_lo_done = sem("g1_w_lo_done")
        hi_done = sem("g1_hi_done")
        lo_done = sem("g1_lo_done")
        tile_done = sem("g1_tile_done")
        evac_done = sem("g1_evac_done")
        al_done = sem("g1_al_done")
        passed = sem("g1_passed")
        cols_in = sem("prep_cols_in")
        rows_in = [sem(f"prep_rows_in{o}") for o in range(2)]
        row_done = [sem(f"prep_row_done{o}") for o in range(2)]
        zeroed = sem("prep_zeroed")
        const_done = sem("prep_const_done")
        lower_set = sem("prep_lower_set")
        v = sem("prep_v")
        signed = sem("prep_signed")
        tied_done = sem("prep_tied_done")
        ranked = sem("prep_ranked")
        scattered = [sem(f"prep_scattered{o}") for o in range(2)]
        sorted_in = sem("prep_sorted_in")
        rows_out = sem("prep_rows_out")
        scat_done = sem("prep_scat_done")
        mapped = sem("prep_mapped")
        looked = sem("prep_looked")
        tabs_done = sem("prep_tabs_done")
        tabs_out = sem("prep_tabs_out")
        f_loaded = sem("filt_loaded")
        f_multiplied = sem("filt_multiplied")
        pre_out = sem("filt_pre_out")
        soft_steps = sem("filt_soft_steps")
        hid_done = sem("filt_hid_done")
        f_done = sem("filt_f_done")
        u_done = sem("filt_u_done")
        u_stored = [sem(f"filt_u_stored{s}") for s in range(2)]

        CONST = 6

        def first(i):
            return isinstance(i, int) and i == 0

        with nc.Block() as block:

            @block.sync
            def _(sp):
                def load(m, s):
                    sp.dma_start(x_in[s][:, :, :],
                                 x_t[:, bass.ds(m * G, G)].rearrange("(c p) n -> p c n", p=P)).then_inc(x_loaded[s], 16)

                def store(m, s):
                    for j in range(2):
                        sp.wait_ge(evac_done, 2 + 2 * m + j + 1)
                        sp.sem_inc(passed, 1)
                        sp.dma_start(h_out[bass.ds(m * G + j * P, P), :], h_sb[2 * s + j][:, :]).then_inc(h_stored[2 * s + j], 16)
                    sp.wait_ge(al_done, 32 + 16 * (m + 1))
                    sp.sem_inc(passed, 1)
                    sp.dma_start(al_out[bass.ds(m * G, G), :].rearrange("(j p) k -> p j k", p=P),
                                 al_sb[s][:, :, :]).then_inc(al_stored[s], 16)

                def loop(start, stop):
                    with sp.Fori(start, stop) as i:
                        for s in range(2):
                            m = 2 * i + s
                            sp.wait_ge(lo_done, m + 1)
                            sp.sem_inc(passed, 1)
                            load(m + 2, s)
                            store(m, s)

                load(0, 0)
                for k in range(2):
                    sp.dma_start(w_raw[:, k, :], w[k * P:(k + 1) * P, :]).then_inc(w_in[k], 16)
                load(1, 1)
                for k in range(2, KC):
                    sp.wait_ge(w_lo_done, k - 1)
                    sp.dma_start(w_raw[:, k % 2, :], w[k * P:(k + 1) * P, :]).then_inc(w_in[k % 2], 16)
                sp.dma_start(a_rows[:, :, :], avec.partition_broadcast(P)).then_inc(a_in, 16)
                loop(0, 9)
                for o, (rec_in, row_out) in enumerate(((rec_d, row_d), (rec_s, row_s))):
                    sp.wait_ge(scattered[o], 16 * ET)
                    sp.dma_start(srt[o][:, :, :], rec_in[0:EP].rearrange("(t p) k -> p t k", p=P)).then_inc(sorted_in, 16)
                    sp.dma_start(nxt[o][:, :, :], rec_in[1:EP + 1].rearrange("(t p) k -> p t k", p=P)).then_inc(sorted_in, 16)
                    sp.dma_start(row_out[1:EP + 1], rec_in[0:EP, 0:1].rearrange("a b -> (a b)"),
                                 allow_slow_non_contiguous=True).then_inc(rows_out, 16)
                loop(9, PASSES - 1)
                for s in range(2):
                    store(MACROS - 2 + s, s)
                for s in range(4):
                    sp.wait_ge(h_stored[s], 16 * PASSES)
                for s in range(2):
                    sp.wait_ge(al_stored[s], 16 * PASSES)
                sp.wait_ge(rows_out, 32)

            @block.gpsimd
            def _(pool):
                pool.dma_start(int_col[:, :, :], ends_col).then_inc(cols_in, 16)
                pool.dma_start(weight[:, :], ew_col).then_inc(cols_in, 16)
                pool.dma_start(int_row, ends_row[0].partition_broadcast(P)).then_inc(rows_in[0], 16)
                pool.iota(tile_row, [[1, ET], [0, P]], base=0, channel_multiplier=0).then_inc(const_done, 1)
                pool.iota(tile_col[:, :], [[1, ET]], base=0, channel_multiplier=0).then_inc(const_done, 1)
                pool.memset(zero[:, :], 0.0).then_inc(const_done, 1)
                pool.iota(r_i[:, :], [[P, ET]], base=0, channel_multiplier=1).then_inc(const_done, 1)
                pool.iota(r_next[:, :], [[P, ET]], base=NP, channel_multiplier=1).then_inc(const_done, 1)
                pool.memset(lower[:, :], 1.0).then_inc(lower_set, 1)
                pool.wait_ge(lower_set, 1)
                pool.affine_select(out=lower[:, :], in_=lower[:, :], compare_op=ALU.is_gt, fill=0.0,
                                   base=0, pattern=[[-1, P]], channel_multiplier=1).then_inc(const_done, 1)
                pool.wait_ge(row_done[0], 1)
                pool.dma_start(int_row, ends_row[1].partition_broadcast(P)).then_inc(rows_in[1], 16)
                pool.dma_start(attr[:, :], attr_t).then_inc(f_loaded, 16)
                pool.dma_start(fw1_sb[:, :], fw1).then_inc(f_loaded, 16)
                pool.dma_start(fb1_sb[:, :], fb1).then_inc(f_loaded, 16)
                pool.dma_start(fw2_sb[:, :], fw2b[:, 0:4 * F]).then_inc(f_loaded, 16)
                pool.dma_start(y[:, :, :], attr4_col).then_inc(f_loaded, 16)
                pool.wait_ge(const_done, CONST)
                pool.wait_ge(v, 1)
                for map_out in (map_d, map_s):
                    pool.dma_start(map_out.rearrange("(p k) o -> p (k o)", p=P), zero[:, :]).then_inc(zeroed, 16)
                for row_out, rec_out in ((row_d, rec_d), (row_s, rec_s)):
                    pool.dma_start(row_out[0:1].rearrange("(a b) -> a b", a=1), ends[0:1, 0, 0:1]).then_inc(zeroed, 16)
                    pool.dma_start(row_out[EP + 1:EP + 2].rearrange("(a b) -> a b", a=1), ends[0:1, 1, 0:1]).then_inc(zeroed, 16)
                    pool.dma_start(rec_out[EP:EP + 1, :], ends[0:1, 1, :]).then_inc(zeroed, 16)
                pool.wait_ge(zeroed, 16 * 8)
                pool.wait_ge(ranked, 2)
                for o, rec_out in enumerate((rec_d, rec_s)):
                    for t in range(ET):
                        pool.indirect_dma_start(rec_out, bass.IndirectOffsetOnAxis(rank_i[:, o, t:t + 1], 0),
                                                rec[o][:, t, :], None).then_inc(scattered[o], 16)
                pool.wait_ge(scat_done, 1)
                for o, map_out in enumerate((map_d, map_s)):
                    for t in range(ET):
                        pool.indirect_dma_start(map_out, bass.IndirectOffsetOnAxis(scat_i[:, o, t:t + 1], 0),
                                                r1[:, t:t + 1], None).then_inc(mapped, 16)
                pool.wait_ge(mapped, 32 * ET)
                for n, (map_in, end) in enumerate(((map_d, 1), (map_d, 0), (map_s, 0), (map_s, 1))):
                    for t in range(ET):
                        pool.indirect_dma_start(
                            found[:, t, n:n + 1], None, map_in,
                            bass.IndirectOffsetOnAxis(node_i[:, 1, end, t:t + 1], 0)).then_inc(looked, 16)
                for g in range(GROUPS):
                    pool.wait_ge(u_done, g + 1)
                    pool.dma_start(u_tab[g * PER * P:(g + 1) * PER * P].rearrange("(t p) k -> p t k", p=P),
                                   u[g % 2][:, :, :]).then_inc(u_stored[g % 2], 16)
                pool.wait_ge(tabs_done, 1)
                pool.dma_start(tab_d.rearrange("(t p) k -> p t k", p=P), out_d[:, :, :]).then_inc(tabs_out, 16)
                pool.dma_start(tab_s.rearrange("(t p) k -> p t k", p=P), out_s[:, :, :]).then_inc(tabs_out, 16)
                pool.wait_ge(tabs_out, 32)
                for s in range(2):
                    pool.wait_ge(u_stored[s], 16 * len(range(s, GROUPS, 2)))

            @block.tensor
            def _(pe):
                pe.sem_inc(tile_done, 4)

                def products(m, i, s):
                    pe.wait_ge(lo_done, m + 1)
                    for j in range(2):
                        pe.wait_ge(evac_done, 2 * m + j + 1)
                        for n in range(2):
                            out = h_ps[j][:, n * 512:(n + 1) * 512]
                            for k in range(KC):
                                if first(m) and j == n == 0:
                                    pe.wait_ge(w_lo_done, k + 1)
                                xh = x_hi[s][:, k, j * P:(j + 1) * P]
                                xl = x_lo[s][:, k, j * P:(j + 1) * P]
                                wh = w_hi[:, k, n * 512:(n + 1) * 512]
                                wl = w_lo[:, k, n * 512:(n + 1) * 512]
                                pe.matmul(out, xh, wh, start=(k == 0), stop=False)
                                pe.matmul(out, xh, wl, start=False, stop=False)
                                last = pe.matmul(out, xl, wh, start=False, stop=(k == KC - 1))
                        last.then_inc(tile_done, 1)

                def body(i):
                    for s in range(2):
                        products(2 * i + s, i, s)

                def loop(start, stop):
                    with pe.Fori(start, stop) as i:
                        body(i)

                def hidden(n):
                    if n >= 4:
                        pe.wait_ge(pre_out, n - 3)
                    pe.matmul(f_ps[n % 4][0:F, :, :], fw1_sb[:, :], attr[:, n * CH:(n + 1) * CH],
                              start=True, stop=True).then_inc(f_multiplied, 1)

                def factors(g):
                    if g >= 4:
                        pe.wait_ge(u_done, g - 3)
                    for t in range(PER):
                        e = (PER * g + t) * P
                        last = pe.matmul(f_ps[g % 4][:, t, :], hid[:, e:e + P], fw2_sb[:, :], start=True, stop=True)
                    last.then_inc(f_done, 1)

                body(0)
                loop(1, RANKED)
                pe.wait_ge(f_loaded, 80)
                for n in range(4):
                    hidden(n)
                body(RANKED)
                for n in range(4, CHUNKS):
                    hidden(n)
                loop(RANKED + 1, RANKED + 3)
                pe.wait_ge(hid_done, 2)
                for g in range(4):
                    factors(g)
                loop(RANKED + 3, RANKED + 6)
                for g in range(4, GROUPS):
                    factors(g)
                loop(RANKED + 6, PASSES)

            @block.scalar
            def _(act):
                act.sem_inc(evac_done, 2)
                n_signs = 0

                def evac(m, i, s, j):
                    act.wait_ge(tile_done, 4 + 2 * m + j + 1)
                    if not first(i):
                        act.wait_ge(h_stored[2 * s + j], 16 * i)
                    act.wait_ge(al_done, 8 * (2 * m + j + 1))
                    act.activation(h_sb[2 * s + j][:, :], h_ps[j][:, :], ACT.Copy).then_inc(evac_done, 1)

                def count(i, n):
                    o, t = n % 2, PER * i + n // 2
                    if first(i) and n < 2:
                        act.wait_ge(row_done[0], 1)
                        act.wait_ge(row_done[1], 1)
                    else:
                        act.wait_ge(signed, 2 * PER * i + n - 1)
                    act.activation(signs[n % 2][:, :], row[o][:, :], ACT.Sign, bias=neg[:, o, bass.ds(t, 1)],
                                   accum_out=later[:, o, bass.ds(t, 1)]).then_inc(signed, 1)

                def body(i, ranking):
                    for s in range(2):
                        for j in range(2):
                            evac(2 * i + s, i, s, j)
                            if ranking:
                                count(i, 4 * s + 2 * j)
                                count(i, 4 * s + 2 * j + 1)

                def copy_hidden(n):
                    act.wait_ge(f_multiplied, n + 1)
                    act.activation(pre[:, n * CH:(n + 1) * CH], f_ps[n % 4][0:F, :, :].rearrange("f t k -> f (t k)"),
                                   ACT.Identity, bias=fb1_sb[:, 0:1]).then_inc(pre_out, 1)

                body(0, True)
                with act.Fori(1, RANKED) as i:
                    body(i, True)
                act.wait_ge(f_loaded, 80)
                for n in range(4):
                    copy_hidden(n)
                body(RANKED, False)
                for n in range(4, CHUNKS):
                    copy_hidden(n)
                act.wait_ge(pre_out, CHUNKS)
                act.activation(mag[:, :], pre[:, :], ACT.Abs).then_inc(soft_steps, 1)
                body(RANKED + 1, False)
                act.wait_ge(soft_steps, 1)
                act.activation(mag[:, :], mag[:, :], ACT.Exp, scale=-1.0).then_inc(soft_steps, 1)
                act.wait_ge(soft_steps, 2)
                act.activation(mag[:, :], mag[:, :], ACT.Ln, bias=half[:, 0:1], scale=0.5).then_inc(soft_steps, 1)
                with act.Fori(RANKED + 2, PASSES) as i:
                    body(i, False)

            @block.vector
            def _(dve):
                steps = 0

                def step(ins):
                    nonlocal steps
                    ins.then_inc(v, 1)
                    steps += 1

                def settle():
                    dve.wait_ge(v, steps)

                def split_w(k):
                    dve.wait_ge(w_in[k % 2], 16 * (k // 2 + 1))
                    dve.tensor_copy(w_hi[:, k, :], w_raw[:, k % 2, :]).then_inc(w_hi_done, 1)
                    dve.wait_ge(w_hi_done, k + 1)
                    dve.tensor_tensor(w_lo[:, k, :], w_raw[:, k % 2, :], w_hi[:, k, :].bitcast(F32),
                                      ALU.subtract).then_inc(w_lo_done, 1)

                def splits(m, i, s):
                    dve.wait_ge(tile_done, 2 * m + 2)
                    dve.wait_ge(x_loaded[s], 16 * (i + 1))
                    dve.tensor_copy(x_hi[s][:, :, :], x_in[s][:, :, :]).then_inc(hi_done, 1)
                    dve.wait_ge(hi_done, m + 1)
                    dve.tensor_tensor(x_lo[s][:, :, :], x_in[s][:, :, :], x_hi[s][:, :, :].bitcast(F32),
                                      ALU.subtract).then_inc(lo_done, 1)

                def attention(m, i, s):
                    if not first(i):
                        dve.wait_ge(al_stored[s], 16 * i)
                    for j in range(2):
                        dve.wait_ge(evac_done, 2 + 2 * m + j + 1)
                        for a in range(2):
                            for hd in range(H):
                                cols = slice(hd * C, (hd + 1) * C)
                                dve.wait_ge(al_done, 32 + 16 * m + 8 * j + 4 * a + hd - 1)
                                dve.tensor_tensor_reduce(
                                    prod[hd % 2][:, :], h_sb[2 * s + j][:, cols], a_rows[:, a, cols], 1.0, 0.0,
                                    ALU.mult, ALU.add, al_sb[s][:, j, a * H + hd:a * H + hd + 1]).then_inc(al_done, 1)

                def tie(i):
                    if not first(i):
                        dve.wait_ge(tied_done, 2 * PER * i)
                    for n in range(2 * PER):
                        o, t = n % 2, PER * i + n // 2
                        dve.scalar_tensor_tensor(ties[:, n, :], row[o][:, bass.ds(t * P, P)], col[:, o, bass.ds(t, 1)],
                                                 lower[:, :], ALU.is_equal, ALU.mult,
                                                 accum_out=tied[:, o, bass.ds(t, 1)]).then_inc(tied_done, 1)

                def body(i, ranking=False, last=False):
                    if ranking:
                        tie(i)
                    splits(2 * i + 1, i, 1)
                    attention(2 * i, i, 0)
                    if not last:
                        splits(2 * i + 2, i + 1, 0)
                    attention(2 * i + 1, i, 1)

                def loop(start, stop, ranking=False):
                    with dve.Fori(start, stop) as i:
                        body(i, ranking)

                dve.sem_inc(al_done, 32)
                dve.memset(ends[:, 0, :], -1.0)
                dve.memset(half[:, :], 0.5)
                dve.memset(hid[F:F + 1, :], 1.0)
                step(dve.memset(ends[:, 1, :], -2.0))
                splits(0, 0, 0)
                for k in range(2):
                    split_w(k)
                dve.wait_ge(const_done, CONST)
                dve.wait_ge(cols_in, 32)
                for o in range(2):
                    step(dve.scalar_tensor_tensor(col[:, o, :], int_col[:, o, :], float(ET), tile_col[:, :],
                                                  ALU.mult, ALU.add))
                settle()
                step(dve.tensor_scalar(neg[:, :, :], col[:, :, :], -1.0, 0.5, ALU.mult, ALU.add))
                for k in range(2, KC):
                    split_w(k)
                settle()
                for o in range(2):
                    dve.wait_ge(rows_in[o], 16)
                    dve.scalar_tensor_tensor(row[o][:, :], int_row, float(ET), tile_row,
                                             ALU.mult, ALU.add).then_inc(row_done[o], 1)
                step(dve.tensor_copy(node[:, :, :], int_col[:, :, :]))
                for o in range(2):
                    step(dve.memset(rec[o][:, :, :], 0.0))
                step(dve.tensor_copy(r_f[:, :], r_i[:, :]))
                step(dve.tensor_copy(dump[:, :], r_next[:, :]))
                dve.wait_ge(a_in, 16)
                dve.wait_ge(row_done[0], 1)
                dve.wait_ge(row_done[1], 1)
                body(0, True)
                loop(1, RANKED, True)

                dve.wait_ge(signed, 2 * ET)
                dve.wait_ge(tied_done, 2 * ET)
                settle()
                step(dve.tensor_scalar(before[:, :, :], later[:, :, :], -0.5, EP / 2, ALU.mult, ALU.add))
                step(dve.tensor_scalar(r1[:, :], r_f[:, :], 1.0, None, ALU.add))
                settle()
                step(dve.tensor_tensor(rank[:, :, :], before[:, :, :], tied[:, :, :], ALU.add))
                settle()
                for o in range(2):
                    dve.tensor_copy(rec[o][:, :, 0], node[:, o, :])
                    dve.tensor_copy(rec[o][:, :, 1], node[:, 1 - o, :])
                    dve.tensor_copy(rec[o][:, :, 2], rank[:, 0, :])
                    dve.tensor_copy(rec[o][:, :, 3], r_f[:, :])
                    dve.tensor_copy(rec[o][:, :, 4], weight[:, :])
                dve.tensor_copy(rank_i[:, :, :], rank[:, :, :]).then_inc(ranked, 2)
                loop(RANKED, RANKED + 2)

                dve.wait_ge(f_loaded, 80)
                for c in range(4):
                    step(dve.tensor_tensor(yr[:, c, :], y[:, :, c], weight[:, :], ALU.mult))
                settle()
                step(dve.tensor_scalar(yr[:, 4:7, :], yr[:, 1:4, :], 3 ** -0.5, None, ALU.mult))
                dve.wait_ge(soft_steps, 3)
                dve.scalar_tensor_tensor(hid[0:F, :], pre[:, :], 0.0, mag[:, :], ALU.max, ALU.add).then_inc(hid_done, 2)
                loop(RANKED + 2, RANKED + 5)

                def use_factors(g):
                    dve.wait_ge(f_done, g + 1)
                    if g >= 2:
                        dve.wait_ge(u_stored[g % 2], 16 * (g // 2))
                    for n, (k, c) in enumerate(((0, 0), (1, 4), (1, 5), (1, 6), (2, 1), (2, 2), (2, 3), (3, 0))):
                        scale = yr[:, c, g * PER:(g + 1) * PER].rearrange("p (t a) -> p t a", a=1)
                        last = dve.tensor_tensor(u[g % 2][:, :, n * F:(n + 1) * F], f_ps[g % 4][:, :, k * F:(k + 1) * F],
                                                 scale.to_broadcast([P, PER, F]), ALU.mult)
                    last.then_inc(u_done, 1)

                dve.wait_ge(sorted_in, 64)
                settle()
                for o in range(2):
                    key = srt[o][:, :, 0]
                    step(dve.tensor_tensor(is_last[:, o, :], key, nxt[o][:, :, 0], ALU.not_equal))
                    step(dve.tensor_tensor(off[:, o, :], key, dump[:, :], ALU.subtract))
                settle()
                step(dve.tensor_tensor(cut[:, :, :], off[:, :, :], is_last[:, :, :], ALU.mult))
                settle()
                for o in range(2):
                    step(dve.tensor_tensor(where[:, o, :], cut[:, o, :], dump[:, :], ALU.add))
                settle()
                for o in range(2):
                    for end in range(2):
                        step(dve.tensor_copy(node_i[:, o, end, :], srt[o][:, :, end]))
                step(dve.tensor_copy(scat_i[:, :, :], where[:, :, :]))
                settle()
                dve.memset(out_d[:, :, :], 0.0)
                step(dve.memset(out_s[:, :, :], 0.0))
                settle()
                dve.sem_inc(scat_done, 1)
                for g in range(2):
                    use_factors(g)
                loop(RANKED + 5, PASSES - 3)
                for n, g in enumerate(range(2, GROUPS)):
                    use_factors(g)
                    body(PASSES - 3 + n, last=(n == 2))

                dve.wait_ge(looked, 16 * 4 * ET)
                f = [found[:, :, n] for n in range(4)]
                for n, (m, own) in enumerate(((f[1], srt[1][:, :, 2]), (f[3], r_f[:, :]))):
                    step(dve.tensor_scalar(has[:, n, :], m, 0.5, None, ALU.is_ge))
                    step(dve.tensor_scalar(alt[:, n, :], own, float(EP), None, ALU.add))
                settle()
                for n, m in enumerate((f[1], f[3])):
                    step(dve.scalar_tensor_tensor(diff[:, n, :], m, -1.0, alt[:, n, :], ALU.add, ALU.subtract))
                settle()
                step(dve.tensor_tensor(gap[:, :, :], diff[:, :, :], has[:, :, :], ALU.mult))
                settle()
                step(dve.tensor_tensor(pick[:, :, :], gap[:, :, :], alt[:, :, :], ALU.add))
                settle()
                di, si = out_d[:, :, :].bitcast(I32), out_s[:, :, :].bitcast(I32)
                dve.tensor_copy(di[:, :, D_SRC], node_i[:, 0, 1, :])
                dve.tensor_copy(di[:, :, D_DST], node_i[:, 0, 0, :])
                dve.tensor_copy(di[:, :, D_OUT], scat_i[:, 0, :])
                dve.tensor_copy(out_d[:, :, KEY], srt[0][:, :, 0])
                dve.tensor_copy(out_d[:, :, D_EW], srt[0][:, :, 4])
                dve.tensor_scalar(si[:, :, S_X2DST], f[0], -1.0, None, ALU.add)
                dve.tensor_copy(si[:, :, S_X2SRC], pick[:, 0, :])
                dve.tensor_scalar(si[:, :, S_X3SRC], f[2], -1.0, None, ALU.add)
                dve.tensor_copy(out_s[:, :, KEY], srt[1][:, :, 0])
                dve.tensor_copy(si[:, :, S_X3DST], pick[:, 1, :])
                dve.tensor_copy(si[:, :, S_OUT], scat_i[:, 1, :])
                dve.tensor_copy(si[:, :, S_EDGE], srt[1][:, :, 3]).then_inc(tabs_done, 1)


def gat_dense(nc, sem, src, w, bias, avec, h_out, al_out):
    K = w.shape[0]
    KC = K // P
    G = 2 * P
    MACROS = NP // G
    FILLS = KC // 2
    with ExitStack() as ctx:
        sb = lambda n, s, d=F32: ctx.enter_context(nc.sbuf_tensor(f"g2_{n}", s, d))
        ps = lambda n, s: ctx.enter_context(nc.psum_tensor(f"g2_{n}", s, F32))
        w_raw = sb("w_raw", [P, 2, HC])
        w_hi = sb("w_hi", [P, KC, HC], F32R)
        w_lo = sb("w_lo", [P, KC, HC], F32R)
        a_rows = sb("a_rows", [P, 2, HC])
        x_in = [sb(f"x_in{s}", [P, 2, K]) for s in range(2)]
        act_t = [sb(f"act_t{s}", [P, KC, G]) for s in range(2)]
        x_hi = [sb(f"x_hi{s}", [P, KC, G], F32R) for s in range(2)]
        x_lo = [sb(f"x_lo{s}", [P, KC, G], F32R) for s in range(2)]
        h_sb = [sb(f"h_sb{s}", [P, HC]) for s in range(4)]
        al_sb = [sb(f"al_sb{s}", [P, 2, 2 * H]) for s in range(2)]
        prod = [sb(f"prod{s}", [P, C]) for s in range(2)]
        h_ps = [ps(f"h_ps{s}", [P, HC]) for s in range(2)]
        ident = sb("ident", [P, P])
        b_col = sb("b_col", [P, KC])
        t_ps = [ps(f"t_ps{s}", [P, 2, G]) for s in range(2)]

        w_in = [sem(f"g2_w_in{s}") for s in range(2)]
        a_in = sem(f"g2_a_in")
        x_loaded = [sem(f"g2_x_loaded{s}") for s in range(2)]
        h_stored = [sem(f"g2_h_stored{s}") for s in range(4)]
        al_stored = [sem(f"g2_al_stored{s}") for s in range(2)]
        w_hi_done = sem(f"g2_w_hi_done")
        w_lo_done = sem(f"g2_w_lo_done")
        hi_done = sem(f"g2_hi_done")
        lo_done = sem(f"g2_lo_done")
        filled = sem(f"g2_filled")
        relu_done = sem(f"g2_relu_done")
        tile_done = sem(f"g2_tile_done")
        evac_done = sem(f"g2_evac_done")
        al_done = sem(f"g2_al_done")
        ident_done = sem(f"g2_ident_done")

        def rows(ap, m):
            return ap[bass.ds(m * G, G), :].rearrange("(j p) k -> p j k", p=P)

        def first(i):
            return isinstance(i, int) and i == 0

        with nc.Block() as block:

            @block.sync
            def _(sp):
                for s in range(2):
                    sp.dma_start(x_in[s][:, :, :], rows(src, s)).then_inc(x_loaded[s], 16)
                sp.dma_start(a_rows[:, :, :], avec.partition_broadcast(P)).then_inc(a_in, 16)
                sp.dma_start(b_col[:, :], bias).then_inc(a_in, 16)
                for k in range(KC):
                    if k >= 2:
                        sp.wait_ge(w_lo_done, k - 1)
                    sp.dma_start(w_raw[:, k % 2, :], w[k * P:(k + 1) * P, :]).then_inc(w_in[k % 2], 16)

                with sp.Fori(0, MACROS // 2 - 1) as i:
                    for s in range(2):
                        m = 2 * i + s
                        sp.wait_ge(filled, FILLS * (m + 1))
                        sp.dma_start(x_in[s][:, :, :], rows(src, m + 2)).then_inc(x_loaded[s], 16)

            @block.gpsimd
            def _(pool):
                pool.memset(ident[:, :], 0.0).then_inc(ident_done, 1)
                pool.wait_ge(ident_done, 1)
                pool.affine_select(out=ident[:, :], in_=ident[:, :], compare_op=ALU.not_equal, fill=1.0,
                                   base=0, pattern=[[-1, P]], channel_multiplier=1).then_inc(ident_done, 1)
                with pool.Fori(0, MACROS // 2) as i:
                    for s in range(2):
                        m = 2 * i + s
                        for j in range(2):
                            pool.wait_ge(evac_done, 2 + 2 * m + j + 1)
                            pool.dma_start(h_out[bass.ds(m * G + j * P, P), :],
                                           h_sb[2 * s + j][:, :]).then_inc(h_stored[2 * s + j], 16)
                        pool.wait_ge(al_done, 32 + 16 * (m + 1))
                        pool.dma_start(rows(al_out, m), al_sb[s][:, :, :]).then_inc(al_stored[s], 16)
                for s in range(4):
                    pool.wait_ge(h_stored[s], 16 * (MACROS // 2))
                for s in range(2):
                    pool.wait_ge(al_stored[s], 16 * (MACROS // 2))

            @block.tensor
            def _(pe):
                pe.sem_inc(tile_done, 4)
                pe.wait_ge(ident_done, 2)

                def transposes(m, i, s):
                    pe.wait_ge(x_loaded[s], 16 * (i + 1))
                    for f in range(FILLS):
                        pe.wait_ge(relu_done, FILLS * m + f + 1)
                        for c in range(2):
                            for j in range(2):
                                k = 2 * f + c
                                last = pe.transpose(t_ps[f % 2][:, c, j * P:(j + 1) * P],
                                                    x_in[s][:, j, k * P:(k + 1) * P], ident[:, :])
                        last.then_inc(filled, 1)

                def products(m, i, s):
                    pe.wait_ge(lo_done, FILLS * (m + 1))
                    for j in range(2):
                        pe.wait_ge(evac_done, 2 * m + j + 1)
                        for n in range(2):
                            out = h_ps[j][:, n * 512:(n + 1) * 512]
                            for k in range(KC):
                                xh = x_hi[s][:, k, j * P:(j + 1) * P]
                                xl = x_lo[s][:, k, j * P:(j + 1) * P]
                                wh = w_hi[:, k, n * 512:(n + 1) * 512]
                                wl = w_lo[:, k, n * 512:(n + 1) * 512]
                                pe.matmul(out, xh, wh, start=(k == 0), stop=False)
                                pe.matmul(out, xh, wl, start=False, stop=False)
                                last = pe.matmul(out, xl, wh, start=False, stop=(k == KC - 1))
                        last.then_inc(tile_done, 1)

                transposes(0, 0, 0)
                pe.wait_ge(w_lo_done, KC)

                def body(i, last):
                    transposes(2 * i + 1, i, 1)
                    products(2 * i, i, 0)
                    if not last:
                        transposes(2 * i + 2, i + 1, 0)
                    products(2 * i + 1, i, 1)

                with pe.Fori(0, MACROS // 2 - 1) as i:
                    body(i, False)
                body(MACROS // 2 - 1, True)

            @block.scalar
            def _(act):
                act.sem_inc(evac_done, 2)
                act.sem_inc(relu_done, 2)
                act.wait_ge(a_in, 32)

                def relus(m, i, s):
                    for f in range(FILLS):
                        act.wait_ge(filled, FILLS * m + f + 1)
                        for c in range(2):
                            k = 2 * f + c
                            last = act.activation(act_t[s][:, k, :], t_ps[f % 2][:, c, :], ACT.Relu,
                                                  bias=b_col[:, k:k + 1])
                        last.then_inc(relu_done, 1)

                def evacs(m, i, s):
                    for j in range(2):
                        act.wait_ge(tile_done, 4 + 2 * m + j + 1)
                        if not first(i):
                            act.wait_ge(h_stored[2 * s + j], 16 * i)
                        act.wait_ge(al_done, 8 * (2 * m + j + 1))
                        act.activation(h_sb[2 * s + j][:, :], h_ps[j][:, :], ACT.Copy).then_inc(evac_done, 1)

                relus(0, 0, 0)

                def body(i, last):
                    relus(2 * i + 1, i, 1)
                    evacs(2 * i, i, 0)
                    if not last:
                        relus(2 * i + 2, i + 1, 0)
                    evacs(2 * i + 1, i, 1)

                body(0, False)
                with act.Fori(1, MACROS // 2 - 1) as i:
                    body(i, False)
                body(MACROS // 2 - 1, True)

            @block.vector
            def _(dve):
                dve.sem_inc(al_done, 32)
                def split_w(k):
                    dve.wait_ge(w_in[k % 2], 16 * (k // 2 + 1))
                    dve.tensor_copy(w_hi[:, k, :], w_raw[:, k % 2, :]).then_inc(w_hi_done, 1)
                    dve.wait_ge(w_hi_done, k + 1)
                    dve.tensor_tensor(w_lo[:, k, :], w_raw[:, k % 2, :], w_hi[:, k, :].bitcast(F32),
                                      ALU.subtract).then_inc(w_lo_done, 1)

                def splits(m, i, s):
                    dve.wait_ge(tile_done, 2 * m + 2)
                    for f in range(FILLS):
                        ks = slice(2 * f, 2 * f + 2)
                        dve.wait_ge(relu_done, 2 + FILLS * m + f + 1)
                        dve.tensor_copy(x_hi[s][:, ks, :], act_t[s][:, ks, :]).then_inc(hi_done, 1)
                        dve.wait_ge(hi_done, FILLS * m + f + 1)
                        dve.tensor_tensor(x_lo[s][:, ks, :], act_t[s][:, ks, :], x_hi[s][:, ks, :].bitcast(F32),
                                          ALU.subtract).then_inc(lo_done, 1)

                def attention(m, i, s):
                    if not first(i):
                        dve.wait_ge(al_stored[s], 16 * i)
                    for j in range(2):
                        dve.wait_ge(evac_done, 2 + 2 * m + j + 1)
                        for a in range(2):
                            for hd in range(H):
                                cols = slice(hd * C, (hd + 1) * C)
                                dve.wait_ge(al_done, 32 + 16 * m + 8 * j + 4 * a + hd - 1)
                                dve.tensor_tensor_reduce(
                                    prod[hd % 2][:, :], h_sb[2 * s + j][:, cols], a_rows[:, a, cols], 1.0, 0.0,
                                    ALU.mult, ALU.add, al_sb[s][:, j, a * H + hd:a * H + hd + 1]).then_inc(al_done, 1)

                for k in range(KC):
                    split_w(k)
                splits(0, 0, 0)
                dve.wait_ge(a_in, 32)

                def body(i, last):
                    splits(2 * i + 1, i, 1)
                    attention(2 * i, i, 0)
                    if not last:
                        splits(2 * i + 2, i + 1, 0)
                    attention(2 * i + 1, i, 1)

                body(0, False)
                with dve.Fori(1, MACROS // 2 - 1) as i:
                    body(i, False)
                body(MACROS // 2 - 1, True)


def gat_edges(nc, sem, name, h_rows, al_rows, row_d, tab_d, bounce, w_tab):
    RING = 4
    with ExitStack() as ctx:
        sb = lambda n, s, d=F32: ctx.enter_context(nc.sbuf_tensor(f"{name}_{n}", s, d))
        ps = lambda n, s: ctx.enter_context(nc.psum_tensor(f"{name}_{n}", s, F32))
        tabs = sb("tabs", [P, ET, TAB])
        al_src = sb("al_src", [P, ET, 2 * H])
        al_dst = sb("al_dst", [P, ET, 2 * H])
        keys = sb("keys", [H, EP + 2])
        same = sb("same", [H, EP + 1])
        cut = sb("cut", [H, EP + 1])
        ident = sb("ident", [P, P])
        score = sb("score", [P, 2, H, ET])
        raised = sb("raised", [P, 2, H, ET])
        top_pair = sb("top_pair", [P, H, ET])
        top_t = sb("top_t", [H * ET, P])
        top_row = sb("top_row", [H, EP])
        fwd = sb("fwd", [H, EP])
        bwd = sb("bwd", [H, EP])
        max_t = sb("max_t", [H * ET, P])
        below = sb("below", [P, 2, H, ET])
        w_all = sb("w_all", [P, ET, 2, H])
        last_row = sb("last_row", [P, 1])
        tab = [sb(f"tab{s}", [P, TAB]) for s in range(RING)]
        w = [sb(f"w{s}", [P, 2, H]) for s in range(RING)]
        key_row = [sb(f"key_row{s}", [P, P]) for s in range(RING)]
        h_src = [sb(f"h_src{s}", [P, HC]) for s in range(RING)]
        h_dst = [sb(f"h_dst{s}", [P, HC]) for s in range(RING)]
        mask = [sb(f"mask{s}", [P, H + 2, P]) for s in range(2)]
        sums = [sb(f"sums{s}", [P, HC + H]) for s in range(2)]
        own = [sb(f"own{s}", [P, HC]) for s in range(2)]
        den = sb("den", [P, 2, H])
        rden = sb("rden", [P, 2, H])
        w_own = sb("w_own", [P, 2, H])
        out = sb("out", [P, ET * HC])
        sum_ps = [ps(f"sum_ps{s}", [P, HC]) for s in range(2)]
        den_ps = [ps(f"den_ps{s}", [P, 512]) for s in range(2)]
        t_ps = ps("t_ps", [P, 512])

        small_in = sem(f"{name}_small_in")
        al_in = sem(f"{name}_al_in")
        const_done = sem(f"{name}_const_done")
        v = sem(f"{name}_v")
        top_turned = sem(f"{name}_top_turned")
        top_copied = sem(f"{name}_top_copied")
        bounced = sem(f"{name}_bounced")
        scanned = sem(f"{name}_scanned")
        max_turned = sem(f"{name}_max_turned")
        below_done = sem(f"{name}_below_done")
        w_done = sem(f"{name}_w_done")
        w_stored = sem(f"{name}_w_stored")
        tab_in = [sem(f"{name}_tab_in{s}") for s in range(RING)]
        h_in = [sem(f"{name}_h_in{s}") for s in range(RING)]
        masks_done = sem(f"{name}_masks_done")
        den_done = sem(f"{name}_den_done")
        own_scaled = sem(f"{name}_own_scaled")
        summed = sem(f"{name}_summed")
        sums_out = sem(f"{name}_sums_out")
        finished = sem(f"{name}_finished")
        scattered = sem(f"{name}_scattered")
        zeroed = sem(f"{name}_zeroed")

        with nc.Block() as block:

            @block.sync
            def _(sp):
                sp.dma_start(tabs[:, :, :], tab_d.rearrange("(t p) k -> p t k", p=P)).then_inc(small_in, 16)
                sp.dma_start(keys[:, :], row_d.partition_broadcast(H)).then_inc(small_in, 16)
                sp.wait_ge(top_copied, 1)
                sp.dma_start(bounce[0], top_t[:, :]).then_inc(bounced, 16)
                sp.wait_ge(bounced, 16)
                sp.dma_start(top_row[:, :], bounce[0].rearrange("(h t) p -> h (t p)", h=H)).then_inc(bounced, 16)
                sp.wait_ge(scanned, 3)
                sp.dma_start(bounce[1].rearrange("(h t) p -> h (t p)", h=H), bwd[:, :]).then_inc(bounced, 16)
                sp.wait_ge(bounced, 48)
                sp.dma_start(max_t[:, :], bounce[1]).then_inc(bounced, 16)
                sp.wait_ge(w_done, 1)
                sp.dma_start(w_tab.rearrange("(t p) k -> p t k", p=P),
                             w_all[:, :, :, :].rearrange("p t a h -> p t (a h)")).then_inc(w_stored, 16)
                sp.wait_ge(w_stored, 16)
                sp.wait_ge(zeroed, 3)
                with sp.Fori(0, ET // RING) as i:
                    for s in range(RING):
                        t = RING * i + s
                        sp.wait_ge(finished, t + 1)
                        if s == RING - 1:
                            sp.wait_ge(masks_done, t - 2)
                        sp.dma_start(tab[s][:, :], tab_d[bass.ds(t * P, P), :]).then_inc(tab_in[s], 16)
                        sp.dma_start(w[s][:, :, :].rearrange("p a h -> p (a h)"),
                                     w_tab[bass.ds(t * P, P), :]).then_inc(tab_in[s], 16)
                        sp.dma_start(key_row[s][:, :],
                                     row_d[bass.ds(t * P + 1, P)].partition_broadcast(P)).then_inc(tab_in[s], 16)

            @block.gpsimd
            def _(pool):
                pool.memset(ident[:, :], 0.0).then_inc(const_done, 1)
                pool.memset(last_row[:, :], 0.0).then_inc(const_done, 1)
                pool.wait_ge(const_done, 2)
                pool.affine_select(out=ident[:, :], in_=ident[:, :], compare_op=ALU.not_equal, fill=1.0,
                                   base=0, pattern=[[-1, P]], channel_multiplier=1).then_inc(const_done, 1)
                pool.affine_select(out=last_row[:, :], in_=last_row[:, :], compare_op=ALU.not_equal, fill=1.0,
                                   base=1 - P, pattern=[[0, 1]], channel_multiplier=1).then_inc(const_done, 1)
                pool.wait_ge(small_in, 32)
                index = lambda t, k: bass.IndirectOffsetOnAxis(tabs[:, t, k:k + 1].bitcast(I32), 0)
                for t in range(ET):
                    pool.indirect_dma_start(al_src[:, t, :], None, al_rows, index(t, D_SRC)).then_inc(al_in, 16)
                    pool.indirect_dma_start(al_dst[:, t, :], None, al_rows, index(t, D_DST)).then_inc(al_in, 16)
                for t in range(ET):
                    s = t % RING
                    if t >= RING:
                        pool.wait_ge(finished, t + 1)
                    pool.indirect_dma_start(h_src[s][:, :], None, h_rows[0:NP], index(t, D_SRC)).then_inc(h_in[s], 16)
                    pool.indirect_dma_start(h_dst[s][:, :], None, h_rows[0:NP], index(t, D_DST)).then_inc(h_in[s], 16)
                pool.wait_ge(finished, RING + ET)
                for t in range(ET):
                    pool.indirect_dma_start(h_rows, index(t, D_OUT), out[:, t * HC:(t + 1) * HC],
                                            None).then_inc(scattered, 16)
                pool.wait_ge(scattered, 16 * ET)

            @block.tensor
            def _(pe):
                pe.sem_inc(summed, 2)
                pe.wait_ge(const_done, 4)
                pe.wait_ge(v, 3)
                pe.transpose(t_ps[0:H * ET, 0:P], top_pair[:, :, :].rearrange("p h t -> p (h t)"),
                             ident[:, :]).then_inc(top_turned, 1)
                pe.wait_ge(bounced, 64)
                pe.wait_ge(top_copied, 1)
                pe.transpose(t_ps[:, 128:128 + H * ET], max_t[:, :], ident[0:H * ET, 0:H * ET]).then_inc(max_turned, 1)
                pe.wait_ge(zeroed, 3)
                with pe.Fori(0, ET // RING) as i:
                    for s in range(RING):
                        t = RING * i + s
                        m = mask[s % 2]
                        pe.wait_ge(masks_done, t + 1)
                        pe.wait_ge(h_in[s], 32 * (i + 1))
                        pe.wait_ge(sums_out, t + 1)
                        for hd in range(H):
                            cols = slice(hd * C, (hd + 1) * C)
                            pe.matmul(sum_ps[s % 2][:, cols], m[:, hd, :], h_src[s][:, cols],
                                      start=(hd % 2 == 0), stop=False, skip_group_check=True)
                        pe.matmul(den_ps[s % 2][:, 0:H], m[:, H, :], w[s][:, 0, :], start=True, stop=False)
                        prev = sums[(s + 1) % 2]
                        pe.wait_ge(sums_out, t + 2)
                        pe.matmul(den_ps[s % 2][:, 0:H], m[:, H + 1, :], prev[:, HC:HC + H], start=False, stop=True)
                        for n in range(2):
                            last = pe.matmul(sum_ps[s % 2][:, n * 512:(n + 1) * 512], m[:, H + 1, :],
                                             prev[:, n * 512:(n + 1) * 512], start=False, stop=True,
                                             skip_group_check=True)
                        last.then_inc(summed, 1)

            @block.scalar
            def _(act):
                act.sem_inc(sums_out, 2)
                act.wait_ge(top_turned, 1)
                act.activation(top_t[:, :], t_ps[0:H * ET, 0:P], ACT.Copy).then_inc(top_copied, 1)
                act.wait_ge(below_done, 2)
                act.activation(w_all[:, :, :, :].rearrange("p t a h -> p a h t"), below[:, :, :, :],
                               ACT.Exp).then_inc(w_done, 1)
                with act.Fori(0, ET // RING) as i:
                    for s in range(RING):
                        t = RING * i + s
                        act.wait_ge(summed, t + 3)
                        act.wait_ge(finished, t + 3)
                        act.activation(sums[s % 2][:, 0:HC], sum_ps[s % 2][:, :], ACT.Copy)
                        act.activation(sums[s % 2][:, HC:HC + H], den_ps[s % 2][:, 0:H], ACT.Copy).then_inc(sums_out, 1)

            @block.vector
            def _(dve):
                dve.sem_inc(finished, 4)
                dve.memset(tab[RING - 1][:, :], -5.0).then_inc(zeroed, 1)
                for s in range(2):
                    dve.memset(sums[s][:, :], 0.0).then_inc(zeroed, 1)
                dve.wait_ge(small_in, 32)
                dve.tensor_tensor(same[:, :], keys[:, 0:EP + 1], keys[:, 1:EP + 2], ALU.is_equal).then_inc(v, 1)
                dve.wait_ge(v, 1)
                dve.tensor_scalar(cut[:, :], same[:, :], -1.0, 1e30, ALU.add, ALU.mult)
                dve.wait_ge(al_in, 16 * 2 * ET)
                hv = lambda ap, k: ap[:, :, k * H:(k + 1) * H].rearrange("p t h -> p h t")
                dve.tensor_tensor(score[:, 0, :, :], hv(al_src, 0), hv(al_dst, 1), ALU.add)
                dve.tensor_tensor(score[:, 1, :, :], hv(al_dst, 0), hv(al_dst, 1), ALU.add).then_inc(v, 1)
                dve.wait_ge(v, 2)
                flat = lambda ap: ap[:, :, :, :].rearrange("p a h t -> p (a h t)")
                dve.scalar_tensor_tensor(flat(raised), flat(score), 0.2, flat(score), ALU.mult, ALU.max).then_inc(below_done, 1)
                dve.wait_ge(below_done, 1)
                dve.tensor_tensor(top_pair[:, :, :], raised[:, 0, :, :], raised[:, 1, :, :], ALU.max).then_inc(v, 1)
                dve.wait_ge(bounced, 32)
                dve.tensor_tensor_scan(fwd[:, :], cut[:, 0:EP], top_row[:, :], 0.0, ALU.add, ALU.max).then_inc(scanned, 1)
                dve.wait_ge(scanned, 1)
                dve.tensor_tensor_scan(bwd[:, ::-1], cut[:, EP:0:-1], fwd[:, ::-1], 0.0, ALU.add, ALU.max).then_inc(scanned, 2)
                dve.wait_ge(max_turned, 1)
                mx = t_ps[:, 128:128 + H * ET].rearrange("p (h t) -> p h t", h=H)
                dve.tensor_tensor(below[:, 0, :, :], raised[:, 0, :, :], mx, ALU.subtract)
                dve.tensor_tensor(below[:, 1, :, :], raised[:, 1, :, :], mx, ALU.subtract).then_inc(below_done, 1)

                def masks(i, s, first):
                    dve.wait_ge(tab_in[s], 48 * (i + 1))
                    t = RING * i + s
                    dve.wait_ge(summed, t + 1)
                    key = tab[s][:, KEY:KEY + 1]
                    m = mask[s % 2]
                    for hd in range(H):
                        dve.tensor_scalar(m[:, hd, :], key_row[s][:, :], key, w[s][:, 0, hd:hd + 1],
                                          ALU.is_equal, ALU.mult)
                    dve.tensor_scalar(m[:, H, :], key_row[s][:, :], key, None, ALU.is_equal)
                    dve.tensor_scalar(m[:, H + 1, :], key_row[s][:, :], tab[(s - 1) % RING][:, KEY:KEY + 1],
                                      last_row[:, 0:1], ALU.is_equal, ALU.mult).then_inc(masks_done, 1)

                def finish(i, s):
                    t = RING * i + s
                    q = s % 2
                    dve.wait_ge(sums_out, t + 3)
                    dve.tensor_tensor(den[:, q, :], sums[q][:, HC:HC + H], w[s][:, 1, :], ALU.add).then_inc(den_done, 1)
                    dve.wait_ge(den_done, 3 * t + 1)
                    dve.reciprocal(rden[:, q, :], den[:, q, :]).then_inc(den_done, 1)
                    dve.wait_ge(den_done, 3 * t + 2)
                    dve.tensor_tensor(w_own[:, q, :], rden[:, q, :], w[s][:, 1, :], ALU.mult).then_inc(den_done, 1)
                    dve.wait_ge(den_done, 3 * t + 3)
                    for hd in range(H):
                        cols = slice(hd * C, (hd + 1) * C)
                        last = dve.tensor_scalar(own[q][:, cols], h_dst[s][:, cols], w_own[:, q, hd:hd + 1], None,
                                                 ALU.mult)
                    last.then_inc(own_scaled, 1)
                    dve.wait_ge(own_scaled, t + 1)
                    for hd in range(H):
                        cols = slice(hd * C, (hd + 1) * C)
                        last = dve.scalar_tensor_tensor(out[:, bass.ds(t * HC + hd * C, C)], sums[q][:, cols],
                                                        rden[:, q, hd:hd + 1], own[q][:, cols], ALU.mult, ALU.add)
                    last.then_inc(finished, 1)

                dve.wait_ge(const_done, 4)
                dve.wait_ge(zeroed, 3)
                masks(0, 0, True)

                def body(i, last):
                    for s in range(RING):
                        if s < RING - 1:
                            masks(i, s + 1, False)
                        elif not last:
                            masks(i + 1, 0, False)
                        finish(i, s)

                with dve.Fori(0, ET // RING - 1) as i:
                    body(i, False)
                body(ET // RING - 1, True)


def fc_dense(nc, sem, src, w, bias, x_rows, b_out, x1_out, y_out):
    KC = HC // P
    G = 2 * P
    MACROS = NP // G
    FILLS = KC // 2
    with ExitStack() as ctx:
        sb = lambda n, s, d=F32: ctx.enter_context(nc.sbuf_tensor(f"fc_{n}", s, d))
        ps = lambda n, s: ctx.enter_context(nc.psum_tensor(f"fc_{n}", s, F32))
        w_raw = sb("w_raw", [P, 2, D])
        w_hi = sb("w_hi", [P, KC, D], F32R)
        w_lo = sb("w_lo", [P, KC, D], F32R)
        b_rows = sb("b_rows", [P, 2, D])
        h_in = [sb(f"h_in{s}", [P, 2, HC]) for s in range(2)]
        x_in = [sb(f"x_in{s}", [P, 2, D]) for s in range(2)]
        x_b = [sb(f"x_b{s}", [P, 2, D]) for s in range(2)]
        act_t = [sb(f"act_t{s}", [P, KC, G]) for s in range(2)]
        x_hi = [sb(f"x_hi{s}", [P, KC, G], F32R) for s in range(2)]
        x_lo = [sb(f"x_lo{s}", [P, KC, G], F32R) for s in range(2)]
        ident = sb("ident", [P, P])
        b_col = sb("b_col", [P, KC])
        z = [sb(f"z{s}", [P, 2, D]) for s in range(2)]
        stats = [sb(f"stats{s}", [P, 2, 6]) for s in range(2)]
        mv = [sb(f"mv{s}", [P, 2, 2]) for s in range(2)]
        ds = [sb(f"ds{s}", [P, 4, 2]) for s in range(2)]
        inv = [sb(f"inv{s}", [P, 2, 2]) for s in range(2)]
        rstd = [sb(f"rstd{s}", [P, 2, 2]) for s in range(2)]
        shift = [sb(f"shift{s}", [P, 2, 2]) for s in range(2)]
        x1 = [sb(f"x1{s}", [P, 2, D]) for s in range(2)]
        y = [sb(f"y{s}", [P, 2, D]) for s in range(2)]
        o_ps = [ps(f"o_ps{s}", [P, D]) for s in range(4)]
        t_ps = [ps(f"t_ps{s}", [P, 2, G]) for s in range(2)]

        w_in = [sem(f"fc_w_in{s}") for s in range(2)]
        b_in = sem("fc_b_in")
        h_loaded = [sem(f"fc_h_loaded{s}") for s in range(2)]
        x_loaded = [sem(f"fc_x_loaded{s}") for s in range(2)]
        x1_stored = [sem(f"fc_x1_stored{s}") for s in range(2)]
        y_stored = [sem(f"fc_y_stored{s}") for s in range(2)]
        w_hi_done = sem("fc_w_hi_done")
        w_lo_done = sem("fc_w_lo_done")
        hi_done = sem("fc_hi_done")
        lo_done = sem("fc_lo_done")
        filled = sem("fc_filled")
        relu_done = sem("fc_relu_done")
        tile_done = sem("fc_tile_done")
        xb_done = sem("fc_xb_done")
        summed = sem("fc_summed")
        ln = sem("fc_ln")
        rooted = sem("fc_rooted")
        x1_done = sem("fc_x1_done")
        ident_done = sem("fc_ident_done")
        passed = sem("fc_passed")
        LN_STEPS = 9

        def rows(ap, m):
            return ap[bass.ds(m * G, G), :].rearrange("(j p) k -> p j k", p=P)

        def first(i):
            return isinstance(i, int) and i == 0

        with nc.Block() as block:

            @block.sync
            def _(sp):
                def load(m, s):
                    sp.dma_start(h_in[s][:, :, :], rows(src, m)).then_inc(h_loaded[s], 16)
                    sp.dma_start(x_in[s][:, :, :], rows(x_rows, m)).then_inc(x_loaded[s], 16)

                load(0, 0)
                sp.dma_start(b_col[:, :], bias).then_inc(b_in, 16)
                sp.dma_start(b_rows[:, 0, :], b_out.partition_broadcast(P)).then_inc(b_in, 16)
                sp.dma_start(b_rows[:, 1, :], b_out.partition_broadcast(P)).then_inc(b_in, 16)
                for k in range(KC):
                    if k >= 2:
                        sp.wait_ge(w_lo_done, k - 1)
                    sp.dma_start(w_raw[:, k % 2, :], w[k * P:(k + 1) * P, :]).then_inc(w_in[k % 2], 16)
                load(1, 1)

                with sp.Fori(0, MACROS // 2 - 1) as i:
                    for s in range(2):
                        m = 2 * i + s
                        sp.wait_ge(filled, FILLS * (m + 1))
                        sp.sem_inc(passed, 1)
                        sp.wait_ge(xb_done, m + 3)
                        sp.sem_inc(passed, 1)
                        load(m + 2, s)

            @block.gpsimd
            def _(pool):
                pool.sem_inc(xb_done, 2)
                pool.memset(ident[:, :], 0.0).then_inc(ident_done, 1)
                pool.wait_ge(ident_done, 1)
                pool.affine_select(out=ident[:, :], in_=ident[:, :], compare_op=ALU.not_equal, fill=1.0,
                                   base=0, pattern=[[-1, P]], channel_multiplier=1).then_inc(ident_done, 1)
                pool.wait_ge(b_in, 48)

                def add_bias(m, i, s):
                    pool.wait_ge(x_loaded[s], 16 * (i + 1))
                    pool.wait_ge(summed, 2 * m + 2)
                    pool.tensor_tensor(x_b[s][:, :, :], x_in[s][:, :, :], b_rows[:, :, :], ALU.add).then_inc(xb_done, 1)

                def store(m, i, s):
                    pool.wait_ge(x1_done, m + 3)
                    pool.sem_inc(passed, 1)
                    pool.dma_start(rows(x1_out, m), x1[s][:, :, :]).then_inc(x1_stored[s], 16)
                    pool.wait_ge(ln, LN_STEPS * (m + 1))
                    pool.sem_inc(passed, 1)
                    pool.dma_start(rows(y_out, m), y[s][:, :, :]).then_inc(y_stored[s], 16)

                add_bias(0, 0, 0)

                def body(i, last):
                    add_bias(2 * i + 1, i, 1)
                    store(2 * i, i, 0)
                    if not last:
                        add_bias(2 * i + 2, i + 1, 0)
                    store(2 * i + 1, i, 1)

                with pool.Fori(0, MACROS // 2 - 1) as i:
                    body(i, False)
                body(MACROS // 2 - 1, True)
                for s in range(2):
                    pool.wait_ge(x1_stored[s], 16 * (MACROS // 2))
                    pool.wait_ge(y_stored[s], 16 * (MACROS // 2))

            @block.tensor
            def _(pe):
                pe.sem_inc(tile_done, 4)
                pe.wait_ge(ident_done, 2)

                def transposes(m, i, s):
                    pe.wait_ge(h_loaded[s], 16 * (i + 1))
                    for f in range(FILLS):
                        pe.wait_ge(relu_done, FILLS * m + f + 1)
                        for c in range(2):
                            for j in range(2):
                                k = 2 * f + c
                                last = pe.transpose(t_ps[f % 2][:, c, j * P:(j + 1) * P],
                                                    h_in[s][:, j, k * P:(k + 1) * P], ident[:, :])
                        last.then_inc(filled, 1)

                def products(m, i, s, tiles):
                    pe.wait_ge(lo_done, FILLS * (m + 1))
                    for j in tiles:
                        pe.wait_ge(summed, 2 * m + j + 1)
                        for k in range(KC):
                            xh = x_hi[s][:, k, j * P:(j + 1) * P]
                            xl = x_lo[s][:, k, j * P:(j + 1) * P]
                            out = o_ps[2 * s + j][:, :]
                            pe.matmul(out, xh, w_hi[:, k, :], start=(k == 0), stop=False)
                            pe.matmul(out, xh, w_lo[:, k, :], start=False, stop=False)
                            last = pe.matmul(out, xl, w_hi[:, k, :], start=False, stop=(k == KC - 1))
                        last.then_inc(tile_done, 1)

                transposes(0, 0, 0)
                pe.wait_ge(w_lo_done, KC)

                def body(i, last):
                    products(2 * i, i, 0, [0])
                    transposes(2 * i + 1, i, 1)
                    products(2 * i, i, 0, [1])
                    products(2 * i + 1, i, 1, [0])
                    if not last:
                        transposes(2 * i + 2, i + 1, 0)
                    products(2 * i + 1, i, 1, [1])

                with pe.Fori(0, MACROS // 2 - 1) as i:
                    body(i, False)
                body(MACROS // 2 - 1, True)

            @block.scalar
            def _(act):
                act.sem_inc(relu_done, 2)
                act.sem_inc(x1_done, 2)
                act.wait_ge(b_in, 48)

                def relus(m, i, s):
                    for f in range(FILLS):
                        act.wait_ge(filled, FILLS * m + f + 1)
                        for c in range(2):
                            k = 2 * f + c
                            last = act.activation(act_t[s][:, k, :], t_ps[f % 2][:, c, :], ACT.Relu,
                                                  bias=b_col[:, k:k + 1])
                        last.then_inc(relu_done, 1)

                def normalize(m, i, s):
                    act.wait_ge(ln, LN_STEPS * m + 7)
                    act.activation(rstd[s][:, :, :], inv[s][:, :, :], ACT.Sqrt).then_inc(rooted, 1)
                    act.wait_ge(ln, LN_STEPS * m + 8)
                    if not first(i):
                        act.wait_ge(x1_stored[s], 16 * i)
                    for j in range(2):
                        last = act.activation(x1[s][:, j, :], z[s][:, j, :], ACT.Identity,
                                              bias=shift[s][:, 0, j:j + 1], scale=rstd[s][:, 0, j:j + 1])
                    last.then_inc(x1_done, 1)

                relus(0, 0, 0)

                def body(i, last):
                    relus(2 * i + 1, i, 1)
                    normalize(2 * i, i, 0)
                    if not last:
                        relus(2 * i + 2, i + 1, 0)
                    normalize(2 * i + 1, i, 1)

                body(0, False)
                with act.Fori(1, MACROS // 2 - 1) as i:
                    body(i, False)
                body(MACROS // 2 - 1, True)

            @block.vector
            def _(dve):
                dve.sem_inc(summed, 4)
                for k in range(KC):
                    dve.wait_ge(w_in[k % 2], 16 * (k // 2 + 1))
                    dve.tensor_copy(w_hi[:, k, :], w_raw[:, k % 2, :]).then_inc(w_hi_done, 1)
                    dve.wait_ge(w_hi_done, k + 1)
                    dve.tensor_tensor(w_lo[:, k, :], w_raw[:, k % 2, :], w_hi[:, k, :].bitcast(F32),
                                      ALU.subtract).then_inc(w_lo_done, 1)

                def splits(m, i, s):
                    dve.wait_ge(tile_done, 2 * m + 2)
                    for f in range(FILLS):
                        ks = slice(2 * f, 2 * f + 2)
                        dve.wait_ge(relu_done, 2 + FILLS * m + f + 1)
                        dve.tensor_copy(x_hi[s][:, ks, :], act_t[s][:, ks, :]).then_inc(hi_done, 1)
                        dve.wait_ge(hi_done, FILLS * m + f + 1)
                        dve.tensor_tensor(x_lo[s][:, ks, :], act_t[s][:, ks, :], x_hi[s][:, ks, :].bitcast(F32),
                                          ALU.subtract).then_inc(lo_done, 1)

                def layer_norm(m, i, s):
                    dve.wait_ge(xb_done, m + 3)
                    dve.wait_ge(x1_done, m + 1)
                    for j in range(2):
                        dve.wait_ge(tile_done, 4 + 2 * m + j + 1)
                        dve.tensor_tensor(z[s][:, j, :], o_ps[2 * s + j][:, :], x_b[s][:, j, :], ALU.add).then_inc(summed, 1)
                        dve.wait_ge(summed, 4 + 2 * m + j + 1)
                        last = dve.bn_stats(stats[s][:, j, :], z[s][:, j, :])
                    last.then_inc(ln, 1)
                    dve.wait_ge(ln, LN_STEPS * m + 1)
                    dve.sem_inc(passed, 1)
                    for j in range(2):
                        last = dve.bn_aggr(mv[s][:, j, :], stats[s][:, j, :])
                    last.then_inc(ln, 1)
                    dve.wait_ge(ln, LN_STEPS * m + 2)
                    var = mv[s][:, :, 1]
                    dve.tensor_scalar(ds[s][:, 0, :], var, EPS, None, ALU.add).then_inc(ln, 1)
                    dve.wait_ge(ln, LN_STEPS * m + 3)
                    for n, (a, b) in enumerate(((0, 2), (2, 3), (3, 1))):
                        dve.scalar_tensor_tensor(ds[s][:, b, :], ds[s][:, a, :], EPS, var,
                                                 ALU.mult, ALU.add).then_inc(ln, 1)
                        dve.wait_ge(ln, LN_STEPS * m + 4 + n)
                    dve.reciprocal(inv[s][:, :, :], ds[s][:, 0:2, :]).then_inc(ln, 1)
                    dve.wait_ge(rooted, m + 1)
                    for n in range(2):
                        last = dve.scalar_tensor_tensor(shift[s][:, n, :], mv[s][:, :, 0], -1.0, rstd[s][:, n, :],
                                                        ALU.mult, ALU.mult)
                    last.then_inc(ln, 1)
                    dve.wait_ge(ln, LN_STEPS * m + 8)
                    if not first(i):
                        dve.wait_ge(y_stored[s], 16 * i)
                    for j in range(2):
                        last = dve.tensor_scalar(y[s][:, j, :], z[s][:, j, :], rstd[s][:, 1, j:j + 1],
                                                 shift[s][:, 1, j:j + 1], ALU.mult, ALU.add)
                    last.then_inc(ln, 1)

                dve.wait_ge(b_in, 48)
                splits(0, 0, 0)

                def body(i, last):
                    splits(2 * i + 1, i, 1)
                    layer_norm(2 * i, i, 0)
                    if not last:
                        splits(2 * i + 2, i + 1, 0)
                    layer_norm(2 * i + 1, i, 1)

                body(0, False)
                with dve.Fori(1, MACROS // 2 - 1) as i:
                    body(i, False)
                body(MACROS // 2 - 1, True)


def conv_edges(nc, sem, x1_rows, row_d, tab_d, w, x2_rows, y_rows):
    RING = 4
    KC = D // P
    with ExitStack() as ctx:
        sb = lambda n, s, d=F32: ctx.enter_context(nc.sbuf_tensor(f"conv_{n}", s, d))
        ps = lambda n, s: ctx.enter_context(nc.psum_tensor(f"conv_{n}", s, F32))
        tabs = sb("tabs", [P, ET, TAB])
        w_raw = sb("w_raw", [P, KC, D])
        w_hi = sb("w_hi", [P, KC, D], F32R)
        w_lo = sb("w_lo", [P, KC, D], F32R)
        ident = sb("ident", [P, P])
        last_row = sb("last_row", [P, 1])
        tab = [sb(f"tab{s}", [P, TAB]) for s in range(RING)]
        key_row = [sb(f"key_row{s}", [P, P]) for s in range(RING)]
        x_src = sb("x_src", [P, ET * D])
        x_dst = [sb(f"x_dst{s}", [P, D]) for s in range(RING)]
        mask = [sb(f"mask{s}", [P, 2, P]) for s in range(2)]
        sums = [sb(f"sums{s}", [P, D]) for s in range(2)]
        t_hi = [sb(f"t_hi{s}", [P, KC, P], F32R) for s in range(2)]
        t_lo = [sb(f"t_lo{s}", [P, KC, P], F32R) for s in range(2)]
        z = sb("z", [P, ET * D])
        stats = sb("stats", [P, 2 * ET * 6])
        mv = sb("mv", [P, 2 * ET, 2])
        ds = sb("ds", [P, 3, 2 * ET])
        inv = sb("inv", [P, 2, 2 * ET])
        rstd = sb("rstd", [P, 2, 2 * ET])
        shift = sb("shift", [P, 2, 2 * ET])
        normed = [sb(f"normed{s}", [P, 3, D]) for s in range(3)]
        sum_ps = [ps(f"sum_ps{s}", [P, D]) for s in range(2)]
        t_ps = [ps(f"t_ps{s}", [P, KC, P]) for s in range(2)]
        y_ps = [ps(f"y_ps{s}", [P, D]) for s in range(2)]

        small_in = sem("conv_small_in")
        w_in = sem("conv_w_in")
        w_split = sem("conv_w_split")
        const_done = sem("conv_const_done")
        zeroed = sem("conv_zeroed")
        tab_in = [sem(f"conv_tab_in{s}") for s in range(RING)]
        src_in = [sem(f"conv_src_in{s}") for s in range(RING)]
        dst_in = [sem(f"conv_dst_in{s}") for s in range(RING)]
        masks_done = sem("conv_masks_done")
        summed = sem("conv_summed")
        sums_out = sem("conv_sums_out")
        turned = sem("conv_turned")
        hi_done = sem("conv_hi_done")
        lo_done = sem("conv_lo_done")
        multiplied = sem("conv_multiplied")
        z_done = sem("conv_z_done")
        stats_done = sem("conv_stats_done")
        ln = sem("conv_ln")
        rooted = sem("conv_rooted")
        x2_done = sem("conv_x2_done")
        y_done = sem("conv_y_done")
        stored = [sem(f"conv_stored{s}") for s in range(3)]
        scattered = [sem(f"conv_scattered{s}") for s in range(3)]

        with nc.Block() as block:

            @block.sync
            def _(sp):
                sp.dma_start(tabs[:, :, :], tab_d.rearrange("(t p) k -> p t k", p=P)).then_inc(small_in, 16)
                sp.dma_start(w_raw[:, :, :], w.rearrange("(c p) n -> p c n", p=P)).then_inc(w_in, 16)
                sp.wait_ge(zeroed, 2)
                with sp.Fori(0, ET // RING) as i:
                    for s in range(RING):
                        t = RING * i + s
                        sp.wait_ge(z_done, t + 1)
                        if s == RING - 1:
                            sp.wait_ge(masks_done, t - 2)
                        sp.dma_start(tab[s][:, :], tab_d[bass.ds(t * P, P), :]).then_inc(tab_in[s], 16)
                        sp.dma_start(key_row[s][:, :],
                                     row_d[bass.ds(t * P + 1, P)].partition_broadcast(P)).then_inc(tab_in[s], 16)
                for t in range(ET):
                    out = normed[t % 3]
                    sp.wait_ge(x2_done, t + 1)
                    sp.dma_start(x2_rows[t * P:(t + 1) * P, :], out[:, 0, :]).then_inc(stored[t % 3], 16)
                    sp.dma_start(x2_rows[EP + t * P:EP + (t + 1) * P, :], out[:, 1, :]).then_inc(stored[t % 3], 16)
                for s in range(3):
                    sp.wait_ge(stored[s], 32 * len(range(s, ET, 3)))

            @block.gpsimd
            def _(pool):
                pool.memset(ident[:, :], 0.0).then_inc(const_done, 1)
                pool.memset(last_row[:, :], 0.0).then_inc(const_done, 1)
                pool.wait_ge(const_done, 2)
                pool.affine_select(out=ident[:, :], in_=ident[:, :], compare_op=ALU.not_equal, fill=1.0,
                                   base=0, pattern=[[-1, P]], channel_multiplier=1).then_inc(const_done, 1)
                pool.affine_select(out=last_row[:, :], in_=last_row[:, :], compare_op=ALU.not_equal, fill=1.0,
                                   base=1 - P, pattern=[[0, 1]], channel_multiplier=1).then_inc(const_done, 1)
                pool.wait_ge(small_in, 16)
                index = lambda t, k: bass.IndirectOffsetOnAxis(tabs[:, t, k:k + 1].bitcast(I32), 0)
                for t in range(ET):
                    s = t % RING
                    if t >= RING:
                        pool.wait_ge(z_done, t + 1)
                    pool.indirect_dma_start(x_src[:, t * D:(t + 1) * D], None, x1_rows,
                                            index(t, D_SRC)).then_inc(src_in[s], 16)
                    pool.indirect_dma_start(x_dst[s][:, :], None, x1_rows, index(t, D_DST)).then_inc(dst_in[s], 16)
                for t in range(ET):
                    pool.wait_ge(y_done, t + 1)
                    pool.indirect_dma_start(y_rows, index(t, D_OUT), normed[t % 3][:, 2, :],
                                            None).then_inc(scattered[t % 3], 16)
                for s in range(3):
                    pool.wait_ge(scattered[s], 16 * len(range(s, ET, 3)))

            @block.tensor
            def _(pe):
                pe.sem_inc(summed, 2)
                pe.sem_inc(turned, 2)
                pe.sem_inc(multiplied, 2)
                pe.wait_ge(const_done, 4)
                pe.wait_ge(zeroed, 2)

                def sum_edges(i, s):
                    t = RING * i + s
                    q = s % 2
                    pe.wait_ge(masks_done, t + 1)
                    pe.wait_ge(src_in[s], 16 * (i + 1))
                    pe.wait_ge(sums_out, t + 1)
                    pe.matmul(sum_ps[q][:, :], mask[q][:, 0, :], x_src[:, bass.ds(t * D, D)], start=True, stop=False)
                    pe.wait_ge(sums_out, t + 2)
                    pe.matmul(sum_ps[q][:, :], mask[q][:, 1, :], sums[1 - q][:, :], start=False, stop=True).then_inc(summed, 1)

                def product(i, s):
                    t = RING * i + s
                    q = s % 2
                    pe.wait_ge(sums_out, t + 3)
                    pe.wait_ge(lo_done, t + 1)
                    for k in range(KC):
                        last = pe.transpose(t_ps[q][:, k, :], sums[q][:, k * P:(k + 1) * P], ident[:, :])
                    last.then_inc(turned, 1)
                    pe.wait_ge(lo_done, t + 3)
                    pe.wait_ge(z_done, t + 3)
                    for k in range(KC):
                        pe.matmul(y_ps[q][:, :], t_hi[q][:, k, :], w_hi[:, k, :], start=(k == 0), stop=False)
                        pe.matmul(y_ps[q][:, :], t_hi[q][:, k, :], w_lo[:, k, :], start=False, stop=False)
                        last = pe.matmul(y_ps[q][:, :], t_lo[q][:, k, :], w_hi[:, k, :], start=False, stop=(k == KC - 1))
                    last.then_inc(multiplied, 1)

                pe.wait_ge(w_split, 2)
                sum_edges(0, 0)

                def body(i, last):
                    for s in range(RING):
                        if s < RING - 1:
                            sum_edges(i, s + 1)
                        elif not last:
                            sum_edges(i + 1, 0)
                        product(i, s)

                with pe.Fori(0, ET // RING - 1) as i:
                    body(i, False)
                body(ET // RING - 1, True)

            @block.scalar
            def _(act):
                act.sem_inc(sums_out, 2)
                with act.Fori(0, ET // RING) as i:
                    for s in range(RING):
                        t = RING * i + s
                        act.wait_ge(summed, t + 3)
                        act.wait_ge(turned, t + 1)
                        act.activation(sums[s % 2][:, :], sum_ps[s % 2][:, :], ACT.Copy).then_inc(sums_out, 1)
                act.wait_ge(ln, 5)
                act.activation(rstd[:, :, :], inv[:, :, :], ACT.Sqrt).then_inc(rooted, 1)
                act.wait_ge(ln, 6)
                for t in range(ET):
                    out = normed[t % 3]
                    if t >= 3:
                        act.wait_ge(stored[t % 3], 32 * (t // 3))
                    act.activation(out[:, 0, :], z[:, t * D:(t + 1) * D], ACT.Identity,
                                   bias=shift[:, 0, 2 * t:2 * t + 1], scale=rstd[:, 0, 2 * t:2 * t + 1])
                    act.activation(out[:, 1, :], x_src[:, t * D:(t + 1) * D], ACT.Identity,
                                   bias=shift[:, 0, 2 * t + 1:2 * t + 2],
                                   scale=rstd[:, 0, 2 * t + 1:2 * t + 2]).then_inc(x2_done, 1)

            @block.vector
            def _(dve):
                dve.sem_inc(lo_done, 2)
                dve.sem_inc(z_done, 4)
                dve.memset(tab[RING - 1][:, :], -5.0).then_inc(zeroed, 1)
                dve.memset(sums[1][:, :], 0.0).then_inc(zeroed, 1)
                dve.wait_ge(w_in, 16)
                dve.tensor_copy(w_hi[:, :, :], w_raw[:, :, :]).then_inc(w_split, 1)
                dve.wait_ge(w_split, 1)
                dve.tensor_tensor(w_lo[:, :, :], w_raw[:, :, :], w_hi[:, :, :].bitcast(F32), ALU.subtract).then_inc(w_split, 1)

                def masks(i, s):
                    t = RING * i + s
                    dve.wait_ge(tab_in[s], 32 * (i + 1))
                    dve.wait_ge(summed, t + 1)
                    m = mask[s % 2]
                    dve.tensor_scalar(m[:, 0, :], key_row[s][:, :], tab[s][:, KEY:KEY + 1], tab[s][:, D_EW:D_EW + 1],
                                      ALU.is_equal, ALU.mult)
                    dve.tensor_scalar(m[:, 1, :], key_row[s][:, :], tab[(s - 1) % RING][:, KEY:KEY + 1],
                                      last_row[:, 0:1], ALU.is_equal, ALU.mult).then_inc(masks_done, 1)

                def split(i, s):
                    t = RING * i + s
                    q = s % 2
                    dve.wait_ge(turned, t + 3)
                    dve.wait_ge(multiplied, t + 1)
                    dve.tensor_copy(t_hi[q][:, :, :], t_ps[q][:, :, :]).then_inc(hi_done, 1)
                    dve.wait_ge(hi_done, t + 1)
                    dve.tensor_tensor(t_lo[q][:, :, :], t_ps[q][:, :, :], t_hi[q][:, :, :].bitcast(F32),
                                      ALU.subtract).then_inc(lo_done, 1)

                def finish(i, s):
                    t = RING * i + s
                    dve.bn_stats(stats[:, bass.ds((2 * t + 1) * 6, 6)], x_src[:, bass.ds(t * D, D)])
                    dve.wait_ge(multiplied, t + 3)
                    dve.wait_ge(dst_in[s], 16 * (i + 1))
                    dve.scalar_tensor_tensor(z[:, bass.ds(t * D, D)], y_ps[s % 2][:, :], 0.0, x_dst[s][:, :],
                                             ALU.max, ALU.add).then_inc(z_done, 1)
                    dve.wait_ge(z_done, t + 5)
                    dve.bn_stats(stats[:, bass.ds(2 * t * 6, 6)], z[:, bass.ds(t * D, D)]).then_inc(stats_done, 1)

                dve.wait_ge(const_done, 4)
                dve.wait_ge(zeroed, 2)
                masks(0, 0)

                def body(i, last):
                    for s in range(RING):
                        if s < RING - 1:
                            masks(i, s + 1)
                        elif not last:
                            masks(i + 1, 0)
                        split(i, s)
                        finish(i, s)

                with dve.Fori(0, ET // RING - 1) as i:
                    body(i, False)
                body(ET // RING - 1, True)
                dve.wait_ge(stats_done, ET)
                for n in range(2 * ET):
                    last = dve.bn_aggr(mv[:, n, :], stats[:, 6 * n:6 * n + 6])
                last.then_inc(ln, 1)
                dve.wait_ge(ln, 1)
                var = mv[:, :, 1]
                dve.tensor_scalar(ds[:, 0, :], var, EPS, None, ALU.add).then_inc(ln, 1)
                for n, (a, b) in enumerate(((0, 2), (2, 1))):
                    dve.wait_ge(ln, 2 + n)
                    dve.scalar_tensor_tensor(ds[:, b, :], ds[:, a, :], EPS, var, ALU.mult, ALU.add).then_inc(ln, 1)
                dve.wait_ge(ln, 4)
                dve.reciprocal(inv[:, :, :], ds[:, 0:2, :]).then_inc(ln, 1)
                dve.wait_ge(rooted, 1)
                for n in range(2):
                    last = dve.scalar_tensor_tensor(shift[:, n, :], mv[:, :, 0], -1.0, rstd[:, n, :], ALU.mult, ALU.mult)
                last.then_inc(ln, 1)
                dve.wait_ge(ln, 6)
                for t in range(ET):
                    if t >= 3:
                        dve.wait_ge(scattered[t % 3], 16 * (t // 3))
                    dve.tensor_scalar(normed[t % 3][:, 2, :], z[:, t * D:(t + 1) * D], rstd[:, 1, 2 * t:2 * t + 1],
                                      shift[:, 1, 2 * t:2 * t + 1], ALU.mult, ALU.add).then_inc(y_done, 1)


def painn_edges(nc, sem, x2_rows, row_s, tab_s, u_tab, w_in, w_o1s, w_o1v, w_o2s, w_o2v, x3_rows):
    RING = 4
    B = P
    F = w_in.shape[2]
    M_COLS = 4 * F + 3 * 2 * F
    with ExitStack() as ctx:
        sb = lambda n, s, d=F32: ctx.enter_context(nc.sbuf_tensor(f"painn_{n}", s, d))
        ps = lambda n, s: ctx.enter_context(nc.psum_tensor(f"painn_{n}", s, F32))
        tabs = sb("tabs", [P, ET, TAB])
        w_in_sb = sb("w_in_sb", [B, 2, F])
        o1s_raw = sb("o1s_raw", [P, B])
        o1v_raw = sb("o1v_raw", [2 * F, B])
        o1s = sb("o1s", [P, B])
        o1v = sb("o1v", [2 * F, B])
        o2s = sb("o2s", [B, B])
        o2v = sb("o2v", [B, B])
        ident = sb("ident", [P, P])
        last_row = sb("last_row", [P, 1])
        half = sb("half", [P, 1])
        tab = [sb(f"tab{s}", [P, TAB]) for s in range(RING)]
        key_row = [sb(f"key_row{s}", [P, P]) for s in range(RING)]
        x_dst = [sb(f"x_dst{s}", [P, D]) for s in range(RING)]
        x_kept = sb("x_kept", [P, ET * D])
        x_src = [sb(f"x_src{s}", [P, D]) for s in range(RING)]
        u = [sb(f"u{s}", [P, 8 * F]) for s in range(RING)]
        x_t = sb("x_t", [B, 4, P])
        feat = sb("feat", [P, 4, F])
        mask = sb("mask", [P, 2, P])
        msg = sb("msg", [P, M_COLS])
        sums = [sb(f"sums{s}", [P, M_COLS]) for s in range(2)]
        sums_t = sb("sums_t", [P, 4, P])
        hid = sb("hid", [B, 4, P])
        mag = sb("mag", [B, P])
        decay = sb("decay", [B, P])
        soft = sb("soft", [B, P])
        scal = sb("scal", [B, P])
        z = sb("z", [P, ET * D])
        stats = sb("stats", [P, 2 * ET * 6])
        mv = sb("mv", [P, 2 * ET, 2])
        var = sb("var", [P, 2 * ET])
        inv = sb("inv", [P, 2 * ET])
        rstd = sb("rstd", [P, 2 * ET])
        shift = sb("shift", [P, 2 * ET])
        normed = [sb(f"normed{s}", [P, 2, D]) for s in range(3)]
        x_ps = ps("x_ps", [B, 4, P])
        feat_ps = ps("feat_ps", [P, 4, F])
        sum_ps = ps("sum_ps", [P, M_COLS])
        sums_t_ps = ps("sums_t_ps", [P, 4, P])
        o1_ps = ps("o1_ps", [B, 4, P])
        o2_ps = ps("o2_ps", [P, 4, B])

        small_in = sem("painn_small_in")
        w_scaled = sem("painn_w_scaled")
        const_done = sem("painn_const_done")
        zeroed = sem("painn_zeroed")
        tab_in = [sem(f"painn_tab_in{s}") for s in range(RING)]
        x_in = [sem(f"painn_x_in{s}") for s in range(RING)]
        kept = sem("painn_kept")
        x_turned = sem("painn_x_turned")
        xt_out = sem("painn_xt_out")
        feat_done = sem("painn_feat_done")
        feat_out = sem("painn_feat_out")
        masks_done = sem("painn_masks_done")
        msg_done = sem("painn_msg_done")
        summed = sem("painn_summed")
        sums_out = sem("painn_sums_out")
        sums_turned = sem("painn_sums_turned")
        st_out = sem("painn_st_out")
        o1_done = sem("painn_o1_done")
        o1_out = sem("painn_o1_out")
        soft_steps = sem("painn_soft_steps")
        scal_done = sem("painn_scal_done")
        o2_done = sem("painn_o2_done")
        z_done = sem("painn_z_done")
        stats_done = sem("painn_stats_done")
        ln = sem("painn_ln")
        rooted = sem("painn_rooted")
        own_done = sem("painn_own_done")
        far_done = sem("painn_far_done")
        stored = [sem(f"painn_stored{s}") for s in range(3)]

        with nc.Block() as block:

            @block.sync
            def _(sp):
                sp.dma_start(tabs[:, :, :], tab_s.rearrange("(t p) k -> p t k", p=P)).then_inc(small_in, 16)
                sp.dma_start(w_in_sb[:, :, :], w_in).then_inc(small_in, 16)
                sp.dma_start(o1s_raw[0:F, :], w_o1s[0:F, :]).then_inc(small_in, 16)
                for c in range(3):
                    sp.dma_start(o1s_raw[(1 + c) * F:(2 + c) * F, :], w_o1s[F:2 * F, :]).then_inc(small_in, 16)
                sp.dma_start(o1v_raw[:, :], w_o1v).then_inc(small_in, 16)
                sp.dma_start(o2s[:, :], w_o2s).then_inc(small_in, 16)
                sp.dma_start(o2v[:, :], w_o2v).then_inc(small_in, 16)
                sp.wait_ge(zeroed, 3)
                with sp.Fori(0, ET // RING) as i:
                    for s in range(RING):
                        t = RING * i + s
                        sp.wait_ge(z_done, t + 1)
                        if s == RING - 1:
                            sp.wait_ge(masks_done, t - 2)
                        sp.dma_start(tab[s][:, :], tab_s[bass.ds(t * P, P), :]).then_inc(tab_in[s], 16)
                        sp.dma_start(key_row[s][:, :],
                                     row_s[bass.ds(t * P + 1, P)].partition_broadcast(P)).then_inc(tab_in[s], 16)
                for t in range(ET):
                    out = normed[t % 3]
                    sp.wait_ge(own_done, t + 1)
                    sp.dma_start(x3_rows[t * P:(t + 1) * P, :], out[:, 0, :]).then_inc(stored[t % 3], 16)
                    sp.wait_ge(far_done, t + 1)
                    sp.dma_start(x3_rows[EP + t * P:EP + (t + 1) * P, :], out[:, 1, :]).then_inc(stored[t % 3], 16)
                for s in range(3):
                    sp.wait_ge(stored[s], 32 * len(range(s, ET, 3)))

            @block.gpsimd
            def _(pool):
                pool.memset(ident[:, :], 0.0).then_inc(const_done, 1)
                pool.memset(last_row[:, :], 0.0).then_inc(const_done, 1)
                pool.memset(half[:, :], 0.5).then_inc(const_done, 1)
                pool.wait_ge(const_done, 3)
                pool.affine_select(out=ident[:, :], in_=ident[:, :], compare_op=ALU.not_equal, fill=1.0,
                                   base=0, pattern=[[-1, P]], channel_multiplier=1).then_inc(const_done, 1)
                pool.affine_select(out=last_row[:, :], in_=last_row[:, :], compare_op=ALU.not_equal, fill=1.0,
                                   base=1 - P, pattern=[[0, 1]], channel_multiplier=1).then_inc(const_done, 1)
                pool.wait_ge(small_in, 16 * 9)
                index = lambda t, k: bass.IndirectOffsetOnAxis(tabs[:, t, k:k + 1].bitcast(I32), 0)

                def keep(t):
                    pool.wait_ge(x_in[t % RING], 48 * (t // RING + 1))
                    pool.tensor_copy(x_kept[:, t * D:(t + 1) * D], x_dst[t % RING][:, :]).then_inc(kept, 1)

                for t in range(ET):
                    s = t % RING
                    if t >= RING:
                        keep(t - RING)
                        pool.wait_ge(z_done, t + 1)
                        pool.wait_ge(kept, t - RING + 1)
                    pool.indirect_dma_start(x_dst[s][:, :], None, x2_rows,
                                            index(t, S_X2DST)).then_inc(x_in[s], 16)
                    pool.indirect_dma_start(u[s][:, :], None, u_tab, index(t, S_EDGE)).then_inc(x_in[s], 16)
                    pool.indirect_dma_start(x_src[s][:, :], None, x2_rows, index(t, S_X2SRC)).then_inc(x_in[s], 16)
                for t in range(ET - RING, ET):
                    keep(t)

            @block.tensor
            def _(pe):
                for done in (feat_done, o1_done, o2_done, summed):
                    pe.sem_inc(done, 1)
                pe.wait_ge(const_done, 5)
                pe.wait_ge(w_scaled, 2)
                pe.wait_ge(zeroed, 3)

                def turn_x(i, s):
                    t = RING * i + s
                    pe.wait_ge(x_in[s], 48 * (i + 1))
                    pe.wait_ge(xt_out, t + 1)
                    pe.transpose(x_ps[:, 0, :], x_dst[s][:, 0:B], ident[:, :])
                    vec = x_dst[s][:, B:D].rearrange("p (b c) -> p c b", c=3)
                    for c in range(3):
                        last = pe.transpose(x_ps[:, 1 + c, :], vec[:, c, :], ident[:, :])
                    last.then_inc(x_turned, 1)

                def features(i, s):
                    t = RING * i + s
                    pe.wait_ge(xt_out, t + 2)
                    pe.wait_ge(feat_out, t + 1)
                    for c in range(4):
                        last = pe.matmul(feat_ps[:, c, :], x_t[:, c, :], w_in_sb[:, min(c, 1), :], start=True, stop=True)
                    last.then_inc(feat_done, 1)

                def sum_edges(i, s):
                    t = RING * i + s
                    pe.wait_ge(masks_done, t + 1)
                    pe.wait_ge(msg_done, 3 * t + 4)
                    pe.wait_ge(sums_out, t + 1)
                    pe.matmul(sum_ps[:, :], mask[:, 0, :], msg[:, :], start=True, stop=False)
                    pe.matmul(sum_ps[:, :], mask[:, 1, :], sums[(s + 1) % 2][:, :], start=False, stop=True).then_inc(summed, 1)

                def turn_sums(i, s):
                    t = RING * i + s
                    pe.wait_ge(sums_out, t + 2)
                    pe.wait_ge(st_out, 2 * t + 1)
                    pe.transpose(sums_t_ps[:, 0, :], sums[s % 2][:, 0:4 * F], ident[:, :])
                    for c in range(3):
                        last = pe.transpose(sums_t_ps[0:2 * F, 1 + c, :], sums[s % 2][:, (4 + 2 * c) * F:(6 + 2 * c) * F],
                                            ident[:, :])
                    last.then_inc(sums_turned, 1)

                def out_one(i, s):
                    t = RING * i + s
                    pe.wait_ge(st_out, 2 * t + 3)
                    pe.wait_ge(o1_out, t + 1)
                    pe.matmul(o1_ps[:, 0, :], o1s[:, :], sums_t[:, 0, :], start=True, stop=True)
                    pe.matmul(o1_ps[:, 1:4, :], o1v[:, :], sums_t[0:2 * F, 1:4, :], start=True, stop=True).then_inc(o1_done, 1)

                def out_two(i, s):
                    t = RING * i + s
                    pe.wait_ge(o1_out, t + 2)
                    pe.wait_ge(z_done, t + 4)
                    for c in range(3):
                        pe.matmul(o2_ps[:, 1 + c, :], hid[:, 1 + c, :], o2v[:, :], start=True, stop=True)
                    pe.wait_ge(scal_done, t + 2)
                    pe.matmul(o2_ps[:, 0, :], scal[:, :], o2s[:, :], start=True, stop=True).then_inc(o2_done, 1)

                turn_x(0, 0)
                features(0, 0)
                sum_edges(0, 0)

                def body(i, last):
                    for s in range(RING):
                        nxt = (i, s + 1) if s < RING - 1 else None if last else (i + 1, 0)
                        if nxt:
                            turn_x(*nxt)
                        turn_sums(i, s)
                        if nxt:
                            features(*nxt)
                        out_one(i, s)
                        if nxt:
                            sum_edges(*nxt)
                        out_two(i, s)

                with pe.Fori(0, ET // RING - 1) as i:
                    body(i, False)
                body(ET // RING - 1, True)

            @block.scalar
            def _(act):
                for done in (xt_out, feat_out, sums_out, st_out, o1_out):
                    act.sem_inc(done, 1)
                act.wait_ge(const_done, 5)

                def copy_xt(i, s):
                    t = RING * i + s
                    act.wait_ge(x_turned, t + 1)
                    act.wait_ge(feat_done, t + 1)
                    act.activation(x_t[:, :, :], x_ps[:, :, :], ACT.Copy).then_inc(xt_out, 1)

                def copy_features(i, s):
                    t = RING * i + s
                    act.wait_ge(feat_done, t + 2)
                    act.wait_ge(msg_done, 3 * t + 1)
                    act.activation(feat[:, :, :], feat_ps[:, :, :], ACT.Copy, scale=B ** -0.5).then_inc(feat_out, 1)

                def copy_sums(i, s):
                    t = RING * i + s
                    act.wait_ge(summed, t + 2)
                    act.activation(sums[s % 2][:, :], sum_ps[:, :], ACT.Copy).then_inc(sums_out, 1)

                def copy_sums_t(i, s):
                    t = RING * i + s
                    act.wait_ge(sums_turned, t + 1)
                    act.wait_ge(o1_done, t + 1)
                    act.activation(sums_t[:, 0, :], sums_t_ps[:, 0, :], ACT.Copy).then_inc(st_out, 1)
                    act.activation(sums_t[0:2 * F, 1:4, :], sums_t_ps[0:2 * F, 1:4, :], ACT.Copy).then_inc(st_out, 1)

                def softplus(i, s):
                    t = RING * i + s
                    act.wait_ge(o1_done, t + 2)
                    act.wait_ge(o2_done, t + 1)
                    act.wait_ge(scal_done, t + 1)
                    act.activation(hid[:, :, :], o1_ps[:, :, :], ACT.Copy).then_inc(o1_out, 1)
                    act.wait_ge(o1_out, t + 2)
                    act.activation(mag[:, :], hid[:, 0, :], ACT.Abs).then_inc(soft_steps, 1)
                    act.wait_ge(soft_steps, 3 * t + 1)
                    act.activation(decay[:, :], mag[:, :], ACT.Exp, scale=-1.0).then_inc(soft_steps, 1)
                    act.wait_ge(soft_steps, 3 * t + 2)
                    act.activation(soft[:, :], decay[:, :], ACT.Ln, bias=half[:, 0:1], scale=0.5).then_inc(soft_steps, 1)

                copy_xt(0, 0)
                copy_features(0, 0)

                def body(i, last):
                    for s in range(RING):
                        nxt = (i, s + 1) if s < RING - 1 else None if last else (i + 1, 0)
                        copy_sums(i, s)
                        if nxt:
                            copy_xt(*nxt)
                        copy_sums_t(i, s)
                        if nxt:
                            copy_features(*nxt)
                        softplus(i, s)

                with act.Fori(0, ET // RING - 1) as i:
                    body(i, False)
                body(ET // RING - 1, True)
                act.wait_ge(ln, 3)
                act.activation(rstd[:, :], inv[:, :], ACT.Sqrt).then_inc(rooted, 1)
                act.wait_ge(ln, 4)
                for t in range(ET):
                    if t >= 3:
                        act.wait_ge(stored[t % 3], 32 * (t // 3))
                    act.activation(normed[t % 3][:, 0, :], z[:, t * D:(t + 1) * D], ACT.Identity,
                                   bias=shift[:, 2 * t:2 * t + 1], scale=rstd[:, 2 * t:2 * t + 1]).then_inc(own_done, 1)

            @block.vector
            def _(dve):
                for done in (msg_done, scal_done):
                    dve.sem_inc(done, 1)
                dve.sem_inc(z_done, 4)
                dve.memset(tab[RING - 1][:, :], -5.0).then_inc(zeroed, 1)
                for s in range(2):
                    dve.memset(sums[s][:, :], 0.0).then_inc(zeroed, 1)
                dve.wait_ge(small_in, 16 * 9)
                dve.tensor_scalar(o1s[:, :], o1s_raw[:, :], (2 * F) ** -0.5, None, ALU.mult).then_inc(w_scaled, 1)
                dve.tensor_scalar(o1v[:, :], o1v_raw[:, :], (2 * F) ** -0.5, None, ALU.mult).then_inc(w_scaled, 1)
                dve.wait_ge(const_done, 5)
                dve.wait_ge(zeroed, 3)

                def masks(i, s):
                    t = RING * i + s
                    dve.wait_ge(tab_in[s], 32 * (i + 1))
                    dve.wait_ge(summed, t + 1)
                    dve.tensor_scalar(mask[:, 0, :], key_row[s][:, :], tab[s][:, KEY:KEY + 1], None, ALU.is_equal)
                    dve.tensor_scalar(mask[:, 1, :], key_row[s][:, :], tab[(s - 1) % RING][:, KEY:KEY + 1],
                                      last_row[:, 0:1], ALU.is_equal, ALU.mult).then_inc(masks_done, 1)

                def messages(i, s):
                    t = RING * i + s
                    dve.wait_ge(x_in[s], 48 * (i + 1))
                    dve.bn_stats(stats[:, bass.ds((2 * t + 1) * 6, 6)], x_dst[s][:, :])
                    dve.wait_ge(feat_out, t + 2)
                    dve.wait_ge(summed, t + 1)
                    flat = feat[:, :, :].rearrange("p c f -> p (c f)")
                    dve.tensor_tensor(msg[:, 0:4 * F], flat, u[s][:, 0:4 * F], ALU.mult).then_inc(msg_done, 1)
                    pairs = msg[:, 4 * F:].rearrange("p (c k f) -> p k c f", c=3, k=2)
                    dve.tensor_tensor(pairs[:, 0, :, :], feat[:, 0:1, :].to_broadcast([P, 3, F]),
                                      u[s][:, 4 * F:7 * F].rearrange("p (c f) -> p c f", c=3), ALU.mult).then_inc(msg_done, 1)
                    dve.tensor_tensor(pairs[:, 1, :, :], feat[:, 1:4, :],
                                      u[s][:, 7 * F:8 * F].rearrange("p (c f) -> p c f", c=1).to_broadcast([P, 3, F]),
                                      ALU.mult).then_inc(msg_done, 1)

                def finish(i, s):
                    t = RING * i + s
                    dve.wait_ge(soft_steps, 3 * t + 3)
                    dve.wait_ge(o2_done, t + 1)
                    dve.scalar_tensor_tensor(scal[:, :], hid[:, 0, :], 0.0, soft[:, :], ALU.max, ALU.add).then_inc(scal_done, 1)
                    dve.wait_ge(o2_done, t + 2)
                    dve.scalar_tensor_tensor(z[:, bass.ds(t * D, B)], o2_ps[:, 0, :], B ** -0.5, x_src[s][:, 0:B],
                                             ALU.mult, ALU.add)
                    vec = lambda ap: ap.rearrange("p (d c) -> p c d", c=3)
                    dve.scalar_tensor_tensor(vec(z[:, bass.ds(t * D + B, 3 * B)]), o2_ps[:, 1:4, :], B ** -0.5,
                                             vec(x_src[s][:, B:D]), ALU.mult, ALU.add).then_inc(z_done, 1)
                    dve.wait_ge(z_done, t + 5)
                    dve.bn_stats(stats[:, bass.ds(2 * t * 6, 6)], z[:, bass.ds(t * D, D)]).then_inc(stats_done, 1)

                masks(0, 0)
                messages(0, 0)

                def body(i, last):
                    for s in range(RING):
                        nxt = (i, s + 1) if s < RING - 1 else None if last else (i + 1, 0)
                        if nxt:
                            masks(*nxt)
                            messages(*nxt)
                        finish(i, s)

                with dve.Fori(0, ET // RING - 1) as i:
                    body(i, False)
                body(ET // RING - 1, True)
                dve.wait_ge(stats_done, ET)
                for n in range(2 * ET):
                    last = dve.bn_aggr(mv[:, n, :], stats[:, 6 * n:6 * n + 6])
                last.then_inc(ln, 1)
                dve.wait_ge(ln, 1)
                dve.tensor_scalar(var[:, :], mv[:, :, 1], EPS, None, ALU.add).then_inc(ln, 1)
                dve.wait_ge(ln, 2)
                dve.reciprocal(inv[:, :], var[:, :]).then_inc(ln, 1)
                dve.wait_ge(rooted, 1)
                dve.scalar_tensor_tensor(shift[:, :], mv[:, :, 0], -1.0, rstd[:, :], ALU.mult, ALU.mult).then_inc(ln, 1)
                dve.wait_ge(ln, 4)
                dve.wait_ge(kept, ET)
                for t in range(ET):
                    if t >= 3:
                        dve.wait_ge(stored[t % 3], 32 * (t // 3))
                    n = 2 * t + 1
                    dve.tensor_scalar(normed[t % 3][:, 1, :], x_kept[:, t * D:(t + 1) * D], rstd[:, n:n + 1],
                                      shift[:, n:n + 1], ALU.mult, ALU.add).then_inc(far_done, 1)


def mlp_edges(nc, sem, x3_rows, row_s, tab_s, w_t, b, y_rows):
    RING = 4
    KC = 2 * D // P
    with ExitStack() as ctx:
        sb = lambda n, s, d=F32: ctx.enter_context(nc.sbuf_tensor(f"mlp_{n}", s, d))
        ps = lambda n, s: ctx.enter_context(nc.psum_tensor(f"mlp_{n}", s, F32))
        tabs = sb("tabs", [P, ET, TAB])
        w_raw = sb("w_raw", [P, 2, D])
        w_hi = sb("w_hi", [P, KC, D], F32R)
        w_lo = sb("w_lo", [P, KC, D], F32R)
        b_rows = sb("b_rows", [P, D])
        ident = sb("ident", [P, P])
        last_row = sb("last_row", [P, 1])
        tab = [sb(f"tab{s}", [P, TAB]) for s in range(RING)]
        key_row = [sb(f"key_row{s}", [P, P]) for s in range(RING)]
        pair = [sb(f"pair{s}", [P, 2, D]) for s in range(RING)]
        mask = [sb(f"mask{s}", [P, 2, P]) for s in range(2)]
        t_hi = [sb(f"t_hi{s}", [P, KC, P], F32R) for s in range(2)]
        t_lo = [sb(f"t_lo{s}", [P, KC, P], F32R) for s in range(2)]
        pre = [sb(f"pre{s}", [P, D]) for s in range(2)]
        msg = [sb(f"msg{s}", [P, D]) for s in range(2)]
        sums = [sb(f"sums{s}", [P, D]) for s in range(2)]
        z = sb("z", [P, ET * D])
        stats = sb("stats", [P, ET * 6])
        mv = sb("mv", [P, ET, 2])
        var = sb("var", [P, ET])
        inv = sb("inv", [P, ET])
        rstd = sb("rstd", [P, ET])
        shift = sb("shift", [P, ET])
        y = [sb(f"y{s}", [P, D]) for s in range(4)]
        t_ps = [ps(f"t_ps{s}", [P, KC // 2, P]) for s in range(2)]
        m_ps = [ps(f"m_ps{s}", [P, D]) for s in range(2)]
        sum_ps = [ps(f"sum_ps{s}", [P, D]) for s in range(2)]

        small_in = sem("mlp_small_in")
        w_in = [sem(f"mlp_w_in{s}") for s in range(2)]
        w_hi_done = sem("mlp_w_hi_done")
        w_lo_done = sem("mlp_w_lo_done")
        const_done = sem("mlp_const_done")
        zeroed = sem("mlp_zeroed")
        tab_in = [sem(f"mlp_tab_in{s}") for s in range(RING)]
        pair_in = [sem(f"mlp_pair_in{s}") for s in range(RING)]
        turned = sem("mlp_turned")
        hi_done = sem("mlp_hi_done")
        lo_done = sem("mlp_lo_done")
        multiplied = sem("mlp_multiplied")
        pre_done = sem("mlp_pre_done")
        msg_done = sem("mlp_msg_done")
        masks_done = sem("mlp_masks_done")
        summed = sem("mlp_summed")
        sums_out = sem("mlp_sums_out")
        z_done = sem("mlp_z_done")
        stats_done = sem("mlp_stats_done")
        ln = sem("mlp_ln")
        rooted = sem("mlp_rooted")
        even_done = sem("mlp_even_done")
        odd_done = sem("mlp_odd_done")
        scattered = [sem(f"mlp_scattered{s}") for s in range(4)]

        with nc.Block() as block:

            @block.sync
            def _(sp):
                sp.dma_start(tabs[:, :, :], tab_s.rearrange("(t p) k -> p t k", p=P)).then_inc(small_in, 16)
                sp.dma_start(b_rows[:, :], b.partition_broadcast(P)).then_inc(small_in, 16)
                for k in range(KC):
                    if k >= 2:
                        sp.wait_ge(w_lo_done, k - 1)
                    sp.dma_start(w_raw[:, k % 2, :], w_t[k * P:(k + 1) * P, :]).then_inc(w_in[k % 2], 16)
                sp.wait_ge(zeroed, 3)
                with sp.Fori(0, ET // RING) as i:
                    for s in range(RING):
                        t = RING * i + s
                        sp.wait_ge(z_done, t + 1)
                        if s == RING - 1:
                            sp.wait_ge(masks_done, t - 2)
                        sp.dma_start(tab[s][:, :], tab_s[bass.ds(t * P, P), :]).then_inc(tab_in[s], 16)
                        sp.dma_start(key_row[s][:, :],
                                     row_s[bass.ds(t * P + 1, P)].partition_broadcast(P)).then_inc(tab_in[s], 16)

            @block.gpsimd
            def _(pool):
                pool.memset(ident[:, :], 0.0).then_inc(const_done, 1)
                pool.memset(last_row[:, :], 0.0).then_inc(const_done, 1)
                pool.wait_ge(const_done, 2)
                pool.affine_select(out=ident[:, :], in_=ident[:, :], compare_op=ALU.not_equal, fill=1.0,
                                   base=0, pattern=[[-1, P]], channel_multiplier=1).then_inc(const_done, 1)
                pool.affine_select(out=last_row[:, :], in_=last_row[:, :], compare_op=ALU.not_equal, fill=1.0,
                                   base=1 - P, pattern=[[0, 1]], channel_multiplier=1).then_inc(const_done, 1)
                pool.wait_ge(small_in, 32)
                index = lambda t, k: bass.IndirectOffsetOnAxis(tabs[:, t, k:k + 1].bitcast(I32), 0)
                for t in range(ET):
                    s = t % RING
                    if t >= RING:
                        pool.wait_ge(z_done, t + 1)
                    pool.indirect_dma_start(pair[s][:, 0, :], None, x3_rows, index(t, S_X3SRC)).then_inc(pair_in[s], 16)
                    pool.indirect_dma_start(pair[s][:, 1, :], None, x3_rows, index(t, S_X3DST)).then_inc(pair_in[s], 16)
                for t in range(ET):
                    pool.wait_ge((even_done, odd_done)[t % 2], t // 2 + 1)
                    pool.indirect_dma_start(y_rows, index(t, S_OUT), y[t % 4][:, :], None).then_inc(scattered[t % 4], 16)
                for s in range(4):
                    pool.wait_ge(scattered[s], 16 * len(range(s, ET, 4)))

            @block.tensor
            def _(pe):
                pe.sem_inc(multiplied, 2)
                pe.sem_inc(summed, 2)
                pe.wait_ge(const_done, 4)

                def turn(i, s):
                    t = RING * i + s
                    pe.wait_ge(pair_in[s], 32 * (i + 1))
                    for n in range(2):
                        pe.wait_ge(lo_done, 2 * t + n + 1)
                        for k in range(KC // 2):
                            last = pe.transpose(t_ps[n][:, k, :], pair[s][:, n, k * P:(k + 1) * P], ident[:, :])
                        last.then_inc(turned, 1)

                def product(i, s):
                    t = RING * i + s
                    q = s % 2
                    pe.wait_ge(pre_done, t + 1)
                    for k in range(KC):
                        if k % (KC // 2) == 0:
                            pe.wait_ge(lo_done, 2 * t + 3 if k else 2 * t + 2)
                        pe.matmul(m_ps[q][:, :], t_hi[q][:, k, :], w_hi[:, k, :], start=(k == 0), stop=False)
                        pe.matmul(m_ps[q][:, :], t_hi[q][:, k, :], w_lo[:, k, :], start=False, stop=False)
                        last = pe.matmul(m_ps[q][:, :], t_lo[q][:, k, :], w_hi[:, k, :], start=False, stop=(k == KC - 1))
                    last.then_inc(multiplied, 1)

                def sum_edges(i, s):
                    t = RING * i + s
                    q = s % 2
                    pe.wait_ge(masks_done, t + 1)
                    pe.wait_ge(msg_done, t + 3)
                    pe.wait_ge(sums_out, t + 1)
                    pe.matmul(sum_ps[q][:, :], mask[q][:, 0, :], msg[q][:, :], start=True, stop=False)
                    pe.wait_ge(sums_out, t + 2)
                    pe.matmul(sum_ps[q][:, :], mask[q][:, 1, :], sums[1 - q][:, :], start=False, stop=True).then_inc(summed, 1)

                pe.wait_ge(zeroed, 3)
                turn(0, 0)
                pe.wait_ge(w_lo_done, KC)
                product(0, 0)
                turn(0, 1)

                def body(i, last):
                    for s in range(RING):
                        if s + 1 < RING:
                            product(i, s + 1)
                        elif not last:
                            product(i + 1, 0)
                        if s + 2 < RING:
                            turn(i, s + 2)
                        elif not last:
                            turn(i + 1, s + 2 - RING)
                        sum_edges(i, s)

                with pe.Fori(0, ET // RING - 1) as i:
                    body(i, False)
                body(ET // RING - 1, True)

            @block.scalar
            def _(act):
                act.sem_inc(sums_out, 2)
                act.sem_inc(msg_done, 2)

                def relu(i, s):
                    t = RING * i + s
                    act.wait_ge(pre_done, t + 3)
                    act.wait_ge(summed, t + 1)
                    act.activation(msg[s % 2][:, :], pre[s % 2][:, :], ACT.Relu).then_inc(msg_done, 1)

                def copy_sums(i, s):
                    t = RING * i + s
                    act.wait_ge(summed, t + 3)
                    act.wait_ge(z_done, t + 3)
                    act.activation(sums[s % 2][:, :], sum_ps[s % 2][:, :], ACT.Copy).then_inc(sums_out, 1)

                relu(0, 0)

                def body(i, last):
                    for s in range(RING):
                        if s + 1 < RING:
                            relu(i, s + 1)
                        elif not last:
                            relu(i + 1, 0)
                        copy_sums(i, s)

                with act.Fori(0, ET // RING - 1) as i:
                    body(i, False)
                body(ET // RING - 1, True)
                act.wait_ge(ln, 3)
                act.activation(rstd[:, :], inv[:, :], ACT.Sqrt).then_inc(rooted, 1)
                act.wait_ge(ln, 4)
                for t in range(0, ET, 2):
                    if t >= 4:
                        act.wait_ge(scattered[t % 4], 16 * (t // 4))
                    act.activation(y[t % 4][:, :], z[:, t * D:(t + 1) * D], ACT.Identity, bias=shift[:, t:t + 1],
                                   scale=rstd[:, t:t + 1]).then_inc(even_done, 1)

            @block.vector
            def _(dve):
                dve.sem_inc(lo_done, 1)
                dve.sem_inc(pre_done, 2)
                dve.sem_inc(z_done, 4)
                dve.memset(tab[RING - 1][:, :], -5.0).then_inc(zeroed, 1)
                for s in range(2):
                    dve.memset(sums[s][:, :], 0.0).then_inc(zeroed, 1)
                for k in range(KC):
                    dve.wait_ge(w_in[k % 2], 16 * (k // 2 + 1))
                    dve.tensor_copy(w_hi[:, k, :], w_raw[:, k % 2, :]).then_inc(w_hi_done, 1)
                    dve.wait_ge(w_hi_done, k + 1)
                    dve.tensor_tensor(w_lo[:, k, :], w_raw[:, k % 2, :], w_hi[:, k, :].bitcast(F32),
                                      ALU.subtract).then_inc(w_lo_done, 1)

                def split(i, s):
                    t = RING * i + s
                    q = s % 2
                    dve.wait_ge(multiplied, t + 1)
                    for n in range(2):
                        ks = slice(n * KC // 2, (n + 1) * KC // 2)
                        dve.wait_ge(turned, 2 * t + n + 1)
                        dve.tensor_copy(t_hi[q][:, ks, :], t_ps[n][:, :, :]).then_inc(hi_done, 1)
                        dve.wait_ge(hi_done, 2 * t + n + 1)
                        dve.tensor_tensor(t_lo[q][:, ks, :], t_ps[n][:, :, :], t_hi[q][:, ks, :].bitcast(F32),
                                          ALU.subtract).then_inc(lo_done, 1)

                def masks(i, s):
                    t = RING * i + s
                    dve.wait_ge(tab_in[s], 32 * (i + 1))
                    dve.wait_ge(summed, t + 1)
                    m = mask[s % 2]
                    dve.tensor_scalar(m[:, 0, :], key_row[s][:, :], tab[s][:, KEY:KEY + 1], None, ALU.is_equal)
                    dve.tensor_scalar(m[:, 1, :], key_row[s][:, :], tab[(s - 1) % RING][:, KEY:KEY + 1],
                                      last_row[:, 0:1], ALU.is_equal, ALU.mult).then_inc(masks_done, 1)

                def add_bias(i, s):
                    t = RING * i + s
                    dve.wait_ge(multiplied, t + 3)
                    dve.wait_ge(msg_done, t + 1)
                    dve.tensor_tensor(pre[s % 2][:, :], m_ps[s % 2][:, :], b_rows[:, :], ALU.add).then_inc(pre_done, 1)

                def finish(i, s):
                    t = RING * i + s
                    dve.wait_ge(sums_out, t + 3)
                    dve.wait_ge(pair_in[s], 32 * (i + 1))
                    dve.tensor_tensor(z[:, bass.ds(t * D, D)], sums[s % 2][:, :], pair[s][:, 0, :], ALU.add).then_inc(z_done, 1)
                    dve.wait_ge(z_done, t + 5)
                    dve.bn_stats(stats[:, bass.ds(t * 6, 6)], z[:, bass.ds(t * D, D)]).then_inc(stats_done, 1)

                dve.wait_ge(small_in, 32)
                dve.wait_ge(const_done, 4)
                dve.wait_ge(zeroed, 3)
                split(0, 0)
                masks(0, 0)
                add_bias(0, 0)
                split(0, 1)

                def body(i, last):
                    for s in range(RING):
                        if s + 1 < RING:
                            masks(i, s + 1)
                            add_bias(i, s + 1)
                        elif not last:
                            masks(i + 1, 0)
                            add_bias(i + 1, 0)
                        if s + 2 < RING:
                            split(i, s + 2)
                        elif not last:
                            split(i + 1, s + 2 - RING)
                        finish(i, s)

                with dve.Fori(0, ET // RING - 1) as i:
                    body(i, False)
                body(ET // RING - 1, True)
                dve.wait_ge(stats_done, ET)
                for t in range(ET):
                    last = dve.bn_aggr(mv[:, t, :], stats[:, 6 * t:6 * t + 6])
                last.then_inc(ln, 1)
                dve.wait_ge(ln, 1)
                dve.tensor_scalar(var[:, :], mv[:, :, 1], EPS, None, ALU.add).then_inc(ln, 1)
                dve.wait_ge(ln, 2)
                dve.reciprocal(inv[:, :], var[:, :]).then_inc(ln, 1)
                dve.wait_ge(rooted, 1)
                dve.scalar_tensor_tensor(shift[:, :], mv[:, :, 0], -1.0, rstd[:, :], ALU.mult, ALU.mult).then_inc(ln, 1)
                dve.wait_ge(ln, 4)
                for t in range(1, ET, 2):
                    if t >= 4:
                        dve.wait_ge(scattered[t % 4], 16 * (t // 4))
                    dve.tensor_scalar(y[t % 4][:, :], z[:, t * D:(t + 1) * D], rstd[:, t:t + 1], shift[:, t:t + 1],
                                      ALU.mult, ALU.add).then_inc(odd_done, 1)


def graph_layers(nc, x_t, x, ends_row, ends_col, ew_col, attr20_t, attr4_col, w1, a1, b1, w2, a2, b2, wfc, bfc,
                 conv_w, w_in, pw1, pb1, pw2b, w_o1s, w_o1v, w_o2s, w_o2v, mlp_w_t, mlp_b, out):
    table = lambda n, s: nc.dram_tensor(n, s, F32, kind="Internal").ap()
    rec_d, rec_s = table("rec_d", [EP + 1, REC]), table("rec_s", [EP + 1, REC])
    row_d, row_s = table("row_d", [EP + 2]), table("row_s", [EP + 2])
    map_d, map_s = table("map_d", [NT, 1]), table("map_s", [NT, 1])
    tab_d, tab_s = table("tab_d", [EP, TAB]), table("tab_s", [EP, TAB])
    h1, al1 = table("h1", [NT, HC]), table("al1", [NP, 2 * H])
    h2, al2 = table("h2", [NT, HC]), table("al2", [NP, 2 * H])
    bounce1, bounce2 = table("bounce1", [2, H * ET, P]), table("bounce2", [2, H * ET, P])
    w_tab1, w_tab2 = table("w_tab1", [EP, 2 * H]), table("w_tab2", [EP, 2 * H])
    x1 = table("x1", [NP, D])
    x2, x3 = table("x2", [2 * EP, D]), table("x3", [2 * EP, D])
    u_tab = table("u_tab", [EP, 256])
    def stage(build, *args):
        held = []

        def sem(name):
            held.append(nc.alloc_semaphore(name=name))
            return held[-1]

        build(nc, sem, *args)
        nc.clear_and_free_semaphores(held)
        nc.all_engine_barrier()

    stage(dense_and_prep, x_t, w1, a1, h1, al1, ends_row, ends_col, ew_col, rec_d, rec_s, row_d, row_s, map_d, map_s,
          tab_d, tab_s, attr20_t, pw1, pb1, pw2b, attr4_col, u_tab)
    stage(gat_edges, "e1", h1, al1, row_d, tab_d, bounce1, w_tab1)
    stage(gat_dense, h1, w2, b1, a2, h2, al2)
    stage(gat_edges, "e2", h2, al2, row_d, tab_d, bounce2, w_tab2)
    stage(fc_dense, h2, wfc, b2, x, bfc, x1, out)
    stage(conv_edges, x1, row_d, tab_d, conv_w, x2, out)
    stage(painn_edges, x2, row_s, tab_s, u_tab, w_in, w_o1s, w_o1v, w_o2s, w_o2v, x3)
    stage(mlp_edges, x3, row_s, tab_s, mlp_w_t, mlp_b, out)


def kernel(**inputs):
    import numpy as np
    import concourse.bacc as bacc
    from concourse.bass_utils import run_bass_kernel_spmd

    a = {k: np.asarray(v) for k, v in inputs.items()}
    g = lambda layer, name: a[f"L{layer}_gnn_{name}"]

    def padded(v, rows):
        return np.concatenate([v, np.zeros((rows - v.shape[0],) + v.shape[1:], v.dtype)])

    own = np.arange(N, N + EP - E, dtype=np.int32)
    ends = np.stack([np.concatenate([a[k].astype(np.int32), own]) for k in ("dst", "src")])
    x = padded(a["x"], NP)
    tiled = lambda v: padded(v, EP).reshape(ET, P, -1).transpose(1, 0, 2)
    columns = lambda v: v.reshape(-1, P).T
    pw2 = np.concatenate([g(2, "W2"), g(2, "b2")[None]])
    pw2 = pw2.reshape(pw2.shape[0], -1, 6).transpose(0, 2, 1).reshape(pw2.shape[0], -1)
    ins = [x.T, x, ends, ends.reshape(2, ET, P).transpose(2, 0, 1), tiled(a["edge_weight"])[:, :, 0],
           padded(a["edge_attr_20"], EP).T, tiled(a["edge_attr_4"]),
           g(0, "W1"), np.stack([g(0, "a_src1").ravel(), g(0, "a_dst1").ravel()]), columns(g(0, "b1")),
           g(0, "W2"), np.stack([g(0, "a_src2").ravel(), g(0, "a_dst2").ravel()]), columns(g(0, "b2")),
           g(0, "Wfc"), g(0, "bfc"), g(1, "weight"), np.stack([g(2, "w_in2f_s"), g(2, "w_in2f_v")], 1),
           g(2, "W1"), g(2, "b1")[:, None], pw2, g(2, "w_f2o1_s"), g(2, "w_f2o1_v"), g(2, "w_f2o2_s"),
           g(2, "w_f2o2_v"), g(3, "W").T, g(3, "b")]

    nc = bacc.Bacc("TRN2", target_bir_lowering=False, num_devices=1)
    arrays, args = {}, []
    for n, v in enumerate(ins):
        v = np.ascontiguousarray(v)
        arrays[f"in_{n}_dram"] = v
        args.append(nc.dram_tensor(f"in_{n}_dram", list(v.shape), mybir.dt.from_np(v.dtype), kind="ExternalInput").ap())
    out = nc.dram_tensor("out_0_dram", [NT, D], F32, kind="ExternalOutput").ap()
    graph_layers(nc, *args, out)
    r = run_bass_kernel_spmd(nc, [arrays], core_ids=[0])
    return r.results[0]["out_0_dram"][:N]
```

```python
from contextlib import ExitStack

import concourse.bass as bass
from concourse import mybir

F32 = mybir.dt.float32
F32R = mybir.dt.float32r
I32 = mybir.dt.int32
ALU = mybir.AluOpType
ACT = mybir.ActivationFunctionType

P = 128
N, E = 10000, 2500
TILES = -(-N // P)
NP = TILES * P
LOOPED = -(-TILES // 4) * 4 * P
ET = -(-E // P)
EP = ET * P
NT = NP + EP
H, C = 4, 256
HC = H * C
D = 512
EPS = 1e-5

REC = 8
TAB = 8
D_SRC, D_DST, D_OUT, KEY, D_EW = range(5)
S_X2DST, S_X2SRC, S_X3SRC, _, S_X3DST, S_OUT, S_EDGE = range(7)


def node_tiles(m):
    return range(1 if isinstance(m, int) and 2 * m + 1 >= TILES else 2)


def dense_and_prep(nc, sem, x_t, w, avec, h_out, al_out, ends_row, ends_col, ew_col, rec_d, rec_s, row_d, row_s,
                   map_d, map_s, tab_d, tab_s, attr_t, fw1, fb1, fw2b, attr4_col, u_tab):
    KC = w.shape[0] // P
    G = 2 * P
    MACROS = LOOPED // G
    PASSES = MACROS // 2
    R, F = attr_t.shape[0], fw1.shape[1]
    CH = 512
    CHUNKS = EP // CH
    PER = 4
    RANKED = ET // PER
    GROUPS = ET // PER
    with ExitStack() as ctx:
        sb = lambda n, s, d=F32: ctx.enter_context(nc.sbuf_tensor(f"g1_{n}", s, d))
        ps = lambda n, s: ctx.enter_context(nc.psum_tensor(f"g1_{n}", s, F32))
        w_raw = sb("w_raw", [P, 2, HC])
        w_hi = sb("w_hi", [P, KC, HC], F32R)
        w_lo = sb("w_lo", [P, KC, HC], F32R)
        a_rows = sb("a_rows", [P, 2, HC])
        x_in = [sb(f"x_in{s}", [P, KC, G]) for s in range(2)]
        x_hi = [sb(f"x_hi{s}", [P, KC, G], F32R) for s in range(2)]
        x_lo = [sb(f"x_lo{s}", [P, KC, G], F32R) for s in range(2)]
        h_sb = [sb(f"h_sb{s}", [P, HC]) for s in range(4)]
        al_sb = [sb(f"al_sb{s}", [P, 2, 2 * H]) for s in range(2)]
        prod = [sb(f"prod{s}", [P, C]) for s in range(2)]
        row = [sb(f"row{o}", [P, EP]) for o in range(2)]
        signs = [sb(f"signs{q}", [P, EP]) for q in range(2)]
        tile_row, int_row = (buffer[:, :].bitcast(I32) for buffer in signs)
        ties = sb("ties", [P, 2 * PER, P])
        int_col = sb("int_col", [P, 2, ET], I32)
        tile_col = sb("tile_col", [P, ET], I32)
        node = sb("node", [P, 2, ET])
        col = sb("col", [P, 2, ET])
        neg = sb("neg", [P, 2, ET])
        lower = sb("lower", [P, P])
        later = sb("later", [P, 2, ET])
        tied = sb("tied", [P, 2, ET])
        before = sb("before", [P, 2, ET])
        rank = sb("rank", [P, 2, ET])
        rank_i = sb("rank_i", [P, 2, ET], I32)
        weight = sb("weight", [P, ET])
        rec = [sb(f"rec{o}", [P, ET, REC]) for o in range(2)]
        srt = [sb(f"srt{o}", [P, ET, REC]) for o in range(2)]
        nxt = [sb(f"nxt{o}", [P, ET, REC]) for o in range(2)]
        ends = sb("ends", [1, 2, REC])
        zero = sb("zero", [P, NT // P])
        r_i = sb("r_i", [P, ET], I32)
        r_f = sb("r_f", [P, ET])
        dump = sb("dump", [P, ET])
        r1 = sb("r1", [P, ET])
        r_next = sb("r_next", [P, ET], I32)
        is_last = sb("is_last", [P, 2, ET])
        off = sb("off", [P, 2, ET])
        cut = sb("cut", [P, 2, ET])
        where = sb("where", [P, 2, ET])
        scat_i = sb("scat_i", [P, 2, ET], I32)
        node_i = sb("node_i", [P, 2, 2, ET], I32)
        found = sb("found", [P, ET, 4])
        has = sb("has", [P, 2, ET])
        alt = sb("alt", [P, 2, ET])
        diff = sb("diff", [P, 2, ET])
        gap = sb("gap", [P, 2, ET])
        pick = sb("pick", [P, 2, ET])
        out_d = sb("out_d", [P, ET, TAB])
        out_s = sb("out_s", [P, ET, TAB])
        attr = sb("attr", [R, EP])
        fw1_sb = sb("fw1_sb", [R, F])
        fb1_sb = sb("fb1_sb", [F, 1])
        fw2_sb = sb("fw2_sb", [F + 1, 4 * F])
        y = sb("y", [P, ET, 4])
        half = sb("half", [F, 1])
        pre = sb("pre", [F, EP])
        mag = sb("mag", [F, EP])
        hid = sb("hid", [F + 1, EP])
        yr = sb("yr", [P, 7, ET])
        u = [sb(f"u{s}", [P, PER, 8 * F]) for s in range(2)]
        h_ps = [ps(f"h_ps{s}", [P, HC]) for s in range(2)]
        f_ps = [ps(f"f_ps{s}", [P, PER, 4 * F]) for s in range(4)]

        w_in = [sem(f"g1_w_in{s}") for s in range(2)]
        a_in = sem("g1_a_in")
        x_loaded = [sem(f"g1_x_loaded{s}") for s in range(2)]
        h_stored = [sem(f"g1_h_stored{s}") for s in range(4)]
        al_stored = [sem(f"g1_al_stored{s}") for s in range(2)]
        w_hi_done = sem("g1_w_hi_done")
        w_lo_done = sem("g1_w_lo_done")
        hi_done = sem("g1_hi_done")
        lo_done = sem("g1_lo_done")
        tile_done = sem("g1_tile_done")
        evac_done = sem("g1_evac_done")
        al_done = sem("g1_al_done")
        passed = sem("g1_passed")
        cols_in = sem("prep_cols_in")
        rows_in = [sem(f"prep_rows_in{o}") for o in range(2)]
        row_done = [sem(f"prep_row_done{o}") for o in range(2)]
        zeroed = sem("prep_zeroed")
        const_done = sem("prep_const_done")
        lower_set = sem("prep_lower_set")
        v = sem("prep_v")
        signed = sem("prep_signed")
        tied_done = sem("prep_tied_done")
        ranked = sem("prep_ranked")
        scattered = [sem(f"prep_scattered{o}") for o in range(2)]
        sorted_in = sem("prep_sorted_in")
        rows_out = sem("prep_rows_out")
        scat_done = sem("prep_scat_done")
        mapped = sem("prep_mapped")
        looked = sem("prep_looked")
        tabs_done = sem("prep_tabs_done")
        tabs_out = sem("prep_tabs_out")
        f_loaded = sem("filt_loaded")
        f_multiplied = sem("filt_multiplied")
        pre_out = sem("filt_pre_out")
        soft_steps = sem("filt_soft_steps")
        hid_done = sem("filt_hid_done")
        f_done = sem("filt_f_done")
        u_done = sem("filt_u_done")
        u_stored = [sem(f"filt_u_stored{s}") for s in range(2)]

        CONST = 6

        def first(i):
            return isinstance(i, int) and i == 0

        with nc.Block() as block:

            @block.sync
            def _(sp):
                def load(m, s):
                    sp.dma_start(x_in[s][:, :, :],
                                 x_t[:, bass.ds(m * G, G)].rearrange("(c p) n -> p c n", p=P)).then_inc(x_loaded[s], 16)

                def store(m, s):
                    for j in node_tiles(m):
                        sp.wait_ge(evac_done, 2 + 2 * m + j + 1)
                        sp.sem_inc(passed, 1)
                        sp.dma_start(h_out[bass.ds(m * G + j * P, P), :], h_sb[2 * s + j][:, :]).then_inc(h_stored[2 * s + j], 16)
                    n = len(node_tiles(m))
                    sp.wait_ge(al_done, 32 + 16 * m + 8 * n)
                    sp.sem_inc(passed, 1)
                    sp.dma_start(al_out[bass.ds(m * G, n * P), :].rearrange("(j p) k -> p j k", p=P),
                                 al_sb[s][:, 0:n, :]).then_inc(al_stored[s], 16)

                def loop(start, stop):
                    with sp.Fori(start, stop) as i:
                        for s in range(2):
                            m = 2 * i + s
                            sp.wait_ge(lo_done, m + 1)
                            sp.sem_inc(passed, 1)
                            load(m + 2, s)
                            store(m, s)

                load(0, 0)
                for k in range(2):
                    sp.dma_start(w_raw[:, k, :], w[k * P:(k + 1) * P, :]).then_inc(w_in[k], 16)
                load(1, 1)
                for k in range(2, KC):
                    sp.wait_ge(w_lo_done, k - 1)
                    sp.dma_start(w_raw[:, k % 2, :], w[k * P:(k + 1) * P, :]).then_inc(w_in[k % 2], 16)
                sp.dma_start(a_rows[:, :, :], avec.partition_broadcast(P)).then_inc(a_in, 16)
                loop(0, 9)
                for o, (rec_in, row_out) in enumerate(((rec_d, row_d), (rec_s, row_s))):
                    sp.wait_ge(scattered[o], 16 * ET)
                    sp.dma_start(srt[o][:, :, :], rec_in[0:EP].rearrange("(t p) k -> p t k", p=P)).then_inc(sorted_in, 16)
                    sp.dma_start(nxt[o][:, :, :], rec_in[1:EP + 1].rearrange("(t p) k -> p t k", p=P)).then_inc(sorted_in, 16)
                    sp.dma_start(row_out[1:EP + 1], rec_in[0:EP, 0:1].rearrange("a b -> (a b)"),
                                 allow_slow_non_contiguous=True).then_inc(rows_out, 16)
                loop(9, PASSES - 1)
                for s in range(2):
                    store(MACROS - 2 + s, s)
                for s in range(4):
                    sp.wait_ge(h_stored[s], 16 * len(range(s, TILES, 4)))
                for s in range(2):
                    sp.wait_ge(al_stored[s], 16 * PASSES)
                sp.wait_ge(rows_out, 32)

            @block.gpsimd
            def _(pool):
                pool.dma_start(int_col[:, :, :], ends_col).then_inc(cols_in, 16)
                pool.dma_start(weight[:, :], ew_col).then_inc(cols_in, 16)
                pool.dma_start(int_row, ends_row[0].partition_broadcast(P)).then_inc(rows_in[0], 16)
                pool.iota(tile_row, [[1, ET], [0, P]], base=0, channel_multiplier=0).then_inc(const_done, 1)
                pool.iota(tile_col[:, :], [[1, ET]], base=0, channel_multiplier=0).then_inc(const_done, 1)
                pool.memset(zero[:, :], 0.0).then_inc(const_done, 1)
                pool.iota(r_i[:, :], [[P, ET]], base=0, channel_multiplier=1).then_inc(const_done, 1)
                pool.iota(r_next[:, :], [[P, ET]], base=NP, channel_multiplier=1).then_inc(const_done, 1)
                pool.memset(lower[:, :], 1.0).then_inc(lower_set, 1)
                pool.wait_ge(lower_set, 1)
                pool.affine_select(out=lower[:, :], in_=lower[:, :], compare_op=ALU.is_gt, fill=0.0,
                                   base=0, pattern=[[-1, P]], channel_multiplier=1).then_inc(const_done, 1)
                pool.wait_ge(row_done[0], 1)
                pool.dma_start(int_row, ends_row[1].partition_broadcast(P)).then_inc(rows_in[1], 16)
                pool.dma_start(attr[:, :], attr_t).then_inc(f_loaded, 16)
                pool.dma_start(fw1_sb[:, :], fw1).then_inc(f_loaded, 16)
                pool.dma_start(fb1_sb[:, :], fb1).then_inc(f_loaded, 16)
                pool.dma_start(fw2_sb[:, :], fw2b[:, 0:4 * F]).then_inc(f_loaded, 16)
                pool.dma_start(y[:, :, :], attr4_col).then_inc(f_loaded, 16)
                pool.wait_ge(const_done, CONST)
                pool.wait_ge(v, 1)
                for map_out in (map_d, map_s):
                    pool.dma_start(map_out.rearrange("(p k) o -> p (k o)", p=P), zero[:, :]).then_inc(zeroed, 16)
                for row_out, rec_out in ((row_d, rec_d), (row_s, rec_s)):
                    pool.dma_start(row_out[0:1].rearrange("(a b) -> a b", a=1), ends[0:1, 0, 0:1]).then_inc(zeroed, 16)
                    pool.dma_start(row_out[EP + 1:EP + 2].rearrange("(a b) -> a b", a=1), ends[0:1, 1, 0:1]).then_inc(zeroed, 16)
                    pool.dma_start(rec_out[EP:EP + 1, :], ends[0:1, 1, :]).then_inc(zeroed, 16)
                pool.wait_ge(zeroed, 16 * 8)
                pool.wait_ge(ranked, 2)
                for o, rec_out in enumerate((rec_d, rec_s)):
                    for t in range(ET):
                        pool.indirect_dma_start(rec_out, bass.IndirectOffsetOnAxis(rank_i[:, o, t:t + 1], 0),
                                                rec[o][:, t, :], None).then_inc(scattered[o], 16)
                pool.wait_ge(scat_done, 1)
                for o, map_out in enumerate((map_d, map_s)):
                    for t in range(ET):
                        pool.indirect_dma_start(map_out, bass.IndirectOffsetOnAxis(scat_i[:, o, t:t + 1], 0),
                                                r1[:, t:t + 1], None).then_inc(mapped, 16)
                pool.wait_ge(mapped, 32 * ET)
                for n, (map_in, end) in enumerate(((map_d, 1), (map_d, 0), (map_s, 0), (map_s, 1))):
                    for t in range(ET):
                        pool.indirect_dma_start(
                            found[:, t, n:n + 1], None, map_in,
                            bass.IndirectOffsetOnAxis(node_i[:, 1, end, t:t + 1], 0)).then_inc(looked, 16)
                for g in range(GROUPS):
                    pool.wait_ge(u_done, g + 1)
                    pool.dma_start(u_tab[g * PER * P:(g + 1) * PER * P].rearrange("(t p) k -> p t k", p=P),
                                   u[g % 2][:, :, :]).then_inc(u_stored[g % 2], 16)
                pool.wait_ge(tabs_done, 1)
                pool.dma_start(tab_d.rearrange("(t p) k -> p t k", p=P), out_d[:, :, :]).then_inc(tabs_out, 16)
                pool.dma_start(tab_s.rearrange("(t p) k -> p t k", p=P), out_s[:, :, :]).then_inc(tabs_out, 16)
                pool.wait_ge(tabs_out, 32)
                for s in range(2):
                    pool.wait_ge(u_stored[s], 16 * len(range(s, GROUPS, 2)))

            @block.tensor
            def _(pe):
                pe.sem_inc(tile_done, 4)

                def first_products():
                    pe.wait_ge(lo_done, 1)
                    for k in range(KC):
                        pe.wait_ge(w_lo_done, k + 1)
                        for j in range(2):
                            xh = x_hi[0][:, k, j * P:(j + 1) * P]
                            xl = x_lo[0][:, k, j * P:(j + 1) * P]
                            for n in range(2):
                                cols = slice(n * 512, (n + 1) * 512)
                                out = h_ps[j][:, cols]
                                pe.matmul(out, xh, w_hi[:, k, cols], start=(k == 0), stop=False)
                                pe.matmul(out, xh, w_lo[:, k, cols], start=False, stop=False)
                                last = pe.matmul(out, xl, w_hi[:, k, cols], start=False, stop=(k == KC - 1))
                            if k == KC - 1:
                                last.then_inc(tile_done, 1)

                def products(m, i, s):
                    pe.wait_ge(lo_done, m + 1)
                    for j in node_tiles(m):
                        pe.wait_ge(evac_done, 2 * m + j + 1)
                        for n in range(2):
                            out = h_ps[j][:, n * 512:(n + 1) * 512]
                            for k in range(KC):
                                xh = x_hi[s][:, k, j * P:(j + 1) * P]
                                xl = x_lo[s][:, k, j * P:(j + 1) * P]
                                wh = w_hi[:, k, n * 512:(n + 1) * 512]
                                wl = w_lo[:, k, n * 512:(n + 1) * 512]
                                pe.matmul(out, xh, wh, start=(k == 0), stop=False)
                                pe.matmul(out, xh, wl, start=False, stop=False)
                                last = pe.matmul(out, xl, wh, start=False, stop=(k == KC - 1))
                        last.then_inc(tile_done, 1)

                def body(i):
                    for s in range(2):
                        products(2 * i + s, i, s)

                def loop(start, stop):
                    with pe.Fori(start, stop) as i:
                        body(i)

                def hidden(n):
                    if n >= 4:
                        pe.wait_ge(pre_out, n - 3)
                    pe.matmul(f_ps[n % 4][0:F, :, :], fw1_sb[:, :], attr[:, n * CH:(n + 1) * CH],
                              start=True, stop=True).then_inc(f_multiplied, 1)

                def factors(g):
                    if g >= 4:
                        pe.wait_ge(u_done, g - 3)
                    for t in range(PER):
                        e = (PER * g + t) * P
                        last = pe.matmul(f_ps[g % 4][:, t, :], hid[:, e:e + P], fw2_sb[:, :], start=True, stop=True)
                    last.then_inc(f_done, 1)

                first_products()
                products(1, 0, 1)
                loop(1, RANKED)
                pe.wait_ge(f_loaded, 80)
                for n in range(4):
                    hidden(n)
                body(RANKED)
                for n in range(4, CHUNKS):
                    hidden(n)
                loop(RANKED + 1, RANKED + 3)
                pe.wait_ge(hid_done, 2)
                for g in range(4):
                    factors(g)
                loop(RANKED + 3, RANKED + 6)
                for g in range(4, GROUPS):
                    factors(g)
                loop(RANKED + 6, PASSES - 1)
                body(PASSES - 1)

            @block.scalar
            def _(act):
                act.sem_inc(evac_done, 2)
                n_signs = 0

                def evac(m, i, s, j):
                    act.wait_ge(tile_done, 4 + 2 * m + j + 1)
                    if not first(i):
                        act.wait_ge(h_stored[2 * s + j], 16 * i)
                    act.wait_ge(al_done, 8 * (2 * m + j + 1))
                    act.activation(h_sb[2 * s + j][:, :], h_ps[j][:, :], ACT.Copy).then_inc(evac_done, 1)

                def count(i, n):
                    o, t = n % 2, PER * i + n // 2
                    if first(i) and n < 2:
                        act.wait_ge(row_done[0], 1)
                        act.wait_ge(row_done[1], 1)
                    else:
                        act.wait_ge(signed, 2 * PER * i + n - 1)
                    act.activation(signs[n % 2][:, :], row[o][:, :], ACT.Sign, bias=neg[:, o, bass.ds(t, 1)],
                                   accum_out=later[:, o, bass.ds(t, 1)]).then_inc(signed, 1)

                def body(i, ranking):
                    for s in range(2):
                        for j in node_tiles(2 * i + s):
                            evac(2 * i + s, i, s, j)
                            if ranking:
                                count(i, 4 * s + 2 * j)
                                count(i, 4 * s + 2 * j + 1)

                def copy_hidden(n):
                    act.wait_ge(f_multiplied, n + 1)
                    act.activation(pre[:, n * CH:(n + 1) * CH], f_ps[n % 4][0:F, :, :].rearrange("f t k -> f (t k)"),
                                   ACT.Identity, bias=fb1_sb[:, 0:1]).then_inc(pre_out, 1)

                body(0, True)
                with act.Fori(1, RANKED) as i:
                    body(i, True)
                act.wait_ge(f_loaded, 80)
                for n in range(4):
                    copy_hidden(n)
                body(RANKED, False)
                for n in range(4, CHUNKS):
                    copy_hidden(n)
                act.wait_ge(pre_out, CHUNKS)
                act.activation(mag[:, :], pre[:, :], ACT.Abs).then_inc(soft_steps, 1)
                body(RANKED + 1, False)
                act.wait_ge(soft_steps, 1)
                act.activation(mag[:, :], mag[:, :], ACT.Exp, scale=-1.0).then_inc(soft_steps, 1)
                act.wait_ge(soft_steps, 2)
                act.activation(mag[:, :], mag[:, :], ACT.Ln, bias=half[:, 0:1], scale=0.5).then_inc(soft_steps, 1)
                with act.Fori(RANKED + 2, PASSES - 1) as i:
                    body(i, False)
                body(PASSES - 1, False)

            @block.vector
            def _(dve):
                steps = 0

                def step(ins):
                    nonlocal steps
                    ins.then_inc(v, 1)
                    steps += 1

                def settle():
                    dve.wait_ge(v, steps)

                def split_w(k):
                    dve.wait_ge(w_in[k % 2], 16 * (k // 2 + 1))
                    dve.tensor_copy(w_hi[:, k, :], w_raw[:, k % 2, :]).then_inc(w_hi_done, 1)
                    dve.wait_ge(w_hi_done, k + 1)
                    dve.tensor_tensor(w_lo[:, k, :], w_raw[:, k % 2, :], w_hi[:, k, :].bitcast(F32),
                                      ALU.subtract).then_inc(w_lo_done, 1)

                def splits(m, i, s):
                    dve.wait_ge(tile_done, 2 * m + 2)
                    dve.wait_ge(x_loaded[s], 16 * (i + 1))
                    dve.tensor_copy(x_hi[s][:, :, :], x_in[s][:, :, :]).then_inc(hi_done, 1)
                    dve.wait_ge(hi_done, m + 1)
                    dve.tensor_tensor(x_lo[s][:, :, :], x_in[s][:, :, :], x_hi[s][:, :, :].bitcast(F32),
                                      ALU.subtract).then_inc(lo_done, 1)

                def attention(m, i, s):
                    if not first(i):
                        dve.wait_ge(al_stored[s], 16 * i)
                    for j in node_tiles(m):
                        dve.wait_ge(evac_done, 2 + 2 * m + j + 1)
                        for a in range(2):
                            for hd in range(H):
                                cols = slice(hd * C, (hd + 1) * C)
                                dve.wait_ge(al_done, 32 + 16 * m + 8 * j + 4 * a + hd - 1)
                                dve.tensor_tensor_reduce(
                                    prod[hd % 2][:, :], h_sb[2 * s + j][:, cols], a_rows[:, a, cols], 1.0, 0.0,
                                    ALU.mult, ALU.add, al_sb[s][:, j, a * H + hd:a * H + hd + 1]).then_inc(al_done, 1)

                def tie(i):
                    if not first(i):
                        dve.wait_ge(tied_done, 2 * PER * i)
                    for n in range(2 * PER):
                        o, t = n % 2, PER * i + n // 2
                        dve.scalar_tensor_tensor(ties[:, n, :], row[o][:, bass.ds(t * P, P)], col[:, o, bass.ds(t, 1)],
                                                 lower[:, :], ALU.is_equal, ALU.mult,
                                                 accum_out=tied[:, o, bass.ds(t, 1)]).then_inc(tied_done, 1)

                def body(i, ranking=False, last=False):
                    if ranking:
                        tie(i)
                    splits(2 * i + 1, i, 1)
                    attention(2 * i, i, 0)
                    if not last:
                        splits(2 * i + 2, i + 1, 0)
                    attention(2 * i + 1, i, 1)

                def loop(start, stop, ranking=False):
                    with dve.Fori(start, stop) as i:
                        body(i, ranking)

                dve.sem_inc(al_done, 32)
                dve.memset(ends[:, 0, :], -1.0)
                dve.memset(half[:, :], 0.5)
                dve.memset(hid[F:F + 1, :], 1.0)
                step(dve.memset(ends[:, 1, :], -2.0))
                splits(0, 0, 0)
                for k in range(2):
                    split_w(k)
                dve.wait_ge(const_done, CONST)
                dve.wait_ge(cols_in, 32)
                for o in range(2):
                    step(dve.scalar_tensor_tensor(col[:, o, :], int_col[:, o, :], float(ET), tile_col[:, :],
                                                  ALU.mult, ALU.add))
                settle()
                step(dve.tensor_scalar(neg[:, :, :], col[:, :, :], -1.0, 0.5, ALU.mult, ALU.add))
                for k in range(2, KC):
                    split_w(k)
                settle()
                for o in range(2):
                    dve.wait_ge(rows_in[o], 16)
                    dve.scalar_tensor_tensor(row[o][:, :], int_row, float(ET), tile_row,
                                             ALU.mult, ALU.add).then_inc(row_done[o], 1)
                step(dve.tensor_copy(node[:, :, :], int_col[:, :, :]))
                for o in range(2):
                    step(dve.memset(rec[o][:, :, :], 0.0))
                step(dve.tensor_copy(r_f[:, :], r_i[:, :]))
                step(dve.tensor_copy(dump[:, :], r_next[:, :]))
                dve.wait_ge(a_in, 16)
                dve.wait_ge(row_done[0], 1)
                dve.wait_ge(row_done[1], 1)
                body(0, True)
                loop(1, RANKED, True)

                dve.wait_ge(signed, 2 * ET)
                dve.wait_ge(tied_done, 2 * ET)
                settle()
                step(dve.tensor_scalar(before[:, :, :], later[:, :, :], -0.5, EP / 2, ALU.mult, ALU.add))
                step(dve.tensor_scalar(r1[:, :], r_f[:, :], 1.0, None, ALU.add))
                settle()
                step(dve.tensor_tensor(rank[:, :, :], before[:, :, :], tied[:, :, :], ALU.add))
                settle()
                for o in range(2):
                    dve.tensor_copy(rec[o][:, :, 0], node[:, o, :])
                    dve.tensor_copy(rec[o][:, :, 1], node[:, 1 - o, :])
                    dve.tensor_copy(rec[o][:, :, 2], rank[:, 0, :])
                    dve.tensor_copy(rec[o][:, :, 3], r_f[:, :])
                    dve.tensor_copy(rec[o][:, :, 4], weight[:, :])
                dve.tensor_copy(rank_i[:, :, :], rank[:, :, :]).then_inc(ranked, 2)
                loop(RANKED, RANKED + 2)

                dve.wait_ge(f_loaded, 80)
                for c in range(4):
                    step(dve.tensor_tensor(yr[:, c, :], y[:, :, c], weight[:, :], ALU.mult))
                settle()
                step(dve.tensor_scalar(yr[:, 4:7, :], yr[:, 1:4, :], 3 ** -0.5, None, ALU.mult))
                dve.wait_ge(soft_steps, 3)
                dve.scalar_tensor_tensor(hid[0:F, :], pre[:, :], 0.0, mag[:, :], ALU.max, ALU.add).then_inc(hid_done, 2)
                loop(RANKED + 2, RANKED + 5)

                def use_factors(g):
                    dve.wait_ge(f_done, g + 1)
                    if g >= 2:
                        dve.wait_ge(u_stored[g % 2], 16 * (g // 2))
                    for n, (k, c) in enumerate(((0, 0), (1, 4), (1, 5), (1, 6), (2, 1), (2, 2), (2, 3), (3, 0))):
                        scale = yr[:, c, g * PER:(g + 1) * PER].rearrange("p (t a) -> p t a", a=1)
                        last = dve.tensor_tensor(u[g % 2][:, :, n * F:(n + 1) * F], f_ps[g % 4][:, :, k * F:(k + 1) * F],
                                                 scale.to_broadcast([P, PER, F]), ALU.mult)
                    last.then_inc(u_done, 1)

                dve.wait_ge(sorted_in, 64)
                settle()
                for o in range(2):
                    key = srt[o][:, :, 0]
                    step(dve.tensor_tensor(is_last[:, o, :], key, nxt[o][:, :, 0], ALU.not_equal))
                    step(dve.tensor_tensor(off[:, o, :], key, dump[:, :], ALU.subtract))
                settle()
                step(dve.tensor_tensor(cut[:, :, :], off[:, :, :], is_last[:, :, :], ALU.mult))
                settle()
                for o in range(2):
                    step(dve.tensor_tensor(where[:, o, :], cut[:, o, :], dump[:, :], ALU.add))
                settle()
                for o in range(2):
                    for end in range(2):
                        step(dve.tensor_copy(node_i[:, o, end, :], srt[o][:, :, end]))
                step(dve.tensor_copy(scat_i[:, :, :], where[:, :, :]))
                settle()
                dve.memset(out_d[:, :, :], 0.0)
                step(dve.memset(out_s[:, :, :], 0.0))
                settle()
                dve.sem_inc(scat_done, 1)
                for g in range(2):
                    use_factors(g)
                loop(RANKED + 5, PASSES - 3)
                for n, g in enumerate(range(2, GROUPS)):
                    use_factors(g)
                    body(PASSES - 3 + n, last=(n == 2))

                dve.wait_ge(looked, 16 * 4 * ET)
                f = [found[:, :, n] for n in range(4)]
                for n, (m, own) in enumerate(((f[1], srt[1][:, :, 2]), (f[3], r_f[:, :]))):
                    step(dve.tensor_scalar(has[:, n, :], m, 0.5, None, ALU.is_ge))
                    step(dve.tensor_scalar(alt[:, n, :], own, float(EP), None, ALU.add))
                settle()
                for n, m in enumerate((f[1], f[3])):
                    step(dve.scalar_tensor_tensor(diff[:, n, :], m, -1.0, alt[:, n, :], ALU.add, ALU.subtract))
                settle()
                step(dve.tensor_tensor(gap[:, :, :], diff[:, :, :], has[:, :, :], ALU.mult))
                settle()
                step(dve.tensor_tensor(pick[:, :, :], gap[:, :, :], alt[:, :, :], ALU.add))
                settle()
                di, si = out_d[:, :, :].bitcast(I32), out_s[:, :, :].bitcast(I32)
                dve.tensor_copy(di[:, :, D_SRC], node_i[:, 0, 1, :])
                dve.tensor_copy(di[:, :, D_DST], node_i[:, 0, 0, :])
                dve.tensor_copy(di[:, :, D_OUT], scat_i[:, 0, :])
                dve.tensor_copy(out_d[:, :, KEY], srt[0][:, :, 0])
                dve.tensor_copy(out_d[:, :, D_EW], srt[0][:, :, 4])
                dve.tensor_scalar(si[:, :, S_X2DST], f[0], -1.0, None, ALU.add)
                dve.tensor_copy(si[:, :, S_X2SRC], pick[:, 0, :])
                dve.tensor_scalar(si[:, :, S_X3SRC], f[2], -1.0, None, ALU.add)
                dve.tensor_copy(out_s[:, :, KEY], srt[1][:, :, 0])
                dve.tensor_copy(si[:, :, S_X3DST], pick[:, 1, :])
                dve.tensor_copy(si[:, :, S_OUT], scat_i[:, 1, :])
                dve.tensor_copy(si[:, :, S_EDGE], srt[1][:, :, 3]).then_inc(tabs_done, 1)


def gat_dense(nc, sem, src, w, bias, avec, h_out, al_out):
    K = w.shape[0]
    KC = K // P
    G = 2 * P
    MACROS = LOOPED // G
    FILLS = KC // 2
    with ExitStack() as ctx:
        sb = lambda n, s, d=F32: ctx.enter_context(nc.sbuf_tensor(f"g2_{n}", s, d))
        ps = lambda n, s: ctx.enter_context(nc.psum_tensor(f"g2_{n}", s, F32))
        w_raw = sb("w_raw", [P, 2, HC])
        w_hi = sb("w_hi", [P, KC, HC], F32R)
        w_lo = sb("w_lo", [P, KC, HC], F32R)
        a_rows = sb("a_rows", [P, 2, HC])
        x_in = [sb(f"x_in{s}", [P, 2, K]) for s in range(2)]
        act_t = [sb(f"act_t{s}", [P, KC, G]) for s in range(2)]
        x_hi = [sb(f"x_hi{s}", [P, KC, G], F32R) for s in range(2)]
        x_lo = [sb(f"x_lo{s}", [P, KC, G], F32R) for s in range(2)]
        h_sb = [sb(f"h_sb{s}", [P, HC]) for s in range(4)]
        al_sb = [sb(f"al_sb{s}", [P, 2, 2 * H]) for s in range(2)]
        prod = [sb(f"prod{s}", [P, C]) for s in range(2)]
        h_ps = [ps(f"h_ps{s}", [P, HC]) for s in range(2)]
        ident = sb("ident", [P, P])
        b_col = sb("b_col", [P, KC])
        t_ps = [ps(f"t_ps{s}", [P, 2, G]) for s in range(FILLS)]

        w_in = [sem(f"g2_w_in{s}") for s in range(2)]
        a_in = sem("g2_a_in")
        b_in = sem("g2_b_in")
        x_loaded = [sem(f"g2_x_loaded{s}") for s in range(2)]
        h_stored = [sem(f"g2_h_stored{s}") for s in range(4)]
        al_stored = [sem(f"g2_al_stored{s}") for s in range(2)]
        w_hi_done = sem("g2_w_hi_done")
        w_lo_done = sem("g2_w_lo_done")
        hi_done = sem("g2_hi_done")
        lo_done = sem("g2_lo_done")
        filled = sem("g2_filled")
        relu_done = sem("g2_relu_done")
        tile_done = sem("g2_tile_done")
        evac_done = sem("g2_evac_done")
        al_done = sem("g2_al_done")
        ident_done = sem("g2_ident_done")

        def rows(ap, m):
            return ap[bass.ds(m * G, len(node_tiles(m)) * P), :].rearrange("(j p) k -> p j k", p=P)

        def first(i):
            return isinstance(i, int) and i == 0

        with nc.Block() as block:

            @block.sync
            def _(sp):
                sp.dma_start(b_col[:, :], bias).then_inc(b_in, 16)
                sp.dma_start(x_in[0][:, :, :], rows(src, 0)).then_inc(x_loaded[0], 16)
                for k in range(KC):
                    if k >= 2:
                        sp.wait_ge(w_lo_done, k - 1)
                    sp.dma_start(w_raw[:, k % 2, :], w[k * P:(k + 1) * P, :]).then_inc(w_in[k % 2], 16)
                sp.dma_start(x_in[1][:, :, :], rows(src, 1)).then_inc(x_loaded[1], 16)
                sp.dma_start(a_rows[:, :, :], avec.partition_broadcast(P)).then_inc(a_in, 16)

                def body(i):
                    for s in range(2):
                        m = 2 * i + s
                        sp.wait_ge(filled, FILLS * (m + 1))
                        sp.dma_start(x_in[s][:, 0:len(node_tiles(m + 2)), :], rows(src, m + 2)).then_inc(x_loaded[s], 16)

                with sp.Fori(0, MACROS // 2 - 2) as i:
                    body(i)
                body(MACROS // 2 - 2)

            @block.gpsimd
            def _(pool):
                pool.memset(ident[:, :], 0.0).then_inc(ident_done, 1)
                pool.wait_ge(ident_done, 1)
                pool.affine_select(out=ident[:, :], in_=ident[:, :], compare_op=ALU.not_equal, fill=1.0,
                                   base=0, pattern=[[-1, P]], channel_multiplier=1).then_inc(ident_done, 1)

                def body(i):
                    for s in range(2):
                        m = 2 * i + s
                        n = len(node_tiles(m))
                        for j in range(n):
                            pool.wait_ge(evac_done, 2 + 2 * m + j + 1)
                            pool.dma_start(h_out[bass.ds(m * G + j * P, P), :],
                                           h_sb[2 * s + j][:, :]).then_inc(h_stored[2 * s + j], 16)
                        pool.wait_ge(al_done, 32 + 16 * m + 8 * n)
                        pool.dma_start(rows(al_out, m), al_sb[s][:, 0:n, :]).then_inc(al_stored[s], 16)

                with pool.Fori(0, MACROS // 2 - 1) as i:
                    body(i)
                body(MACROS // 2 - 1)
                for s in range(4):
                    pool.wait_ge(h_stored[s], 16 * len(range(s, TILES, 4)))
                for s in range(2):
                    pool.wait_ge(al_stored[s], 16 * (MACROS // 2))

            @block.tensor
            def _(pe):
                pe.sem_inc(tile_done, 4)
                pe.wait_ge(ident_done, 2)

                def transposes(m, i, s):
                    pe.wait_ge(x_loaded[s], 16 * (i + 1))
                    for f in range(FILLS):
                        pe.wait_ge(relu_done, FILLS * m + f + 1)
                        for c in range(2):
                            for j in node_tiles(m):
                                k = 2 * f + c
                                last = pe.transpose(t_ps[f][:, c, j * P:(j + 1) * P],
                                                    x_in[s][:, j, k * P:(k + 1) * P], ident[:, :])
                        last.then_inc(filled, 1)

                def first_products():
                    pe.wait_ge(lo_done, FILLS)
                    for k in range(KC):
                        pe.wait_ge(w_lo_done, k + 1)
                        for j in range(2):
                            xh = x_hi[0][:, k, j * P:(j + 1) * P]
                            xl = x_lo[0][:, k, j * P:(j + 1) * P]
                            for n in range(2):
                                cols = slice(n * 512, (n + 1) * 512)
                                out = h_ps[j][:, cols]
                                pe.matmul(out, xh, w_hi[:, k, cols], start=(k == 0), stop=False)
                                pe.matmul(out, xh, w_lo[:, k, cols], start=False, stop=False)
                                last = pe.matmul(out, xl, w_hi[:, k, cols], start=False, stop=(k == KC - 1))
                            if k == KC - 1:
                                last.then_inc(tile_done, 1)

                def products(m, s, tiles):
                    pe.wait_ge(lo_done, FILLS * (m + 1))
                    for j in tiles:
                        pe.wait_ge(evac_done, 2 * m + j + 1)
                        for n in range(2):
                            out = h_ps[j][:, n * 512:(n + 1) * 512]
                            for k in range(KC):
                                xh = x_hi[s][:, k, j * P:(j + 1) * P]
                                xl = x_lo[s][:, k, j * P:(j + 1) * P]
                                wh = w_hi[:, k, n * 512:(n + 1) * 512]
                                wl = w_lo[:, k, n * 512:(n + 1) * 512]
                                pe.matmul(out, xh, wh, start=(k == 0), stop=False)
                                pe.matmul(out, xh, wl, start=False, stop=False)
                                last = pe.matmul(out, xl, wh, start=False, stop=(k == KC - 1))
                        last.then_inc(tile_done, 1)

                def body(i, last):
                    if first(i):
                        transposes(0, 0, 0)
                        first_products()
                        transposes(1, 0, 1)
                    else:
                        products(2 * i, 0, [0])
                        transposes(2 * i + 1, i, 1)
                        products(2 * i, 0, [1])
                    products(2 * i + 1, 1, [0])
                    if not last:
                        transposes(2 * i + 2, i + 1, 0)
                    if len(node_tiles(2 * i + 1)) == 2:
                        products(2 * i + 1, 1, [1])

                body(0, False)
                with pe.Fori(1, MACROS // 2 - 1) as i:
                    body(i, False)
                body(MACROS // 2 - 1, True)

            @block.scalar
            def _(act):
                act.sem_inc(evac_done, 2)
                act.sem_inc(relu_done, FILLS)
                act.wait_ge(b_in, 16)

                def relus(m, i, s):
                    width = P * len(node_tiles(m))
                    for f in range(FILLS):
                        act.wait_ge(filled, FILLS * m + f + 1)
                        for c in range(2):
                            k = 2 * f + c
                            last = act.activation(act_t[s][:, k, 0:width], t_ps[f][:, c, 0:width], ACT.Relu,
                                                  bias=b_col[:, k:k + 1])
                        last.then_inc(relu_done, 1)

                def evacs(m, i, s):
                    for j in node_tiles(m):
                        act.wait_ge(tile_done, 4 + 2 * m + j + 1)
                        if not first(i):
                            act.wait_ge(h_stored[2 * s + j], 16 * i)
                        act.wait_ge(al_done, 8 * (2 * m + j + 1))
                        act.activation(h_sb[2 * s + j][:, :], h_ps[j][:, :], ACT.Copy).then_inc(evac_done, 1)

                relus(0, 0, 0)

                def body(i, last):
                    relus(2 * i + 1, i, 1)
                    evacs(2 * i, i, 0)
                    if not last:
                        relus(2 * i + 2, i + 1, 0)
                    evacs(2 * i + 1, i, 1)

                body(0, False)
                with act.Fori(1, MACROS // 2 - 1) as i:
                    body(i, False)
                body(MACROS // 2 - 1, True)

            @block.vector
            def _(dve):
                dve.sem_inc(al_done, 32)
                def split_w(k):
                    dve.wait_ge(w_in[k % 2], 16 * (k // 2 + 1))
                    dve.tensor_copy(w_hi[:, k, :], w_raw[:, k % 2, :]).then_inc(w_hi_done, 1)
                    dve.wait_ge(w_hi_done, k + 1)
                    dve.tensor_tensor(w_lo[:, k, :], w_raw[:, k % 2, :], w_hi[:, k, :].bitcast(F32),
                                      ALU.subtract).then_inc(w_lo_done, 1)

                def splits(m, i, s):
                    dve.wait_ge(tile_done, 2 * m + 2)
                    width = P * len(node_tiles(m))
                    for f in range(FILLS):
                        ks = slice(2 * f, 2 * f + 2)
                        dve.wait_ge(relu_done, FILLS + FILLS * m + f + 1)
                        hi, lo, whole = (v[s][:, ks, 0:width] for v in (x_hi, x_lo, act_t))
                        dve.tensor_copy(hi, whole).then_inc(hi_done, 1)
                        dve.wait_ge(hi_done, FILLS * m + f + 1)
                        dve.tensor_tensor(lo, whole, hi.bitcast(F32), ALU.subtract).then_inc(lo_done, 1)

                def attention(m, i, s):
                    if not first(i):
                        dve.wait_ge(al_stored[s], 16 * i)
                    for j in node_tiles(m):
                        dve.wait_ge(evac_done, 2 + 2 * m + j + 1)
                        for a in range(2):
                            for hd in range(H):
                                cols = slice(hd * C, (hd + 1) * C)
                                dve.wait_ge(al_done, 32 + 16 * m + 8 * j + 4 * a + hd - 1)
                                dve.tensor_tensor_reduce(
                                    prod[hd % 2][:, :], h_sb[2 * s + j][:, cols], a_rows[:, a, cols], 1.0, 0.0,
                                    ALU.mult, ALU.add, al_sb[s][:, j, a * H + hd:a * H + hd + 1]).then_inc(al_done, 1)

                splits(0, 0, 0)
                for k in range(KC):
                    split_w(k)
                dve.wait_ge(a_in, 16)

                def body(i, last):
                    splits(2 * i + 1, i, 1)
                    attention(2 * i, i, 0)
                    if not last:
                        splits(2 * i + 2, i + 1, 0)
                    attention(2 * i + 1, i, 1)

                body(0, False)
                with dve.Fori(1, MACROS // 2 - 1) as i:
                    body(i, False)
                body(MACROS // 2 - 1, True)


def gat_edges(nc, sem, name, h_rows, al_rows, row_d, tab_d, bounce):
    RING = 4
    EARLY = 9
    with ExitStack() as ctx:
        sb = lambda n, s, d=F32: ctx.enter_context(nc.sbuf_tensor(f"{name}_{n}", s, d))
        ps = lambda n, s: ctx.enter_context(nc.psum_tensor(f"{name}_{n}", s, F32))
        tabs = sb("tabs", [P, ET, TAB])
        al_src = sb("al_src", [P, ET, 2 * H])
        al_dst = sb("al_dst", [P, ET, 2 * H])
        h_src = sb("h_src", [P, ET * HC])
        out = sb("out", [P, ET * HC])
        held = [h_src[0:H, EARLY * HC + n * (EP + 2):EARLY * HC + (n + 1) * (EP + 2)] for n in range(4)]
        keys = held[0]
        same = held[1][:, 0:EP + 1]
        cut = held[2][:, 0:EP + 1]
        top_row = held[3][:, 0:EP]
        fwd = held[1][:, 0:EP]
        bwd = held[0][:, 0:EP]
        key_col = sb("key_col", [P, ET + 1])
        ident = sb("ident", [P, P])
        score = sb("score", [P, 2, H, ET])
        raised = sb("raised", [P, 2, H, ET])
        top_pair = sb("top_pair", [P, H, ET])
        top_t = sb("top_t", [H * ET, P])
        max_t = sb("max_t", [H * ET, P])
        below = sb("below", [P, 2, H, ET])
        w_all = sb("w_all", [P, ET, 2, H])
        last_row = sb("last_row", [P, 1])
        key_row = [sb(f"key_row{s}", [P, P]) for s in range(RING)]
        mask = [sb(f"mask{s}", [P, H + 2, P]) for s in range(2)]
        sums = [sb(f"sums{s}", [P, HC + H]) for s in range(2)]
        den = sb("den", [P, 2, H])
        rden = sb("rden", [P, 2, H])
        w_own = sb("w_own", [P, 2, H])
        sum_ps = [ps(f"sum_ps{s}", [P, HC]) for s in range(2)]
        den_ps = [ps(f"den_ps{s}", [P, 512]) for s in range(2)]
        t_ps = ps("t_ps", [P, 512])

        small_in = sem(f"{name}_small_in")
        al_in = sem(f"{name}_al_in")
        const_done = sem(f"{name}_const_done")
        v = sem(f"{name}_v")
        top_turned = sem(f"{name}_top_turned")
        top_copied = sem(f"{name}_top_copied")
        bounced = sem(f"{name}_bounced")
        scanned = sem(f"{name}_scanned")
        max_turned = sem(f"{name}_max_turned")
        below_done = sem(f"{name}_below_done")
        w_done = sem(f"{name}_w_done")
        keys_in = [sem(f"{name}_keys_in{s}") for s in range(RING)]
        h_in = [sem(f"{name}_h_in{s}") for s in range(RING)]
        masks_done = sem(f"{name}_masks_done")
        den_done = sem(f"{name}_den_done")
        own_scaled = sem(f"{name}_own_scaled")
        summed = sem(f"{name}_summed")
        sums_out = sem(f"{name}_sums_out")
        finished = sem(f"{name}_finished")
        scattered = sem(f"{name}_scattered")
        zeroed = sem(f"{name}_zeroed")

        def weights(t, own):
            return w_all[:, bass.ds(t, 1), own, :].rearrange("p t h -> p (t h)")

        with nc.Block() as block:

            @block.sync
            def _(sp):
                sp.dma_start(tabs[:, :, :], tab_d.rearrange("(t p) k -> p t k", p=P)).then_inc(small_in, 16)
                sp.dma_start(keys, row_d.partition_broadcast(H)).then_inc(small_in, 16)
                sp.wait_ge(top_copied, 1)
                sp.dma_start(bounce[0], top_t[:, :]).then_inc(bounced, 16)
                sp.wait_ge(bounced, 16)
                sp.dma_start(top_row, bounce[0].rearrange("(h t) p -> h (t p)", h=H)).then_inc(bounced, 16)
                sp.wait_ge(scanned, 3)
                sp.dma_start(bounce[1].rearrange("(h t) p -> h (t p)", h=H), bwd).then_inc(bounced, 16)
                sp.wait_ge(bounced, 48)
                sp.dma_start(max_t[:, :], bounce[1]).then_inc(bounced, 16)
                with sp.Fori(0, ET // RING) as i:
                    for s in range(RING):
                        t = RING * i + s
                        sp.wait_ge(masks_done, t + 1)
                        sp.dma_start(key_row[s][:, :],
                                     row_d[bass.ds(t * P + 1, P)].partition_broadcast(P)).then_inc(keys_in[s], 16)

            @block.gpsimd
            def _(pool):
                pool.memset(ident[:, :], 0.0).then_inc(const_done, 1)
                pool.memset(last_row[:, :], 0.0).then_inc(const_done, 1)
                pool.wait_ge(const_done, 2)
                pool.affine_select(out=ident[:, :], in_=ident[:, :], compare_op=ALU.not_equal, fill=1.0,
                                   base=0, pattern=[[-1, P]], channel_multiplier=1).then_inc(const_done, 1)
                pool.affine_select(out=last_row[:, :], in_=last_row[:, :], compare_op=ALU.not_equal, fill=1.0,
                                   base=1 - P, pattern=[[0, 1]], channel_multiplier=1).then_inc(const_done, 1)
                pool.wait_ge(small_in, 32)
                index = lambda t, k: bass.IndirectOffsetOnAxis(tabs[:, t, k:k + 1].bitcast(I32), 0)

                def gather(t):
                    s = t % RING
                    if t >= RING:
                        pool.wait_ge(h_in[s], 32 * (t // RING))
                    span = slice(t * HC, (t + 1) * HC)
                    pool.indirect_dma_start(h_src[:, span], None, h_rows[0:NP], index(t, D_SRC)).then_inc(h_in[s], 16)
                    pool.indirect_dma_start(out[:, span], None, h_rows[0:NP], index(t, D_DST)).then_inc(h_in[s], 16)

                for t in range(ET):
                    pool.indirect_dma_start(al_src[:, t, :], None, al_rows, index(t, D_SRC)).then_inc(al_in, 16)
                    pool.indirect_dma_start(al_dst[:, t, :], None, al_rows, index(t, D_DST)).then_inc(al_in, 16)
                    if t % 5 == 4:
                        gather(t // 5)
                for t in range(ET // 5, EARLY):
                    gather(t)
                pool.wait_ge(bounced, 48)
                for t in range(EARLY, ET):
                    gather(t)
                for s in range(RING):
                    pool.wait_ge(h_in[s], 32 * (ET // RING))
                for t in range(ET):
                    pool.wait_ge(finished, RING + t + 1)
                    pool.indirect_dma_start(h_rows, index(t, D_OUT), out[:, t * HC:(t + 1) * HC],
                                            None).then_inc(scattered, 16)
                pool.wait_ge(scattered, 16 * ET)

            @block.tensor
            def _(pe):
                pe.sem_inc(summed, 2)
                pe.wait_ge(const_done, 4)
                pe.wait_ge(v, 3)
                pe.transpose(t_ps[0:H * ET, 0:P], top_pair[:, :, :].rearrange("p h t -> p (h t)"),
                             ident[:, :]).then_inc(top_turned, 1)
                pe.wait_ge(bounced, 64)
                pe.wait_ge(top_copied, 1)
                pe.transpose(t_ps[:, 128:128 + H * ET], max_t[:, :], ident[0:H * ET, 0:H * ET]).then_inc(max_turned, 1)
                pe.wait_ge(zeroed, 2)
                pe.wait_ge(w_done, 1)
                with pe.Fori(0, ET // RING) as i:
                    for s in range(RING):
                        t = RING * i + s
                        m = mask[s % 2]
                        pe.wait_ge(masks_done, t + 1 + RING)
                        pe.wait_ge(h_in[s], 32 * (i + 1))
                        pe.wait_ge(sums_out, t + 1)
                        for hd in range(H):
                            cols = slice(hd * C, (hd + 1) * C)
                            pe.matmul(sum_ps[s % 2][:, cols], m[:, hd, :], h_src[:, bass.ds(t * HC + hd * C, C)],
                                      start=(hd % 2 == 0), stop=False, skip_group_check=True)
                        pe.matmul(den_ps[s % 2][:, 0:H], m[:, H, :], weights(t, 0), start=True, stop=False)
                        prev = sums[(s + 1) % 2]
                        pe.wait_ge(sums_out, t + 2)
                        pe.matmul(den_ps[s % 2][:, 0:H], m[:, H + 1, :], prev[:, HC:HC + H], start=False, stop=True)
                        for n in range(2):
                            last = pe.matmul(sum_ps[s % 2][:, n * 512:(n + 1) * 512], m[:, H + 1, :],
                                             prev[:, n * 512:(n + 1) * 512], start=False, stop=True,
                                             skip_group_check=True)
                        last.then_inc(summed, 1)

            @block.scalar
            def _(act):
                act.sem_inc(sums_out, 2)
                act.sem_inc(own_scaled, 2)
                act.wait_ge(top_turned, 1)
                act.activation(top_t[:, :], t_ps[0:H * ET, 0:P], ACT.Copy).then_inc(top_copied, 1)
                act.wait_ge(below_done, 2)
                act.activation(w_all[:, :, :, :].rearrange("p t a h -> p a h t"), below[:, :, :, :],
                               ACT.Exp).then_inc(w_done, 1)
                with act.Fori(0, ET // RING) as i:
                    for s in range(RING):
                        t = RING * i + s
                        act.wait_ge(summed, t + 3)
                        act.wait_ge(finished, t + 3)
                        act.activation(sums[s % 2][:, 0:HC], sum_ps[s % 2][:, :], ACT.Copy)
                        act.activation(sums[s % 2][:, HC:HC + H], den_ps[s % 2][:, 0:H], ACT.Copy).then_inc(sums_out, 1)
                        act.wait_ge(den_done, 3 * t + 3)
                        act.wait_ge(h_in[s], 32 * (i + 1))
                        for hd in range(H):
                            row = out[:, bass.ds(t * HC + hd * C, C)]
                            last = act.activation(row, row, ACT.Copy, scale=w_own[:, s % 2, hd:hd + 1])
                        last.then_inc(own_scaled, 1)

            @block.vector
            def _(dve):
                dve.sem_inc(finished, 4)
                dve.sem_inc(masks_done, RING)
                dve.memset(key_col[:, 0:1], -5.0).then_inc(zeroed, 1)
                dve.memset(sums[1][:, :], 0.0).then_inc(zeroed, 1)
                dve.wait_ge(small_in, 32)
                dve.tensor_copy(key_col[:, 1:ET + 1], tabs[:, :, KEY])
                dve.tensor_tensor(same, keys[:, 0:EP + 1], keys[:, 1:EP + 2], ALU.is_equal).then_inc(v, 1)
                dve.wait_ge(v, 1)
                dve.tensor_scalar(cut, same, -1.0, 1e30, ALU.add, ALU.mult)
                dve.wait_ge(al_in, 16 * 2 * ET)
                hv = lambda ap, k: ap[:, :, k * H:(k + 1) * H].rearrange("p t h -> p h t")
                dve.tensor_tensor(score[:, 0, :, :], hv(al_src, 0), hv(al_dst, 1), ALU.add)
                dve.tensor_tensor(score[:, 1, :, :], hv(al_dst, 0), hv(al_dst, 1), ALU.add).then_inc(v, 1)
                dve.wait_ge(v, 2)
                flat = lambda ap: ap[:, :, :, :].rearrange("p a h t -> p (a h t)")
                dve.scalar_tensor_tensor(flat(raised), flat(score), 0.2, flat(score), ALU.mult, ALU.max).then_inc(below_done, 1)
                dve.wait_ge(below_done, 1)
                dve.tensor_tensor(top_pair[:, :, :], raised[:, 0, :, :], raised[:, 1, :, :], ALU.max).then_inc(v, 1)
                dve.wait_ge(bounced, 32)
                dve.tensor_tensor_scan(fwd, cut[:, 0:EP], top_row, 0.0, ALU.add, ALU.max).then_inc(scanned, 1)
                dve.wait_ge(scanned, 1)
                dve.tensor_tensor_scan(bwd[:, ::-1], cut[:, EP:0:-1], fwd[:, ::-1], 0.0, ALU.add, ALU.max).then_inc(scanned, 2)
                dve.wait_ge(max_turned, 1)
                mx = t_ps[:, 128:128 + H * ET].rearrange("p (h t) -> p h t", h=H)
                dve.tensor_tensor(below[:, 0, :, :], raised[:, 0, :, :], mx, ALU.subtract)
                dve.tensor_tensor(below[:, 1, :, :], raised[:, 1, :, :], mx, ALU.subtract).then_inc(below_done, 1)

                def masks(i, s):
                    dve.wait_ge(keys_in[s], 16 * (i + 1))
                    t = RING * i + s
                    dve.wait_ge(summed, t + 1)
                    key = key_col[:, bass.ds(t + 1, 1)]
                    m = mask[s % 2]
                    for hd in range(H):
                        weight = w_all[:, bass.ds(t, 1), 0, hd:hd + 1].rearrange("p t h -> p (t h)")
                        dve.tensor_scalar(m[:, hd, :], key_row[s][:, :], key, weight, ALU.is_equal, ALU.mult)
                    dve.tensor_scalar(m[:, H, :], key_row[s][:, :], key, None, ALU.is_equal)
                    dve.tensor_scalar(m[:, H + 1, :], key_row[s][:, :], key_col[:, bass.ds(t, 1)],
                                      last_row[:, 0:1], ALU.is_equal, ALU.mult).then_inc(masks_done, 1)

                def shares(i, s):
                    t = RING * i + s
                    q = s % 2
                    dve.wait_ge(sums_out, t + 3)
                    dve.wait_ge(own_scaled, t + 1)
                    dve.tensor_tensor(den[:, q, :], sums[q][:, HC:HC + H], weights(t, 1), ALU.add).then_inc(den_done, 1)
                    dve.wait_ge(den_done, 3 * t + 1)
                    dve.reciprocal(rden[:, q, :], den[:, q, :]).then_inc(den_done, 1)
                    dve.wait_ge(den_done, 3 * t + 2)
                    dve.tensor_tensor(w_own[:, q, :], rden[:, q, :], weights(t, 1), ALU.mult).then_inc(den_done, 1)

                def finish(i, s):
                    t = RING * i + s
                    q = s % 2
                    dve.wait_ge(own_scaled, t + 3)
                    for hd in range(H):
                        cols = slice(hd * C, (hd + 1) * C)
                        row = out[:, bass.ds(t * HC + hd * C, C)]
                        last = dve.scalar_tensor_tensor(row, sums[q][:, cols], rden[:, q, hd:hd + 1], row,
                                                        ALU.mult, ALU.add)
                    last.then_inc(finished, 1)

                dve.wait_ge(const_done, 4)
                dve.wait_ge(zeroed, 2)
                dve.wait_ge(w_done, 1)
                masks(0, 0)
                masks(0, 1)

                def body(i, last):
                    for s in range(RING):
                        shares(i, s)
                        if s + 2 < RING:
                            masks(i, s + 2)
                        elif not last:
                            masks(i + 1, s + 2 - RING)
                        finish(i, s)

                with dve.Fori(0, ET // RING - 1) as i:
                    body(i, False)
                body(ET // RING - 1, True)


def fc_dense(nc, sem, src, w, bias, x_rows, b_out, x1_out, y_out):
    KC = HC // P
    G = 2 * P
    MACROS = LOOPED // G
    FILLS = KC // 2
    with ExitStack() as ctx:
        sb = lambda n, s, d=F32: ctx.enter_context(nc.sbuf_tensor(f"fc_{n}", s, d))
        ps = lambda n, s: ctx.enter_context(nc.psum_tensor(f"fc_{n}", s, F32))
        w_raw = sb("w_raw", [P, 2, D])
        w_hi = sb("w_hi", [P, KC, D], F32R)
        w_lo = sb("w_lo", [P, KC, D], F32R)
        b_rows = sb("b_rows", [P, 2, D])
        h_in = [sb(f"h_in{s}", [P, 2, HC]) for s in range(2)]
        x_in = [sb(f"x_in{s}", [P, 2, D]) for s in range(2)]
        x_b = [sb(f"x_b{s}", [P, 2, D]) for s in range(2)]
        act_t = [sb(f"act_t{s}", [P, KC, G]) for s in range(2)]
        x_hi = [sb(f"x_hi{s}", [P, KC, G], F32R) for s in range(2)]
        x_lo = [sb(f"x_lo{s}", [P, KC, G], F32R) for s in range(2)]
        ident = sb("ident", [P, P])
        b_col = sb("b_col", [P, KC])
        z = [sb(f"z{s}", [P, 2, D]) for s in range(2)]
        stats = [sb(f"stats{s}", [P, 2, 6]) for s in range(2)]
        mv = [sb(f"mv{s}", [P, 2, 2]) for s in range(2)]
        ds = [sb(f"ds{s}", [P, 4, 2]) for s in range(2)]
        inv = [sb(f"inv{s}", [P, 2, 2]) for s in range(2)]
        rstd = [sb(f"rstd{s}", [P, 2, 2]) for s in range(2)]
        shift = [sb(f"shift{s}", [P, 2, 2]) for s in range(2)]
        x1 = [sb(f"x1{s}", [P, 2, D]) for s in range(2)]
        y = [sb(f"y{s}", [P, 2, D]) for s in range(2)]
        o_ps = [ps(f"o_ps{s}", [P, D]) for s in range(4)]
        t_ps = [ps(f"t_ps{s}", [P, 2, G]) for s in range(FILLS)]

        w_in = [sem(f"fc_w_in{s}") for s in range(2)]
        b_in = sem("fc_b_in")
        b_rows_in = sem("fc_b_rows_in")
        h_loaded = [sem(f"fc_h_loaded{s}") for s in range(2)]
        x_loaded = [sem(f"fc_x_loaded{s}") for s in range(2)]
        x1_stored = [sem(f"fc_x1_stored{s}") for s in range(2)]
        y_stored = [sem(f"fc_y_stored{s}") for s in range(2)]
        w_hi_done = sem("fc_w_hi_done")
        w_lo_done = sem("fc_w_lo_done")
        hi_done = sem("fc_hi_done")
        lo_done = sem("fc_lo_done")
        filled = sem("fc_filled")
        relu_done = sem("fc_relu_done")
        tile_done = sem("fc_tile_done")
        xb_done = sem("fc_xb_done")
        summed = sem("fc_summed")
        ln = sem("fc_ln")
        rooted = sem("fc_rooted")
        x1_done = sem("fc_x1_done")
        ident_done = sem("fc_ident_done")
        passed = sem("fc_passed")
        LN_STEPS = 9

        def rows(ap, m):
            return ap[bass.ds(m * G, len(node_tiles(m)) * P), :].rearrange("(j p) k -> p j k", p=P)

        def first(i):
            return isinstance(i, int) and i == 0

        with nc.Block() as block:

            @block.sync
            def _(sp):
                def load(m, s):
                    n = len(node_tiles(m))
                    sp.dma_start(h_in[s][:, 0:n, :], rows(src, m)).then_inc(h_loaded[s], 16)
                    sp.dma_start(x_in[s][:, 0:n, :], rows(x_rows, m)).then_inc(x_loaded[s], 16)

                load(0, 0)
                sp.dma_start(b_col[:, :], bias).then_inc(b_in, 16)
                for k in range(KC):
                    if k >= 2:
                        sp.wait_ge(w_lo_done, k - 1)
                    sp.dma_start(w_raw[:, k % 2, :], w[k * P:(k + 1) * P, :]).then_inc(w_in[k % 2], 16)
                load(1, 1)
                sp.dma_start(b_rows[:, 0, :], b_out.partition_broadcast(P)).then_inc(b_rows_in, 16)
                sp.dma_start(b_rows[:, 1, :], b_out.partition_broadcast(P)).then_inc(b_rows_in, 16)

                def body(i):
                    for s in range(2):
                        m = 2 * i + s
                        sp.wait_ge(filled, FILLS * (m + 1))
                        sp.sem_inc(passed, 1)
                        sp.wait_ge(xb_done, m + 3)
                        sp.sem_inc(passed, 1)
                        load(m + 2, s)

                with sp.Fori(0, MACROS // 2 - 2) as i:
                    body(i)
                body(MACROS // 2 - 2)

            @block.gpsimd
            def _(pool):
                pool.sem_inc(xb_done, 2)
                pool.memset(ident[:, :], 0.0).then_inc(ident_done, 1)
                pool.wait_ge(ident_done, 1)
                pool.affine_select(out=ident[:, :], in_=ident[:, :], compare_op=ALU.not_equal, fill=1.0,
                                   base=0, pattern=[[-1, P]], channel_multiplier=1).then_inc(ident_done, 1)
                pool.wait_ge(b_rows_in, 32)

                def add_bias(m, i, s):
                    pool.wait_ge(x_loaded[s], 16 * (i + 1))
                    pool.wait_ge(summed, 2 * m + 2)
                    n = len(node_tiles(m))
                    pool.tensor_tensor(x_b[s][:, 0:n, :], x_in[s][:, 0:n, :], b_rows[:, 0:n, :],
                                       ALU.add).then_inc(xb_done, 1)

                def store(m, i, s):
                    n = len(node_tiles(m))
                    pool.wait_ge(x1_done, m + 3)
                    pool.sem_inc(passed, 1)
                    pool.dma_start(rows(x1_out, m), x1[s][:, 0:n, :]).then_inc(x1_stored[s], 16)
                    pool.wait_ge(ln, LN_STEPS * (m + 1))
                    pool.sem_inc(passed, 1)
                    pool.dma_start(rows(y_out, m), y[s][:, 0:n, :]).then_inc(y_stored[s], 16)

                add_bias(0, 0, 0)

                def body(i, last):
                    add_bias(2 * i + 1, i, 1)
                    store(2 * i, i, 0)
                    if not last:
                        add_bias(2 * i + 2, i + 1, 0)
                    store(2 * i + 1, i, 1)

                with pool.Fori(0, MACROS // 2 - 1) as i:
                    body(i, False)
                body(MACROS // 2 - 1, True)
                for s in range(2):
                    pool.wait_ge(x1_stored[s], 16 * (MACROS // 2))
                    pool.wait_ge(y_stored[s], 16 * (MACROS // 2))

            @block.tensor
            def _(pe):
                pe.sem_inc(tile_done, 4)
                pe.wait_ge(ident_done, 2)

                def transposes(m, i, s):
                    pe.wait_ge(h_loaded[s], 16 * (i + 1))
                    for f in range(FILLS):
                        pe.wait_ge(relu_done, FILLS * m + f + 1)
                        for c in range(2):
                            for j in node_tiles(m):
                                k = 2 * f + c
                                last = pe.transpose(t_ps[f][:, c, j * P:(j + 1) * P],
                                                    h_in[s][:, j, k * P:(k + 1) * P], ident[:, :])
                        last.then_inc(filled, 1)

                def first_products():
                    pe.wait_ge(lo_done, FILLS)
                    for k in range(KC):
                        pe.wait_ge(w_lo_done, k + 1)
                        for j in range(2):
                            xh = x_hi[0][:, k, j * P:(j + 1) * P]
                            xl = x_lo[0][:, k, j * P:(j + 1) * P]
                            out = o_ps[j][:, :]
                            pe.matmul(out, xh, w_hi[:, k, :], start=(k == 0), stop=False)
                            pe.matmul(out, xh, w_lo[:, k, :], start=False, stop=False)
                            last = pe.matmul(out, xl, w_hi[:, k, :], start=False, stop=(k == KC - 1))
                            if k == KC - 1:
                                last.then_inc(tile_done, 1)

                def products(m, i, s, tiles):
                    pe.wait_ge(lo_done, FILLS * (m + 1))
                    for j in tiles:
                        pe.wait_ge(summed, 2 * m + j + 1)
                        for k in range(KC):
                            xh = x_hi[s][:, k, j * P:(j + 1) * P]
                            xl = x_lo[s][:, k, j * P:(j + 1) * P]
                            out = o_ps[2 * s + j][:, :]
                            pe.matmul(out, xh, w_hi[:, k, :], start=(k == 0), stop=False)
                            pe.matmul(out, xh, w_lo[:, k, :], start=False, stop=False)
                            last = pe.matmul(out, xl, w_hi[:, k, :], start=False, stop=(k == KC - 1))
                        last.then_inc(tile_done, 1)

                def body(i, last):
                    if first(i):
                        transposes(0, 0, 0)
                        first_products()
                        transposes(1, 0, 1)
                    else:
                        products(2 * i, i, 0, [0])
                        transposes(2 * i + 1, i, 1)
                        products(2 * i, i, 0, [1])
                    products(2 * i + 1, i, 1, [0])
                    if not last:
                        transposes(2 * i + 2, i + 1, 0)
                    if len(node_tiles(2 * i + 1)) == 2:
                        products(2 * i + 1, i, 1, [1])

                body(0, False)
                with pe.Fori(1, MACROS // 2 - 1) as i:
                    body(i, False)
                body(MACROS // 2 - 1, True)

            @block.scalar
            def _(act):
                act.sem_inc(relu_done, FILLS)
                act.sem_inc(x1_done, 2)
                act.wait_ge(b_in, 16)

                def relus(m, i, s):
                    width = P * len(node_tiles(m))
                    for f in range(FILLS):
                        act.wait_ge(filled, FILLS * m + f + 1)
                        for c in range(2):
                            k = 2 * f + c
                            last = act.activation(act_t[s][:, k, 0:width], t_ps[f][:, c, 0:width], ACT.Relu,
                                                  bias=b_col[:, k:k + 1])
                        last.then_inc(relu_done, 1)

                def normalize(m, i, s):
                    act.wait_ge(ln, LN_STEPS * m + 7)
                    act.activation(rstd[s][:, :, :], inv[s][:, :, :], ACT.Sqrt).then_inc(rooted, 1)
                    act.wait_ge(ln, LN_STEPS * m + 8)
                    if not first(i):
                        act.wait_ge(x1_stored[s], 16 * i)
                    for j in node_tiles(m):
                        last = act.activation(x1[s][:, j, :], z[s][:, j, :], ACT.Identity,
                                              bias=shift[s][:, 0, j:j + 1], scale=rstd[s][:, 0, j:j + 1])
                    last.then_inc(x1_done, 1)

                relus(0, 0, 0)

                def body(i, last):
                    relus(2 * i + 1, i, 1)
                    normalize(2 * i, i, 0)
                    if not last:
                        relus(2 * i + 2, i + 1, 0)
                    normalize(2 * i + 1, i, 1)

                body(0, False)
                with act.Fori(1, MACROS // 2 - 1) as i:
                    body(i, False)
                body(MACROS // 2 - 1, True)

            @block.vector
            def _(dve):
                dve.sem_inc(summed, 4)
                def splits(m, i, s):
                    dve.wait_ge(tile_done, 2 * m + 2)
                    width = P * len(node_tiles(m))
                    for f in range(FILLS):
                        ks = slice(2 * f, 2 * f + 2)
                        dve.wait_ge(relu_done, FILLS + FILLS * m + f + 1)
                        hi, lo, whole = (v[s][:, ks, 0:width] for v in (x_hi, x_lo, act_t))
                        dve.tensor_copy(hi, whole).then_inc(hi_done, 1)
                        dve.wait_ge(hi_done, FILLS * m + f + 1)
                        dve.tensor_tensor(lo, whole, hi.bitcast(F32), ALU.subtract).then_inc(lo_done, 1)

                def layer_norm(m, i, s):
                    dve.wait_ge(xb_done, m + 3)
                    dve.wait_ge(x1_done, m + 1)
                    for j in node_tiles(m):
                        dve.wait_ge(tile_done, 4 + 2 * m + j + 1)
                        dve.tensor_tensor(z[s][:, j, :], o_ps[2 * s + j][:, :], x_b[s][:, j, :], ALU.add).then_inc(summed, 1)
                        dve.wait_ge(summed, 4 + 2 * m + j + 1)
                        last = dve.bn_stats(stats[s][:, j, :], z[s][:, j, :])
                    last.then_inc(ln, 1)
                    dve.wait_ge(ln, LN_STEPS * m + 1)
                    dve.sem_inc(passed, 1)
                    for j in node_tiles(m):
                        last = dve.bn_aggr(mv[s][:, j, :], stats[s][:, j, :])
                    last.then_inc(ln, 1)
                    dve.wait_ge(ln, LN_STEPS * m + 2)
                    var = mv[s][:, :, 1]
                    dve.tensor_scalar(ds[s][:, 0, :], var, EPS, None, ALU.add).then_inc(ln, 1)
                    dve.wait_ge(ln, LN_STEPS * m + 3)
                    for n, (a, b) in enumerate(((0, 2), (2, 3), (3, 1))):
                        dve.scalar_tensor_tensor(ds[s][:, b, :], ds[s][:, a, :], EPS, var,
                                                 ALU.mult, ALU.add).then_inc(ln, 1)
                        dve.wait_ge(ln, LN_STEPS * m + 4 + n)
                    dve.reciprocal(inv[s][:, :, :], ds[s][:, 0:2, :]).then_inc(ln, 1)
                    dve.wait_ge(rooted, m + 1)
                    for n in range(2):
                        last = dve.scalar_tensor_tensor(shift[s][:, n, :], mv[s][:, :, 0], -1.0, rstd[s][:, n, :],
                                                        ALU.mult, ALU.mult)
                    last.then_inc(ln, 1)
                    dve.wait_ge(ln, LN_STEPS * m + 8)
                    if not first(i):
                        dve.wait_ge(y_stored[s], 16 * i)
                    for j in node_tiles(m):
                        last = dve.tensor_scalar(y[s][:, j, :], z[s][:, j, :], rstd[s][:, 1, j:j + 1],
                                                 shift[s][:, 1, j:j + 1], ALU.mult, ALU.add)
                    last.then_inc(ln, 1)


                splits(0, 0, 0)
                for k in range(KC):
                    dve.wait_ge(w_in[k % 2], 16 * (k // 2 + 1))
                    dve.tensor_copy(w_hi[:, k, :], w_raw[:, k % 2, :]).then_inc(w_hi_done, 1)
                    dve.wait_ge(w_hi_done, k + 1)
                    dve.tensor_tensor(w_lo[:, k, :], w_raw[:, k % 2, :], w_hi[:, k, :].bitcast(F32),
                                      ALU.subtract).then_inc(w_lo_done, 1)

                def body(i, last):
                    splits(2 * i + 1, i, 1)
                    layer_norm(2 * i, i, 0)
                    if not last:
                        splits(2 * i + 2, i + 1, 0)
                    layer_norm(2 * i + 1, i, 1)

                body(0, False)
                with dve.Fori(1, MACROS // 2 - 1) as i:
                    body(i, False)
                body(MACROS // 2 - 1, True)


def conv_edges(nc, sem, x1_rows, row_d, tab_d, w, x2_rows, y_rows):
    RING = 4
    AHEAD = 8
    KC = D // P
    with ExitStack() as ctx:
        sb = lambda n, s, d=F32: ctx.enter_context(nc.sbuf_tensor(f"conv_{n}", s, d))
        ps = lambda n, s: ctx.enter_context(nc.psum_tensor(f"conv_{n}", s, F32))
        tabs = sb("tabs", [P, ET, TAB])
        keys = sb("keys", [P, ET + 1])
        key_rows = sb("key_rows", [P, EP])
        w_raw = sb("w_raw", [P, KC, D])
        w_hi = sb("w_hi", [P, KC, D], F32R)
        w_lo = sb("w_lo", [P, KC, D], F32R)
        ident = sb("ident", [P, P])
        last_row = sb("last_row", [P, 1])
        x_src = sb("x_src", [P, ET * D])
        x_dst = sb("x_dst", [P, ET * D])
        mask = [sb(f"mask{s}", [P, 2, P]) for s in range(2)]
        sums = [sb(f"sums{s}", [P, D]) for s in range(2)]
        t_hi = [sb(f"t_hi{s}", [P, KC, P], F32R) for s in range(2)]
        t_lo = [sb(f"t_lo{s}", [P, KC, P], F32R) for s in range(2)]
        z = [sb(f"z{s}", [P, D]) for s in range(2)]
        stats = [sb(f"stats{s}", [P, 2, 6]) for s in range(2)]
        mv = [sb(f"mv{s}", [P, 2, 2]) for s in range(2)]
        ds = [sb(f"ds{s}", [P, 4]) for s in range(2)]
        log_d = [sb(f"log_d{s}", [P, 3]) for s in range(2)]
        rstd = [sb(f"rstd{s}", [P, 3]) for s in range(2)]
        shift = [sb(f"shift{s}", [P, 3]) for s in range(2)]
        x2 = [sb(f"x2{s}", [P, 2, D]) for s in range(2)]
        y = [sb(f"y{s}", [P, D]) for s in range(RING)]
        sum_ps = [ps(f"sum_ps{s}", [P, D]) for s in range(2)]
        t_ps = [ps(f"t_ps{s}", [P, KC, P]) for s in range(2)]
        y_ps = [ps(f"y_ps{s}", [P, D]) for s in range(2)]

        tabs_in = sem("conv_tabs_in")
        w_in = sem("conv_w_in")
        w_split = sem("conv_w_split")
        const_done = sem("conv_const_done")
        zeroed = sem("conv_zeroed")
        keys_in = sem("conv_keys_in")
        x_in = [sem(f"conv_x_in{s}") for s in range(RING)]
        masks_done = sem("conv_masks_done")
        summed = sem("conv_summed")
        sums_out = sem("conv_sums_out")
        turned = sem("conv_turned")
        hi_done = sem("conv_hi_done")
        lo_done = sem("conv_lo_done")
        multiplied = sem("conv_multiplied")
        z_done = sem("conv_z_done")
        ln = sem("conv_ln")
        logged = sem("conv_logged")
        rooted = sem("conv_rooted")
        x2_done = sem("conv_x2_done")
        x2_stored = sem("conv_x2_stored")
        x2_freed = sem("conv_x2_freed")
        y_done = sem("conv_y_done")
        y_scattered = sem("conv_y_scattered")
        y_freed = sem("conv_y_freed")
        passed = sem("conv_passed")
        LN_STEPS = 6

        with nc.Block() as block:

            @block.sync
            def _(sp):
                sp.dma_start(tabs[:, :, :], tab_d.rearrange("(t p) k -> p t k", p=P)).then_inc(tabs_in, 16)
                sp.dma_start(key_rows[:, :], row_d[1:EP + 1].partition_broadcast(P)).then_inc(keys_in, 16)
                sp.dma_start(w_raw[:, :, :], w.rearrange("(c p) n -> p c n", p=P)).then_inc(w_in, 16)
                sp.sem_inc(x2_freed, 2)
                halves = x2_rows.rearrange("(a e) n -> a e n", a=2)
                with sp.Fori(0, ET // 2) as i:
                    for s in range(2):
                        t = 2 * i + s
                        sp.wait_ge(x2_done, t + 3)
                        sp.sem_inc(passed, 1)
                        sp.dma_start(halves[:, bass.ds(t * P, P), :].rearrange("a p n -> p a n"),
                                     x2[s][:, :, :]).then_inc(x2_stored, 16)
                        sp.wait_ge(x2_stored, 16 * (t + 1))
                        sp.sem_inc(x2_freed, 1)

            @block.gpsimd
            def _(pool):
                pool.memset(ident[:, :], 0.0).then_inc(const_done, 1)
                pool.memset(last_row[:, :], 0.0).then_inc(const_done, 1)
                pool.wait_ge(const_done, 2)
                pool.affine_select(out=ident[:, :], in_=ident[:, :], compare_op=ALU.not_equal, fill=1.0,
                                   base=0, pattern=[[-1, P]], channel_multiplier=1).then_inc(const_done, 1)
                pool.affine_select(out=last_row[:, :], in_=last_row[:, :], compare_op=ALU.not_equal, fill=1.0,
                                   base=1 - P, pattern=[[0, 1]], channel_multiplier=1).then_inc(const_done, 1)
                pool.sem_inc(y_freed, RING)
                pool.wait_ge(tabs_in, 16)
                index = lambda t, k: bass.IndirectOffsetOnAxis(tabs[:, t, k:k + 1].bitcast(I32), 0)
                for t in range(ET + AHEAD):
                    if t < ET:
                        s = t % RING
                        if t >= RING:
                            pool.wait_ge(x_in[s], 32 * (t // RING))
                        pool.indirect_dma_start(x_src[:, t * D:(t + 1) * D], None, x1_rows, index(t, D_SRC)).then_inc(x_in[s], 16)
                        pool.indirect_dma_start(x_dst[:, t * D:(t + 1) * D], None, x1_rows, index(t, D_DST)).then_inc(x_in[s], 16)
                    if t >= AHEAD:
                        e = t - AHEAD
                        if e:
                            pool.wait_ge(y_scattered, 16 * e)
                            pool.sem_inc(y_freed, 1)
                        pool.wait_ge(y_done, e + 1)
                        pool.indirect_dma_start(y_rows, index(e, D_OUT), y[e % RING][:, :], None).then_inc(y_scattered, 16)
                pool.wait_ge(y_scattered, 16 * ET)

            @block.tensor
            def _(pe):
                pe.sem_inc(summed, 2)
                pe.sem_inc(turned, 2)
                pe.sem_inc(multiplied, 2)
                pe.wait_ge(const_done, 4)
                pe.wait_ge(zeroed, 1)

                def sum_edges(i, s):
                    t = RING * i + s
                    q = s % 2
                    pe.wait_ge(masks_done, t + 1)
                    pe.wait_ge(x_in[s], 32 * (i + 1))
                    pe.wait_ge(sums_out, t + 1)
                    pe.matmul(sum_ps[q][:, :], mask[q][:, 0, :], x_src[:, bass.ds(t * D, D)], start=True, stop=False)
                    pe.wait_ge(sums_out, t + 2)
                    pe.matmul(sum_ps[q][:, :], mask[q][:, 1, :], sums[1 - q][:, :], start=False, stop=True).then_inc(summed, 1)

                def turn(i, s):
                    t = RING * i + s
                    q = s % 2
                    pe.wait_ge(sums_out, t + 3)
                    pe.wait_ge(lo_done, t + 1)
                    for k in range(KC):
                        last = pe.transpose(t_ps[q][:, k, :], sums[q][:, k * P:(k + 1) * P], ident[:, :])
                    last.then_inc(turned, 1)

                def product(i, s):
                    t = RING * i + s
                    q = s % 2
                    pe.wait_ge(lo_done, t + 3)
                    pe.wait_ge(z_done, t + 1)
                    for k in range(KC):
                        pe.matmul(y_ps[q][:, :], t_hi[q][:, k, :], w_hi[:, k, :], start=(k == 0), stop=False)
                        pe.matmul(y_ps[q][:, :], t_hi[q][:, k, :], w_lo[:, k, :], start=False, stop=False)
                        last = pe.matmul(y_ps[q][:, :], t_lo[q][:, k, :], w_hi[:, k, :], start=False, stop=(k == KC - 1))
                    last.then_inc(multiplied, 1)

                sum_edges(0, 0)
                turn(0, 0)
                sum_edges(0, 1)
                pe.wait_ge(w_split, 2)

                def body(i, last):
                    for s in range(RING):
                        product(i, s)
                        if s + 1 < RING:
                            turn(i, s + 1)
                        elif not last:
                            turn(i + 1, 0)
                        if s + 2 < RING:
                            sum_edges(i, s + 2)
                        elif not last:
                            sum_edges(i + 1, s + 2 - RING)

                with pe.Fori(0, ET // RING - 1) as i:
                    body(i, False)
                body(ET // RING - 1, True)

            @block.scalar
            def _(act):
                act.sem_inc(sums_out, 2)
                act.sem_inc(x2_done, 2)
                act.preload_act_table_set("natural_log_exp_and_others")

                def copy_sums(i, s):
                    t = RING * i + s
                    act.wait_ge(summed, t + 3)
                    act.wait_ge(turned, t + 1)
                    act.activation(sums[s % 2][:, :], sum_ps[s % 2][:, :], ACT.Copy).then_inc(sums_out, 1)

                def normalize(i, s):
                    t = RING * i + s
                    q = s % 2
                    act.wait_ge(ln, LN_STEPS * t + 5)
                    act.activation(log_d[q][:, :], ds[q][:, 0:3], ACT.Ln).then_inc(logged, 1)
                    act.wait_ge(logged, t + 1)
                    act.activation(rstd[q][:, :], log_d[q][:, :], ACT.Exp, scale=-0.5).then_inc(rooted, 1)
                    act.wait_ge(ln, LN_STEPS * t + 6)
                    act.wait_ge(x2_freed, t + 1)
                    act.activation(x2[q][:, 0, :], z[q][:, :], ACT.Identity, bias=shift[q][:, 0:1], scale=rstd[q][:, 0:1])
                    act.activation(x2[q][:, 1, :], x_src[:, bass.ds(t * D, D)], ACT.Identity,
                                   bias=shift[q][:, 1:2], scale=rstd[q][:, 1:2]).then_inc(x2_done, 1)

                copy_sums(0, 0)
                copy_sums(0, 1)

                def body(i, last):
                    for s in range(RING):
                        if s + 2 < RING:
                            copy_sums(i, s + 2)
                        elif not last:
                            copy_sums(i + 1, s + 2 - RING)
                        normalize(i, s)

                with act.Fori(0, ET // RING - 1) as i:
                    body(i, False)
                body(ET // RING - 1, True)

            @block.vector
            def _(dve):
                dve.sem_inc(lo_done, 2)
                dve.sem_inc(z_done, 2)
                dve.memset(sums[1][:, :], 0.0).then_inc(zeroed, 1)
                dve.memset(keys[:, 0:1], -5.0)
                dve.wait_ge(tabs_in, 16)
                dve.tensor_copy(keys[:, 1:ET + 1], tabs[:, :, KEY]).then_inc(keys_in, 1)
                dve.wait_ge(keys_in, 17)
                dve.wait_ge(const_done, 4)

                def masks(i, s):
                    t = RING * i + s
                    dve.wait_ge(summed, t + 1)
                    m = mask[s % 2]
                    row = key_rows[:, bass.ds(t * P, P)]
                    dve.tensor_scalar(m[:, 0, :], row, keys[:, bass.ds(t + 1, 1)],
                                      tabs[:, bass.ds(t, 1), D_EW:D_EW + 1].rearrange("p a b -> p (a b)"),
                                      ALU.is_equal, ALU.mult)
                    dve.tensor_scalar(m[:, 1, :], row, keys[:, bass.ds(t, 1)], last_row[:, 0:1],
                                      ALU.is_equal, ALU.mult).then_inc(masks_done, 1)

                def split(i, s):
                    t = RING * i + s
                    q = s % 2
                    dve.wait_ge(turned, t + 3)
                    dve.wait_ge(multiplied, t + 1)
                    dve.tensor_copy(t_hi[q][:, :, :], t_ps[q][:, :, :]).then_inc(hi_done, 1)
                    dve.wait_ge(hi_done, t + 1)
                    dve.tensor_tensor(t_lo[q][:, :, :], t_ps[q][:, :, :], t_hi[q][:, :, :].bitcast(F32),
                                      ALU.subtract).then_inc(lo_done, 1)

                def factors(i, s):
                    t = RING * i + s
                    q = s % 2
                    dve.wait_ge(multiplied, t + 3)
                    dve.wait_ge(x_in[s], 32 * (i + 1))
                    dve.wait_ge(x2_done, t + 1)
                    dve.scalar_tensor_tensor(z[q][:, :], y_ps[q][:, :], 0.0, x_dst[:, bass.ds(t * D, D)],
                                             ALU.max, ALU.add).then_inc(z_done, 1)
                    dve.bn_stats(stats[q][:, 1, :], x_src[:, bass.ds(t * D, D)])
                    dve.wait_ge(z_done, t + 3)
                    dve.bn_stats(stats[q][:, 0, :], z[q][:, :]).then_inc(ln, 1)
                    dve.wait_ge(ln, LN_STEPS * t + 1)
                    dve.sem_inc(passed, 1)
                    for n in range(2):
                        last = dve.bn_aggr(mv[q][:, n, :], stats[q][:, n, :])
                    last.then_inc(ln, 1)
                    dve.wait_ge(ln, LN_STEPS * t + 2)
                    dve.tensor_scalar(ds[q][:, 0:2], mv[q][:, :, 1], EPS, None, ALU.add).then_inc(ln, 1)
                    for n, (a, b) in enumerate(((0, 3), (3, 2))):
                        dve.wait_ge(ln, LN_STEPS * t + 3 + n)
                        dve.scalar_tensor_tensor(ds[q][:, b:b + 1], ds[q][:, a:a + 1], EPS, mv[q][:, 0:1, 1],
                                                 ALU.mult, ALU.add).then_inc(ln, 1)

                def finish(i, s):
                    t = RING * i + s
                    q = s % 2
                    dve.wait_ge(rooted, t + 1)
                    dve.scalar_tensor_tensor(shift[q][:, 0:2], mv[q][:, :, 0], -1.0, rstd[q][:, 0:2], ALU.mult, ALU.mult)
                    dve.scalar_tensor_tensor(shift[q][:, 2:3], mv[q][:, 0:1, 0], -1.0, rstd[q][:, 2:3],
                                             ALU.mult, ALU.mult).then_inc(ln, 1)
                    dve.wait_ge(ln, LN_STEPS * t + 6)
                    dve.wait_ge(y_freed, t + 1)
                    dve.tensor_scalar(y[s][:, :], z[q][:, :], rstd[q][:, 2:3], shift[q][:, 2:3],
                                      ALU.mult, ALU.add).then_inc(y_done, 1)

                masks(0, 0)
                masks(0, 1)
                dve.wait_ge(w_in, 16)
                dve.tensor_copy(w_hi[:, :, :], w_raw[:, :, :]).then_inc(w_split, 1)
                dve.wait_ge(w_split, 1)
                dve.tensor_tensor(w_lo[:, :, :], w_raw[:, :, :], w_hi[:, :, :].bitcast(F32), ALU.subtract).then_inc(w_split, 1)
                split(0, 0)
                masks(0, 2)

                def body(i, last):
                    for s in range(RING):
                        if s + 1 < RING:
                            split(i, s + 1)
                        elif not last:
                            split(i + 1, 0)
                        factors(i, s)
                        if s + 3 < RING:
                            masks(i, s + 3)
                        elif not last:
                            masks(i + 1, s + 3 - RING)
                        finish(i, s)

                with dve.Fori(0, ET // RING - 1) as i:
                    body(i, False)
                body(ET // RING - 1, True)


def painn_edges(nc, sem, x2_rows, row_s, tab_s, u_tab, w_in_d, w_o1s, w_o1v, w_o2s, w_o2v, x3_rows):
    RING = 4
    GROUPS = ET // RING
    NORMALIZED = ((), (0,), (1,), (2, 3))
    B = P
    F = w_in_d.shape[2]
    M_COLS = 4 * F + 3 * 2 * F
    with ExitStack() as ctx:
        sb = lambda n, s, d=F32: ctx.enter_context(nc.sbuf_tensor(f"painn_{n}", s, d))
        ps = lambda n, s: ctx.enter_context(nc.psum_tensor(f"painn_{n}", s, F32))
        tabs = sb("tabs", [P, ET, TAB])
        w_in_sb = sb("w_in_sb", [B, 2, F])
        o1s_raw = sb("o1s_raw", [P, B])
        o1v_raw = sb("o1v_raw", [2 * F, B])
        o1s = sb("o1s", [P, B])
        o1v = sb("o1v", [2 * F, B])
        o2s = sb("o2s", [B, B])
        o2v = sb("o2v", [B, B])
        ident = sb("ident", [P, P])
        last_row = sb("last_row", [P, 1])
        half = sb("half", [P, 1])
        keys = sb("keys", [P, ET + 1])
        key_rows = sb("key_rows", [P, EP])
        x_dst = [sb(f"x_dst{s}", [P, D]) for s in range(RING)]
        x_kept = sb("x_kept", [P, ET * D])
        z = sb("z", [P, ET * D])
        u = [sb(f"u{s}", [P, 8 * F]) for s in range(RING)]
        x_t = sb("x_t", [B, 4, P])
        feat = sb("feat", [P, 4, F])
        mask = sb("mask", [P, 2, P])
        msg = sb("msg", [P, M_COLS])
        sums = [sb(f"sums{s}", [P, M_COLS]) for s in range(2)]
        sums_t = sb("sums_t", [P, 4, P])
        hid = [sb(f"hid{s}", [B, 3, P]) for s in range(RING)]
        hid_s = sb("hid_s", [B, RING, P])
        soft = sb("soft", [B, RING, P])
        scal = sb("scal", [B, RING, P])
        stats = sb("stats", [P, RING, 2, 6])
        mv = sb("mv", [P, RING, 2, 2])
        log_var = sb("log_var", [P, RING, 2])
        eps = sb("eps", [P, 1])
        rstd = sb("rstd", [P, RING, 2])
        shift = sb("shift", [P, RING, 2])
        normed = [sb(f"normed{s}", [P, 2, D]) for s in range(RING)]
        x_ps = ps("x_ps", [B, 4, P])
        feat_ps = ps("feat_ps", [P, 4, F])
        sum_ps = ps("sum_ps", [P, M_COLS])
        sums_t_ps = ps("sums_t_ps", [P, 4, P])
        o1_ps = ps("o1_ps", [B, 4, P])
        o2_ps = ps("o2_ps", [P, 4, B])

        tabs_in = sem("painn_tabs_in")
        w_in = sem("painn_w_in")
        keys_in = sem("painn_keys_in")
        w_scaled = sem("painn_w_scaled")
        const_done = sem("painn_const_done")
        zeroed = sem("painn_zeroed")
        x_in = [sem(f"painn_x_in{s}") for s in range(RING)]
        kept = sem("painn_kept")
        x_turned = sem("painn_x_turned")
        xt_out = sem("painn_xt_out")
        feat_done = sem("painn_feat_done")
        feat_out = sem("painn_feat_out")
        masks_done = sem("painn_masks_done")
        msg_done = sem("painn_msg_done")
        summed = sem("painn_summed")
        sums_out = sem("painn_sums_out")
        sums_turned = sem("painn_sums_turned")
        st_out = sem("painn_st_out")
        o1_done = sem("painn_o1_done")
        o1_out = sem("painn_o1_out")
        soft_steps = sem("painn_soft_steps")
        scal_done = sem("painn_scal_done")
        o2_done = sem("painn_o2_done")
        z_done = sem("painn_z_done")
        ln = sem("painn_ln")
        logged = sem("painn_logged")
        rooted = sem("painn_rooted")
        own_done = sem("painn_own_done")
        far_done = sem("painn_far_done")
        stored = sem("painn_stored")
        freed = sem("painn_freed")
        passed = sem("painn_passed")
        LN_STEPS = RING + 2

        with nc.Block() as block:

            @block.sync
            def _(sp):
                sp.dma_start(tabs[:, :, :], tab_s.rearrange("(t p) k -> p t k", p=P)).then_inc(tabs_in, 16)
                sp.dma_start(w_in_sb[:, :, :], w_in_d).then_inc(w_in, 16)
                sp.dma_start(key_rows[:, :], row_s[1:EP + 1].partition_broadcast(P)).then_inc(keys_in, 16)
                sp.dma_start(o1s_raw[0:F, :], w_o1s[0:F, :]).then_inc(w_in, 16)
                for c in range(3):
                    sp.dma_start(o1s_raw[(1 + c) * F:(2 + c) * F, :], w_o1s[F:2 * F, :]).then_inc(w_in, 16)
                sp.dma_start(o1v_raw[:, :], w_o1v).then_inc(w_in, 16)
                sp.dma_start(o2s[:, :], w_o2s).then_inc(w_in, 16)
                sp.dma_start(o2v[:, :], w_o2v).then_inc(w_in, 16)
                sp.sem_inc(freed, RING)
                halves = x3_rows.rearrange("(a e) n -> a e n", a=2)
                with sp.Fori(0, GROUPS) as i:
                    for s in range(RING):
                        t = RING * i + s
                        sp.wait_ge(own_done, t + 2)
                        sp.sem_inc(passed, 1)
                        sp.wait_ge(far_done, t + 2)
                        sp.sem_inc(passed, 1)
                        sp.dma_start(halves[:, bass.ds(t * P, P), :].rearrange("a p n -> p a n"),
                                     normed[s][:, :, :]).then_inc(stored, 16)
                        sp.wait_ge(stored, 16 * (t + 1))
                        sp.sem_inc(freed, 1)

            @block.gpsimd
            def _(pool):
                pool.memset(ident[:, :], 0.0).then_inc(const_done, 1)
                pool.memset(last_row[:, :], 0.0).then_inc(const_done, 1)
                pool.memset(half[:, :], 0.5).then_inc(const_done, 1)
                pool.memset(eps[:, :], EPS).then_inc(const_done, 1)
                pool.wait_ge(const_done, 4)
                pool.affine_select(out=ident[:, :], in_=ident[:, :], compare_op=ALU.not_equal, fill=1.0,
                                   base=0, pattern=[[-1, P]], channel_multiplier=1).then_inc(const_done, 1)
                pool.affine_select(out=last_row[:, :], in_=last_row[:, :], compare_op=ALU.not_equal, fill=1.0,
                                   base=1 - P, pattern=[[0, 1]], channel_multiplier=1).then_inc(const_done, 1)
                pool.wait_ge(tabs_in, 16)
                index = lambda t, k: bass.IndirectOffsetOnAxis(tabs[:, t, k:k + 1].bitcast(I32), 0)

                def keep(t):
                    pool.wait_ge(x_in[t % RING], 48 * (t // RING + 1))
                    pool.tensor_copy(x_kept[:, t * D:(t + 1) * D], x_dst[t % RING][:, :]).then_inc(kept, 1)

                for t in range(ET):
                    s = t % RING
                    if t >= RING:
                        keep(t - RING)
                        pool.wait_ge(kept, t - RING + 1)
                        pool.wait_ge(x_turned, t - RING + 1)
                        pool.wait_ge(msg_done, 3 * (t - RING + 1) + 1)
                    pool.indirect_dma_start(x_dst[s][:, :], None, x2_rows,
                                            index(t, S_X2DST)).then_inc(x_in[s], 16)
                    pool.indirect_dma_start(u[s][:, :], None, u_tab, index(t, S_EDGE)).then_inc(x_in[s], 16)
                    pool.indirect_dma_start(z[:, t * D:(t + 1) * D], None, x2_rows, index(t, S_X2SRC)).then_inc(x_in[s], 16)
                for t in range(ET - RING, ET):
                    keep(t)

            @block.tensor
            def _(pe):
                for done in (feat_done, o1_done, summed):
                    pe.sem_inc(done, 1)
                pe.sem_inc(o2_done, RING)
                pe.wait_ge(const_done, 6)
                pe.wait_ge(zeroed, 2)

                def turn_x(i, s):
                    t = RING * i + s
                    pe.wait_ge(x_in[s], 48 * (i + 1))
                    pe.wait_ge(xt_out, t + 1)
                    pe.transpose(x_ps[:, 0, :], x_dst[s][:, 0:B], ident[:, :])
                    vec = x_dst[s][:, B:D].rearrange("p (b c) -> p c b", c=3)
                    for c in range(3):
                        last = pe.transpose(x_ps[:, 1 + c, :], vec[:, c, :], ident[:, :])
                    last.then_inc(x_turned, 1)

                def features(i, s):
                    t = RING * i + s
                    pe.wait_ge(xt_out, t + 2)
                    pe.wait_ge(feat_out, t + 1)
                    for c in range(4):
                        last = pe.matmul(feat_ps[:, c, :], x_t[:, c, :], w_in_sb[:, min(c, 1), :], start=True, stop=True)
                    last.then_inc(feat_done, 1)

                def sum_edges(i, s):
                    t = RING * i + s
                    pe.wait_ge(masks_done, t + 1)
                    pe.wait_ge(msg_done, 3 * t + 4)
                    pe.wait_ge(sums_out, t + 1)
                    pe.matmul(sum_ps[:, :], mask[:, 0, :], msg[:, :], start=True, stop=False)
                    pe.matmul(sum_ps[:, :], mask[:, 1, :], sums[(s + 1) % 2][:, :], start=False, stop=True).then_inc(summed, 1)

                def turn_sums(i, s):
                    t = RING * i + s
                    pe.wait_ge(sums_out, t + 2)
                    pe.wait_ge(st_out, 2 * t + 1)
                    pe.transpose(sums_t_ps[:, 0, :], sums[s % 2][:, 0:4 * F], ident[:, :])
                    for c in range(3):
                        last = pe.transpose(sums_t_ps[0:2 * F, 1 + c, :], sums[s % 2][:, (4 + 2 * c) * F:(6 + 2 * c) * F],
                                            ident[:, :])
                    last.then_inc(sums_turned, 1)

                def out_one(i, s):
                    t = RING * i + s
                    pe.wait_ge(st_out, 2 * t + 3)
                    pe.wait_ge(o1_out, t + 1)
                    pe.matmul(o1_ps[:, 0, :], o1s[:, :], sums_t[:, 0, :], start=True, stop=True)
                    pe.matmul(o1_ps[:, 1:4, :], o1v[:, :], sums_t[0:2 * F, 1:4, :], start=True, stop=True).then_inc(o1_done, 1)

                def out_two(i, s):
                    t = RING * i + s
                    pe.wait_ge(o1_out, t + 2)
                    pe.wait_ge(z_done, t + 1)
                    for c in range(3):
                        pe.matmul(o2_ps[:, 1 + c, :], hid[s][:, c, :], o2v[:, :], start=True, stop=True)
                    pe.wait_ge(scal_done, i + 2)
                    pe.matmul(o2_ps[:, 0, :], scal[:, s, :], o2s[:, :], start=True, stop=True).then_inc(o2_done, 1)

                pe.wait_ge(w_in, 16 * 8)
                turn_x(0, 0)
                features(0, 0)
                sum_edges(0, 0)
                pe.wait_ge(w_scaled, 2)

                def body(i, own=True, last=False, before=True):
                    for s in range(RING):
                        nxt = (i, s + 1) if s < RING - 1 else (i + 1, 0)
                        if not own or (last and s == RING - 1):
                            nxt = None
                        if nxt:
                            turn_x(*nxt)
                        if own:
                            turn_sums(i, s)
                        if nxt:
                            features(*nxt)
                        if before:
                            out_two(i - 1, s)
                        if own:
                            out_one(i, s)
                        if nxt:
                            sum_edges(*nxt)

                body(0, before=False)
                with pe.Fori(1, GROUPS - 1) as i:
                    body(i)
                body(GROUPS - 1, last=True)
                body(GROUPS, own=False)

            @block.scalar
            def _(act):
                for done in (xt_out, feat_out, sums_out, st_out, o1_out, own_done):
                    act.sem_inc(done, 1)
                act.wait_ge(const_done, 6)

                act.preload_act_table_set("natural_log_exp_and_others")

                def copy_xt(i, s):
                    t = RING * i + s
                    act.wait_ge(x_turned, t + 1)
                    act.wait_ge(feat_done, t + 1)
                    act.activation(x_t[:, :, :], x_ps[:, :, :], ACT.Copy).then_inc(xt_out, 1)

                def copy_features(i, s):
                    t = RING * i + s
                    act.wait_ge(feat_done, t + 2)
                    act.wait_ge(msg_done, 3 * t + 1)
                    act.activation(feat[:, :, :], feat_ps[:, :, :], ACT.Copy, scale=B ** -0.5).then_inc(feat_out, 1)

                def copy_sums(i, s):
                    t = RING * i + s
                    act.wait_ge(summed, t + 2)
                    act.activation(sums[s % 2][:, :], sum_ps[:, :], ACT.Copy).then_inc(sums_out, 1)

                def copy_sums_t(i, s):
                    t = RING * i + s
                    act.wait_ge(sums_turned, t + 1)
                    act.wait_ge(o1_done, t + 1)
                    act.activation(sums_t[:, 0, :], sums_t_ps[:, 0, :], ACT.Copy).then_inc(st_out, 1)
                    act.activation(sums_t[0:2 * F, 1:4, :], sums_t_ps[0:2 * F, 1:4, :], ACT.Copy).then_inc(st_out, 1)

                def copy_hidden(i, s):
                    t = RING * i + s
                    act.wait_ge(o1_done, t + 2)
                    act.wait_ge(o2_done, t + 1)
                    act.wait_ge(scal_done, i + 1)
                    act.activation(hid_s[:, s, :], o1_ps[:, 0, :], ACT.Copy)
                    act.activation(hid[s][:, :, :], o1_ps[:, 1:4, :], ACT.Copy).then_inc(o1_out, 1)

                def softplus(i):
                    act.wait_ge(o1_out, RING * (i + 1) + 1)
                    act.activation(soft[:, :, :], hid_s[:, :, :], ACT.Abs).then_inc(soft_steps, 1)
                    act.wait_ge(soft_steps, 3 * i + 1)
                    act.activation(soft[:, :, :], soft[:, :, :], ACT.Exp, scale=-1.0).then_inc(soft_steps, 1)
                    act.wait_ge(soft_steps, 3 * i + 2)
                    act.activation(soft[:, :, :], soft[:, :, :], ACT.Ln, bias=half[:, 0:1], scale=0.5).then_inc(soft_steps, 1)

                def root(i):
                    act.wait_ge(ln, LN_STEPS * i + RING + 1)
                    act.activation(log_var[:, :, :], mv[:, :, :, 1], ACT.Ln, bias=eps[:, 0:1]).then_inc(logged, 1)
                    act.wait_ge(logged, i + 1)
                    act.wait_ge(own_done, RING * i + 1)
                    act.wait_ge(far_done, RING * i + 1)
                    act.activation(rstd[:, :, :], log_var[:, :, :], ACT.Exp, scale=-0.5).then_inc(rooted, 1)

                def normalize(i, s):
                    t = RING * i + s
                    act.wait_ge(ln, LN_STEPS * (i + 1))
                    act.wait_ge(freed, t + 1)
                    act.activation(normed[s][:, 0, :], z[:, bass.ds(t * D, D)], ACT.Identity,
                                   bias=shift[:, s, 0:1], scale=rstd[:, s, 0:1]).then_inc(own_done, 1)

                copy_xt(0, 0)
                copy_features(0, 0)

                def body(i, own=True, last=False, before=True, older=True):
                    for s in range(RING):
                        nxt = (i, s + 1) if s < RING - 1 else (i + 1, 0)
                        if not own or (last and s == RING - 1):
                            nxt = None
                        if own:
                            copy_sums(i, s)
                        if nxt:
                            copy_xt(*nxt)
                        if own:
                            copy_sums_t(i, s)
                        if nxt:
                            copy_features(*nxt)
                        if own:
                            copy_hidden(i, s)
                        if older:
                            if s == 0:
                                root(i - 2)
                            for e in NORMALIZED[s]:
                                normalize(i - 2, e)
                    if own:
                        softplus(i)

                body(0, before=False, older=False)
                body(1, older=False)
                with act.Fori(2, GROUPS - 1) as i:
                    body(i)
                body(GROUPS - 1, last=True)
                body(GROUPS, own=False)
                body(GROUPS + 1, own=False, before=False)

            @block.vector
            def _(dve):
                for done in (msg_done, scal_done, z_done, far_done):
                    dve.sem_inc(done, 1)
                dve.memset(keys[:, 0:1], -5.0)
                for s in range(2):
                    dve.memset(sums[s][:, :], 0.0).then_inc(zeroed, 1)
                def masks(i, s):
                    t = RING * i + s
                    dve.wait_ge(summed, t + 1)
                    row = key_rows[:, bass.ds(t * P, P)]
                    dve.tensor_scalar(mask[:, 0, :], row, keys[:, bass.ds(t + 1, 1)], None, ALU.is_equal)
                    dve.tensor_scalar(mask[:, 1, :], row, keys[:, bass.ds(t, 1)], last_row[:, 0:1],
                                      ALU.is_equal, ALU.mult).then_inc(masks_done, 1)

                def messages(i, s):
                    t = RING * i + s
                    dve.wait_ge(x_in[s], 48 * (i + 1))
                    dve.wait_ge(feat_out, t + 2)
                    dve.wait_ge(summed, t + 1)
                    flat = feat[:, :, :].rearrange("p c f -> p (c f)")
                    dve.tensor_tensor(msg[:, 0:4 * F], flat, u[s][:, 0:4 * F], ALU.mult).then_inc(msg_done, 1)
                    pairs = msg[:, 4 * F:].rearrange("p (c k f) -> p k c f", c=3, k=2)
                    dve.tensor_tensor(pairs[:, 0, :, :], feat[:, 0:1, :].to_broadcast([P, 3, F]),
                                      u[s][:, 4 * F:7 * F].rearrange("p (c f) -> p c f", c=3), ALU.mult).then_inc(msg_done, 1)
                    dve.tensor_tensor(pairs[:, 1, :, :], feat[:, 1:4, :],
                                      u[s][:, 7 * F:8 * F].rearrange("p (c f) -> p c f", c=1).to_broadcast([P, 3, F]),
                                      ALU.mult).then_inc(msg_done, 1)

                def scalars(i):
                    dve.wait_ge(soft_steps, 3 * i + 3)
                    dve.wait_ge(o2_done, RING * (i + 1))
                    dve.scalar_tensor_tensor(scal[:, :, :], hid_s[:, :, :], 0.0, soft[:, :, :],
                                             ALU.max, ALU.add).then_inc(scal_done, 1)

                def add(i, s):
                    t = RING * i + s
                    dve.wait_ge(o2_done, t + 1 + RING)
                    dve.wait_ge(x_in[s], 48 * (i + 1))
                    own = z[:, bass.ds(t * D, B)]
                    dve.scalar_tensor_tensor(own, o2_ps[:, 0, :], B ** -0.5, own, ALU.mult, ALU.add)
                    vec = z[:, bass.ds(t * D + B, 3 * B)].rearrange("p (d c) -> p c d", c=3)
                    dve.scalar_tensor_tensor(vec, o2_ps[:, 1:4, :], B ** -0.5, vec, ALU.mult, ALU.add).then_inc(z_done, 1)
                    dve.wait_ge(kept, t + 1)
                    dve.sem_inc(passed, 1)
                    dve.bn_stats(stats[:, s, 1, :], x_kept[:, bass.ds(t * D, D)])
                    dve.wait_ge(z_done, t + 2)
                    dve.sem_inc(passed, 1)
                    dve.bn_stats(stats[:, s, 0, :], z[:, bass.ds(t * D, D)]).then_inc(ln, 1)

                def factors(i):
                    k = LN_STEPS * i + RING
                    dve.wait_ge(ln, k)
                    dve.sem_inc(passed, 1)
                    for s in range(RING):
                        for n in range(2):
                            last = dve.bn_aggr(mv[:, s, n, :], stats[:, s, n, :])
                    last.then_inc(ln, 1)
                    dve.wait_ge(rooted, i + 1)
                    dve.wait_ge(own_done, RING * i + 1)
                    dve.scalar_tensor_tensor(shift[:, :, :], mv[:, :, :, 0], -1.0, rstd[:, :, :],
                                             ALU.mult, ALU.mult).then_inc(ln, 1)

                def normalize(i, s):
                    t = RING * i + s
                    dve.wait_ge(ln, LN_STEPS * (i + 1))
                    dve.wait_ge(freed, t + 1)
                    dve.tensor_scalar(normed[s][:, 1, :], x_kept[:, bass.ds(t * D, D)], rstd[:, s, 1:2],
                                      shift[:, s, 1:2], ALU.mult, ALU.add).then_inc(far_done, 1)

                dve.wait_ge(tabs_in, 16)
                dve.tensor_copy(keys[:, 1:ET + 1], tabs[:, :, KEY]).then_inc(keys_in, 1)
                dve.wait_ge(keys_in, 17)
                dve.wait_ge(const_done, 6)
                masks(0, 0)
                messages(0, 0)
                dve.wait_ge(w_in, 16 * 8)
                dve.tensor_scalar(o1s[:, :], o1s_raw[:, :], (2 * F) ** -0.5, None, ALU.mult).then_inc(w_scaled, 1)
                dve.tensor_scalar(o1v[:, :], o1v_raw[:, :], (2 * F) ** -0.5, None, ALU.mult).then_inc(w_scaled, 1)

                def body(i, own=True, last=False, before=True, older=True):
                    for s in range(RING):
                        nxt = (i, s + 1) if s < RING - 1 else (i + 1, 0)
                        if own and not (last and s == RING - 1):
                            masks(*nxt)
                            messages(*nxt)
                        if older and s == 0:
                            factors(i - 2)
                        if before:
                            add(i - 1, s)
                        if older:
                            for e in NORMALIZED[s]:
                                normalize(i - 2, e)
                    if own:
                        scalars(i)

                body(0, before=False, older=False)
                body(1, older=False)
                with dve.Fori(2, GROUPS - 1) as i:
                    body(i)
                body(GROUPS - 1, last=True)
                body(GROUPS, own=False)
                body(GROUPS + 1, own=False, before=False)


def mlp_edges(nc, sem, x3_rows, row_s, tab_s, w_t, b, y_rows):
    RING = 4
    KC = 2 * D // P
    with ExitStack() as ctx:
        sb = lambda n, s, d=F32: ctx.enter_context(nc.sbuf_tensor(f"mlp_{n}", s, d))
        ps = lambda n, s: ctx.enter_context(nc.psum_tensor(f"mlp_{n}", s, F32))
        tabs = sb("tabs", [P, ET, TAB])
        w_raw = sb("w_raw", [P, 2, D])
        w_hi = sb("w_hi", [P, KC, D], F32R)
        w_lo = sb("w_lo", [P, KC, D], F32R)
        b_rows = sb("b_rows", [P, D])
        ident = sb("ident", [P, P])
        last_row = sb("last_row", [P, 1])
        keys = sb("keys", [P, ET + 1])
        key_rows = sb("key_rows", [P, EP])
        pair = [sb(f"pair{s}", [P, 2, D]) for s in range(RING)]
        mask = [sb(f"mask{s}", [P, 2, P]) for s in range(2)]
        t_hi = [sb(f"t_hi{s}", [P, KC, P], F32R) for s in range(2)]
        t_lo = [sb(f"t_lo{s}", [P, KC, P], F32R) for s in range(2)]
        pre = [sb(f"pre{s}", [P, D]) for s in range(2)]
        msg = [sb(f"msg{s}", [P, D]) for s in range(2)]
        sums = [sb(f"sums{s}", [P, D]) for s in range(2)]
        own = [sb(f"own{s}", [P, D]) for s in range(RING)]
        z = [sb(f"z{s}", [P, D]) for s in range(2)]
        stats = [sb(f"stats{s}", [P, 6]) for s in range(2)]
        mv = [sb(f"mv{s}", [P, 2]) for s in range(2)]
        var = [sb(f"var{s}", [P, 1]) for s in range(2)]
        inv = [sb(f"inv{s}", [P, 1]) for s in range(2)]
        rstd = [sb(f"rstd{s}", [P, 1]) for s in range(2)]
        shift = [sb(f"shift{s}", [P, 1]) for s in range(2)]
        y = [sb(f"y{s}", [P, D]) for s in range(RING)]
        t_ps = [ps(f"t_ps{s}", [P, KC // 2, P]) for s in range(2)]
        m_ps = [ps(f"m_ps{s}", [P, D]) for s in range(2)]
        sum_ps = [ps(f"sum_ps{s}", [P, D]) for s in range(2)]

        tabs_in = sem("mlp_tabs_in")
        keys_in = sem("mlp_keys_in")
        b_in = sem("mlp_b_in")
        w_in = [sem(f"mlp_w_in{s}") for s in range(2)]
        w_hi_done = sem("mlp_w_hi_done")
        w_lo_done = sem("mlp_w_lo_done")
        const_done = sem("mlp_const_done")
        zeroed = sem("mlp_zeroed")
        pair_in = [sem(f"mlp_pair_in{s}") for s in range(RING)]
        turned = sem("mlp_turned")
        hi_done = sem("mlp_hi_done")
        lo_done = sem("mlp_lo_done")
        multiplied = sem("mlp_multiplied")
        pre_done = sem("mlp_pre_done")
        msg_done = sem("mlp_msg_done")
        masks_done = sem("mlp_masks_done")
        summed = sem("mlp_summed")
        sums_out = sem("mlp_sums_out")
        own_done = sem("mlp_own_done")
        z_done = sem("mlp_z_done")
        ln = sem("mlp_ln")
        rooted = sem("mlp_rooted")
        y_done = sem("mlp_y_done")
        y_scattered = sem("mlp_y_scattered")
        y_freed = sem("mlp_y_freed")
        passed = sem("mlp_passed")
        LN_STEPS = 5

        with nc.Block() as block:

            @block.sync
            def _(sp):
                sp.dma_start(tabs[:, :, :], tab_s.rearrange("(t p) k -> p t k", p=P)).then_inc(tabs_in, 16)
                for k in range(2):
                    sp.dma_start(w_raw[:, k, :], w_t[k * P:(k + 1) * P, :]).then_inc(w_in[k], 16)
                sp.dma_start(key_rows[:, :], row_s[1:EP + 1].partition_broadcast(P)).then_inc(keys_in, 16)
                sp.dma_start(b_rows[:, :], b.partition_broadcast(P)).then_inc(b_in, 16)
                for k in range(2, KC):
                    sp.wait_ge(w_lo_done, k - 1)
                    sp.dma_start(w_raw[:, k % 2, :], w_t[k * P:(k + 1) * P, :]).then_inc(w_in[k % 2], 16)

            @block.gpsimd
            def _(pool):
                pool.memset(ident[:, :], 0.0).then_inc(const_done, 1)
                pool.memset(last_row[:, :], 0.0).then_inc(const_done, 1)
                pool.wait_ge(const_done, 2)
                pool.affine_select(out=ident[:, :], in_=ident[:, :], compare_op=ALU.not_equal, fill=1.0,
                                   base=0, pattern=[[-1, P]], channel_multiplier=1).then_inc(const_done, 1)
                pool.affine_select(out=last_row[:, :], in_=last_row[:, :], compare_op=ALU.not_equal, fill=1.0,
                                   base=1 - P, pattern=[[0, 1]], channel_multiplier=1).then_inc(const_done, 1)
                pool.sem_inc(y_freed, RING)
                pool.wait_ge(tabs_in, 16)
                index = lambda t, k: bass.IndirectOffsetOnAxis(tabs[:, t, k:k + 1].bitcast(I32), 0)
                for t in range(ET + RING):
                    s = t % RING
                    if t < ET:
                        if t >= RING:
                            pool.wait_ge(turned, 2 * (t - RING + 1))
                            pool.wait_ge(own_done, t - RING + 1)
                        pool.indirect_dma_start(pair[s][:, 0, :], None, x3_rows, index(t, S_X3SRC)).then_inc(pair_in[s], 16)
                        pool.indirect_dma_start(pair[s][:, 1, :], None, x3_rows, index(t, S_X3DST)).then_inc(pair_in[s], 16)
                    if t >= RING:
                        e = t - RING
                        if e:
                            pool.wait_ge(y_scattered, 16 * e)
                            pool.sem_inc(y_freed, 1)
                        pool.wait_ge(y_done, e + 3)
                        pool.indirect_dma_start(y_rows, index(e, S_OUT), y[s][:, :], None).then_inc(y_scattered, 16)
                pool.wait_ge(y_scattered, 16 * ET)

            @block.tensor
            def _(pe):
                pe.sem_inc(multiplied, 2)
                pe.sem_inc(summed, 2)
                pe.wait_ge(const_done, 4)

                def turn(i, s):
                    t = RING * i + s
                    pe.wait_ge(pair_in[s], 32 * (i + 1))
                    for n in range(2):
                        pe.wait_ge(lo_done, 2 * t + n + 1)
                        for k in range(KC // 2):
                            last = pe.transpose(t_ps[n][:, k, :], pair[s][:, n, k * P:(k + 1) * P], ident[:, :])
                        last.then_inc(turned, 1)

                def product(i, s, peeled=False):
                    t = RING * i + s
                    q = s % 2
                    pe.wait_ge(pre_done, t + 1)
                    for k in range(KC):
                        if k % (KC // 2) == 0:
                            pe.wait_ge(lo_done, 2 * t + 4 if k else 2 * t + 3)
                        if peeled:
                            pe.wait_ge(w_lo_done, k + 1)
                        pe.matmul(m_ps[q][:, :], t_hi[q][:, k, :], w_hi[:, k, :], start=(k == 0), stop=False)
                        pe.matmul(m_ps[q][:, :], t_hi[q][:, k, :], w_lo[:, k, :], start=False, stop=False)
                        last = pe.matmul(m_ps[q][:, :], t_lo[q][:, k, :], w_hi[:, k, :], start=False, stop=(k == KC - 1))
                    last.then_inc(multiplied, 1)

                def sum_edges(i, s):
                    t = RING * i + s
                    q = s % 2
                    pe.wait_ge(masks_done, t + 1)
                    pe.wait_ge(msg_done, t + 3)
                    pe.wait_ge(sums_out, t + 1)
                    pe.matmul(sum_ps[q][:, :], mask[q][:, 0, :], msg[q][:, :], start=True, stop=False)
                    pe.wait_ge(sums_out, t + 2)
                    pe.matmul(sum_ps[q][:, :], mask[q][:, 1, :], sums[1 - q][:, :], start=False, stop=True).then_inc(summed, 1)

                pe.wait_ge(zeroed, 1)
                turn(0, 0)
                turn(0, 1)
                product(0, 0, peeled=True)

                def body(i, last):
                    for s in range(RING):
                        if s + 2 < RING:
                            turn(i, s + 2)
                        elif not last:
                            turn(i + 1, s + 2 - RING)
                        if s + 1 < RING:
                            product(i, s + 1)
                        elif not last:
                            product(i + 1, 0)
                        sum_edges(i, s)

                with pe.Fori(0, ET // RING - 1) as i:
                    body(i, False)
                body(ET // RING - 1, True)

            @block.scalar
            def _(act):
                act.sem_inc(sums_out, 2)
                act.sem_inc(msg_done, 2)
                act.sem_inc(y_done, 2)

                def relu(i, s):
                    t = RING * i + s
                    act.wait_ge(pre_done, t + 3)
                    act.wait_ge(summed, t + 1)
                    act.activation(msg[s % 2][:, :], pre[s % 2][:, :], ACT.Relu).then_inc(msg_done, 1)

                def copy_sums(i, s):
                    t = RING * i + s
                    act.wait_ge(summed, t + 3)
                    act.wait_ge(z_done, t + 3)
                    act.activation(sums[s % 2][:, :], sum_ps[s % 2][:, :], ACT.Copy).then_inc(sums_out, 1)

                def normalize(i, s):
                    t = RING * i + s
                    q = s % 2
                    act.wait_ge(ln, LN_STEPS * t + 4)
                    act.activation(rstd[q][:, :], inv[q][:, :], ACT.Sqrt).then_inc(rooted, 1)
                    act.wait_ge(ln, LN_STEPS * t + 5)
                    act.wait_ge(y_freed, t + 1)
                    act.activation(y[s][:, :], z[q][:, :], ACT.Identity, bias=shift[q][:, 0:1],
                                   scale=rstd[q][:, 0:1]).then_inc(y_done, 1)

                def keep(i, s):
                    t = RING * i + s
                    act.wait_ge(pair_in[s], 32 * (i + 1))
                    act.wait_ge(z_done, t + 1)
                    act.activation(own[s][:, :], pair[s][:, 0, :], ACT.Copy).then_inc(own_done, 1)

                keep(0, 0)
                keep(0, 1)
                relu(0, 0)

                def body(i, last):
                    for s in range(RING):
                        if s + 2 < RING:
                            keep(i, s + 2)
                        elif not last:
                            keep(i + 1, s + 2 - RING)
                        if s + 1 < RING:
                            relu(i, s + 1)
                        elif not last:
                            relu(i + 1, 0)
                        copy_sums(i, s)
                        normalize(i, s)

                with act.Fori(0, ET // RING - 1) as i:
                    body(i, False)
                body(ET // RING - 1, True)

            @block.vector
            def _(dve):
                dve.sem_inc(lo_done, 2)
                dve.sem_inc(pre_done, 2)
                dve.sem_inc(z_done, 4)
                dve.memset(sums[1][:, :], 0.0).then_inc(zeroed, 1)
                dve.memset(keys[:, 0:1], -5.0)
                def split(i, s):
                    t = RING * i + s
                    q = s % 2
                    dve.wait_ge(multiplied, t + 1)
                    for n in range(2):
                        ks = slice(n * KC // 2, (n + 1) * KC // 2)
                        dve.wait_ge(turned, 2 * t + n + 1)
                        dve.tensor_copy(t_hi[q][:, ks, :], t_ps[n][:, :, :]).then_inc(hi_done, 1)
                        dve.wait_ge(hi_done, 2 * t + n + 1)
                        dve.tensor_tensor(t_lo[q][:, ks, :], t_ps[n][:, :, :], t_hi[q][:, ks, :].bitcast(F32),
                                          ALU.subtract).then_inc(lo_done, 1)

                def masks(i, s):
                    t = RING * i + s
                    dve.wait_ge(summed, t + 1)
                    m = mask[s % 2]
                    row = key_rows[:, bass.ds(t * P, P)]
                    dve.tensor_scalar(m[:, 0, :], row, keys[:, bass.ds(t + 1, 1)], None, ALU.is_equal)
                    dve.tensor_scalar(m[:, 1, :], row, keys[:, bass.ds(t, 1)], last_row[:, 0:1],
                                      ALU.is_equal, ALU.mult).then_inc(masks_done, 1)

                def add_bias(i, s):
                    t = RING * i + s
                    dve.wait_ge(multiplied, t + 3)
                    dve.wait_ge(msg_done, t + 1)
                    dve.tensor_tensor(pre[s % 2][:, :], m_ps[s % 2][:, :], b_rows[:, :], ALU.add).then_inc(pre_done, 1)

                def finish(i, s):
                    t = RING * i + s
                    q = s % 2
                    dve.wait_ge(sums_out, t + 3)
                    dve.wait_ge(own_done, t + 1)
                    dve.wait_ge(y_done, t + 1)
                    dve.tensor_tensor(z[q][:, :], sums[q][:, :], own[s][:, :], ALU.add).then_inc(z_done, 1)
                    dve.wait_ge(z_done, t + 5)
                    dve.bn_stats(stats[q][:, :], z[q][:, :]).then_inc(ln, 1)
                    dve.wait_ge(ln, LN_STEPS * t + 1)
                    dve.sem_inc(passed, 1)
                    dve.bn_aggr(mv[q][:, :], stats[q][:, :]).then_inc(ln, 1)
                    dve.wait_ge(ln, LN_STEPS * t + 2)
                    dve.tensor_scalar(var[q][:, :], mv[q][:, 1:2], EPS, None, ALU.add).then_inc(ln, 1)
                    dve.wait_ge(ln, LN_STEPS * t + 3)
                    dve.reciprocal(inv[q][:, :], var[q][:, :]).then_inc(ln, 1)
                    dve.wait_ge(rooted, t + 1)
                    dve.scalar_tensor_tensor(shift[q][:, :], mv[q][:, 0:1], -1.0, rstd[q][:, :],
                                             ALU.mult, ALU.mult).then_inc(ln, 1)

                split(0, 0)
                split(0, 1)
                for k in range(KC):
                    dve.wait_ge(w_in[k % 2], 16 * (k // 2 + 1))
                    dve.tensor_copy(w_hi[:, k, :], w_raw[:, k % 2, :]).then_inc(w_hi_done, 1)
                    dve.wait_ge(w_hi_done, k + 1)
                    dve.tensor_tensor(w_lo[:, k, :], w_raw[:, k % 2, :], w_hi[:, k, :].bitcast(F32),
                                      ALU.subtract).then_inc(w_lo_done, 1)
                dve.wait_ge(tabs_in, 16)
                dve.tensor_copy(keys[:, 1:ET + 1], tabs[:, :, KEY]).then_inc(keys_in, 1)
                dve.wait_ge(keys_in, 17)
                dve.wait_ge(b_in, 16)
                dve.wait_ge(const_done, 4)
                masks(0, 0)
                add_bias(0, 0)

                def body(i, last):
                    for s in range(RING):
                        if s + 2 < RING:
                            split(i, s + 2)
                        elif not last:
                            split(i + 1, s + 2 - RING)
                        if s + 1 < RING:
                            masks(i, s + 1)
                            add_bias(i, s + 1)
                        elif not last:
                            masks(i + 1, 0)
                            add_bias(i + 1, 0)
                        finish(i, s)

                with dve.Fori(0, ET // RING - 1) as i:
                    body(i, False)
                body(ET // RING - 1, True)


def graph_layers(nc, x_t, x, ends_row, ends_col, ew_col, attr20_t, attr4_col, w1, a1, b1, w2, a2, b2, wfc, bfc,
                 conv_w, w_in, pw1, pb1, pw2b, w_o1s, w_o1v, w_o2s, w_o2v, mlp_w_t, mlp_b, out):
    table = lambda n, s: nc.dram_tensor(n, s, F32, kind="Internal").ap()
    rec_d, rec_s = table("rec_d", [EP + 1, REC]), table("rec_s", [EP + 1, REC])
    row_d, row_s = table("row_d", [EP + 2]), table("row_s", [EP + 2])
    map_d, map_s = table("map_d", [NT, 1]), table("map_s", [NT, 1])
    tab_d, tab_s = table("tab_d", [EP, TAB]), table("tab_s", [EP, TAB])
    h1, al1 = table("h1", [NT, HC]), table("al1", [NP, 2 * H])
    h2, al2 = table("h2", [NT, HC]), table("al2", [NP, 2 * H])
    bounce1, bounce2 = table("bounce1", [2, H * ET, P]), table("bounce2", [2, H * ET, P])
    x1 = table("x1", [NP, D])
    x2, x3 = table("x2", [2 * EP, D]), table("x3", [2 * EP, D])
    u_tab = table("u_tab", [EP, 256])
    def stage(build, *args):
        held = []

        def sem(name):
            held.append(nc.alloc_semaphore(name=name))
            return held[-1]

        build(nc, sem, *args)
        nc.clear_and_free_semaphores(held)
        nc.all_engine_barrier()

    stage(dense_and_prep, x_t, w1, a1, h1, al1, ends_row, ends_col, ew_col, rec_d, rec_s, row_d, row_s, map_d, map_s,
          tab_d, tab_s, attr20_t, pw1, pb1, pw2b, attr4_col, u_tab)
    stage(gat_edges, "e1", h1, al1, row_d, tab_d, bounce1)
    stage(gat_dense, h1, w2, b1, a2, h2, al2)
    stage(gat_edges, "e2", h2, al2, row_d, tab_d, bounce2)
    stage(fc_dense, h2, wfc, b2, x, bfc, x1, out)
    stage(conv_edges, x1, row_d, tab_d, conv_w, x2, out)
    stage(painn_edges, x2, row_s, tab_s, u_tab, w_in, w_o1s, w_o1v, w_o2s, w_o2v, x3)
    stage(mlp_edges, x3, row_s, tab_s, mlp_w_t, mlp_b, out)


def kernel(**inputs):
    import numpy as np
    import concourse.bacc as bacc
    from concourse.bass_utils import run_bass_kernel_spmd

    a = {k: np.asarray(v) for k, v in inputs.items()}
    g = lambda layer, name: a[f"L{layer}_gnn_{name}"]

    def padded(v, rows):
        return np.concatenate([v, np.zeros((rows - v.shape[0],) + v.shape[1:], v.dtype)])

    own = np.arange(N, N + EP - E, dtype=np.int32)
    ends = np.stack([np.concatenate([a[k].astype(np.int32), own]) for k in ("dst", "src")])
    x = padded(a["x"], LOOPED)
    tiled = lambda v: padded(v, EP).reshape(ET, P, -1).transpose(1, 0, 2)
    columns = lambda v: v.reshape(-1, P).T
    pw2 = np.concatenate([g(2, "W2"), g(2, "b2")[None]])
    pw2 = pw2.reshape(pw2.shape[0], -1, 6).transpose(0, 2, 1).reshape(pw2.shape[0], -1)
    ins = [x.T, x, ends, ends.reshape(2, ET, P).transpose(2, 0, 1), tiled(a["edge_weight"])[:, :, 0],
           padded(a["edge_attr_20"], EP).T, tiled(a["edge_attr_4"]),
           g(0, "W1"), np.stack([g(0, "a_src1").ravel(), g(0, "a_dst1").ravel()]), columns(g(0, "b1")),
           g(0, "W2"), np.stack([g(0, "a_src2").ravel(), g(0, "a_dst2").ravel()]), columns(g(0, "b2")),
           g(0, "Wfc"), g(0, "bfc"), g(1, "weight"), np.stack([g(2, "w_in2f_s"), g(2, "w_in2f_v")], 1),
           g(2, "W1"), g(2, "b1")[:, None], pw2, g(2, "w_f2o1_s"), g(2, "w_f2o1_v"), g(2, "w_f2o2_s"),
           g(2, "w_f2o2_v"), g(3, "W").T, g(3, "b")]

    nc = bacc.Bacc("TRN2", target_bir_lowering=False, num_devices=1)
    arrays, args = {}, []
    for n, v in enumerate(ins):
        v = np.ascontiguousarray(v)
        arrays[f"in_{n}_dram"] = v
        args.append(nc.dram_tensor(f"in_{n}_dram", list(v.shape), mybir.dt.from_np(v.dtype), kind="ExternalInput").ap())
    out = nc.dram_tensor("out_0_dram", [NT, D], F32, kind="ExternalOutput").ap()
    graph_layers(nc, *args, out)
    r = run_bass_kernel_spmd(nc, [arrays], core_ids=[0])
    return r.results[0]["out_0_dram"][:N]
```
